# Optimizing a Trainium2 kernel written in Bass

```python
import numpy as np
import jax
import jax.numpy as jnp

def _softmax(x, axis=-1):
    return jax.nn.softmax(x, axis=axis)

def _gelu(x):
    return jax.nn.gelu(x, approximate=True)

def _silu(x):
    return jax.nn.silu(x)

def _sigmoid(x):
    return jax.nn.sigmoid(x)

def _layernorm(x, axis=-1, eps=1e-05):
    m = jnp.mean(x, axis=axis, keepdims=True)
    v = jnp.var(x, axis=axis, keepdims=True)
    return (x - m) / jnp.sqrt(v + eps)

def _scatter_add(tgt, idx, src, axis=0):
    return tgt.at[idx].add(src)

def _segment_sum(src, seg, n):
    return jax.ops.segment_sum(src, seg, n)
kernel_name = 'mk_seq_postln_d1_jaxref_r4_9e5422'

def setup_inputs(seed: int=0):
    np.random.seed(seed)
    _w = jnp.asarray

    def _L0_attn_setup():
        import jax, jax.numpy as jnp
        import numpy as np
        D_MODEL = 512
        H = 16
        HKV = 4
        DS = 32
        DG = 32
        DV = 64
        B, T = (2, 1024)
        MB = 64
        LW = 256
        ROPE_BASE = 10000.0
        NEG_INF = -1000000000.0

        def _rope(x, pos, base):
            d = x.shape[-1]
            inv_freq = 1.0 / base ** (jnp.arange(0, d, 2, dtype=jnp.float32) / d)
            ang = pos.astype(jnp.float32)[:, None] * inv_freq
            cos, sin = (jnp.cos(ang), jnp.sin(ang))
            x1, x2 = jnp.split(x, 2, axis=-1)
            return jnp.concatenate([x1 * cos - x2 * sin, x2 * cos + x1 * sin], axis=-1)
        key = jax.random.key(seed)
        ks = jax.random.split(key, 8)
        w = lambda k, sh: jax.random.normal(k, sh, jnp.float32) * 0.02
        return {'x': jax.random.normal(ks[0], (B, T, D_MODEL), jnp.float32), 'Wq_sem': w(ks[1], (D_MODEL, H * DS)), 'Wk_sem': w(ks[2], (D_MODEL, HKV * DS)), 'Wq_geo': w(ks[3], (D_MODEL, H * DG)), 'Wk_geo': w(ks[4], (D_MODEL, HKV * DG)), 'Wv': w(ks[5], (D_MODEL, HKV * DV)), 'Wo': w(ks[6], (H * DV, D_MODEL)), 'logit_scale': jnp.zeros((H,), jnp.float32)}
    _L0_attn_in = _L0_attn_setup()

    def _L0_ffn_setup():
        import jax, jax.numpy as jnp
        import numpy as np
        HIDDEN = 512
        INTER = 2048
        SCALE = 64.0

        def fwht(x):
            orig_shape = x.shape
            n = orig_shape[-1]
            x = x.reshape(-1, n)
            h = 1
            while h < n:
                x = x.reshape(-1, n // (2 * h), 2, h)
                a, b = (x[:, :, 0, :], x[:, :, 1, :])
                x = jnp.stack([a + b, a - b], axis=2).reshape(-1, n)
                h *= 2
            return (x / jnp.sqrt(jnp.asarray(n, x.dtype))).reshape(orig_shape)
        key = jax.random.key(seed)
        ks = jax.random.split(key, 8)
        inp = jax.random.normal(ks[0], (4, 512, HIDDEN), dtype=jnp.float32)
        SU_ug = jnp.where(jax.random.bernoulli(ks[1], 0.5, (HIDDEN,)), 1.0, -1.0).astype(jnp.float32)
        SU_dp = jnp.where(jax.random.bernoulli(ks[2], 0.5, (INTER,)), 1.0, -1.0).astype(jnp.float32)
        Wscale_ug = jax.random.uniform(ks[3], (2 * INTER,), jnp.float32, 0.5, 1.5)
        Wscale_dp = jax.random.uniform(ks[4], (HIDDEN,), jnp.float32, 0.5, 1.5)
        W_up = jax.random.normal(ks[5], (INTER, HIDDEN), dtype=jnp.float32) * 0.02
        W_gate = jax.random.normal(ks[6], (INTER, HIDDEN), dtype=jnp.float32) * 0.02
        W_down = jax.random.normal(ks[7], (HIDDEN, INTER), dtype=jnp.float32) * 0.02
        return {'input': inp, 'SU_ug': SU_ug, 'SU_dp': SU_dp, 'Wscale_ug': Wscale_ug, 'Wscale_dp': Wscale_dp, 'W_up': W_up, 'W_gate': W_gate, 'W_down': W_down}
    _L0_ffn_in = _L0_ffn_setup()
    _d = {'L0_attn_x': _L0_attn_in['x'], 'L0_attn_Wq_sem': _L0_attn_in['Wq_sem'], 'L0_attn_Wk_sem': _L0_attn_in['Wk_sem'], 'L0_attn_Wq_geo': _L0_attn_in['Wq_geo'], 'L0_attn_Wk_geo': _L0_attn_in['Wk_geo'], 'L0_attn_Wv': _L0_attn_in['Wv'], 'L0_attn_Wo': _L0_attn_in['Wo'], 'L0_attn_logit_scale': _L0_attn_in['logit_scale'], 'L0_ffn_SU_ug': _L0_ffn_in['SU_ug'], 'L0_ffn_SU_dp': _L0_ffn_in['SU_dp'], 'L0_ffn_Wscale_ug': _L0_ffn_in['Wscale_ug'], 'L0_ffn_Wscale_dp': _L0_ffn_in['Wscale_dp'], 'L0_ffn_W_up': _L0_ffn_in['W_up'], 'L0_ffn_W_gate': _L0_ffn_in['W_gate'], 'L0_ffn_W_down': _L0_ffn_in['W_down']}
    _x0 = _d['L0_attn_x']
    _d['L0_attn_x'] = jax.random.normal(jax.random.fold_in(jax.random.key(seed), 1), (4, 1024, 512), dtype=_x0.dtype)
    del _x0
    return _d

def reference(L0_attn_x, L0_attn_Wq_sem, L0_attn_Wk_sem, L0_attn_Wq_geo, L0_attn_Wk_geo, L0_attn_Wv, L0_attn_Wo, L0_attn_logit_scale, L0_ffn_SU_ug, L0_ffn_SU_dp, L0_ffn_Wscale_ug, L0_ffn_Wscale_dp, L0_ffn_W_up, L0_ffn_W_gate, L0_ffn_W_down):

    def _L0_attn_ref(x, Wq_sem, Wk_sem, Wq_geo, Wk_geo, Wv, Wo, logit_scale):
        import jax, jax.numpy as jnp
        import numpy as np
        D_MODEL = 512
        H = 16
        HKV = 4
        DS = 32
        DG = 32
        DV = 64
        B, T = (2, 1024)
        MB = 64
        LW = 256
        ROPE_BASE = 10000.0
        NEG_INF = -1000000000.0

        def _rope(x, pos, base):
            d = x.shape[-1]
            inv_freq = 1.0 / base ** (jnp.arange(0, d, 2, dtype=jnp.float32) / d)
            ang = pos.astype(jnp.float32)[:, None] * inv_freq
            cos, sin = (jnp.cos(ang), jnp.sin(ang))
            x1, x2 = jnp.split(x, 2, axis=-1)
            return jnp.concatenate([x1 * cos - x2 * sin, x2 * cos + x1 * sin], axis=-1)
        Bq, Tq = (x.shape[0], x.shape[1])
        split = lambda y, h, d: y.reshape(Bq, Tq, h, d).transpose(0, 2, 1, 3)
        q_sem = split(x @ Wq_sem, H, DS)
        k_sem = split(x @ Wk_sem, HKV, DS)
        q_geo = split(x @ Wq_geo, H, DG)
        k_geo = split(x @ Wk_geo, HKV, DG)
        v = split(x @ Wv, HKV, DV)
        pos = jnp.arange(Tq)
        q_geo = _rope(q_geo, pos, ROPE_BASE)
        k_geo = _rope(k_geo, pos, ROPE_BASE)
        remote = Tq - LW
        nblk = remote // MB
        pool = lambda a: jnp.concatenate([a[:, :, :remote].reshape(Bq, HKV, nblk, MB, a.shape[-1]).mean(axis=3), a[:, :, remote:]], axis=2)
        k_sem2, k_geo2, v2 = (pool(k_sem), pool(k_geo), pool(v))
        k_pos = jnp.concatenate([jnp.arange(nblk) * MB + (MB - 1), jnp.arange(remote, Tq)])
        rep = lambda a: jnp.repeat(a, H // HKV, axis=1)
        k_sem2, k_geo2, v2 = (rep(k_sem2), rep(k_geo2), rep(v2))
        scores = jnp.einsum('bhqd,bhkd->bhqk', q_sem, k_sem2) * (1.0 / jnp.sqrt(float(DS))) + jnp.einsum('bhqd,bhkd->bhqk', q_geo, k_geo2) * (1.0 / jnp.sqrt(float(DG)))
        scores = scores * jnp.exp(logit_scale)[None, :, None, None]
        mask = k_pos[None, :] <= pos[:, None]
        scores = jnp.where(mask[None, None], scores, NEG_INF)
        probs = jax.nn.softmax(scores, axis=-1)
        out = jnp.einsum('bhqk,bhkd->bhqd', probs, v2)
        out = out.transpose(0, 2, 1, 3).reshape(Bq, Tq, H * DV)
        return out @ Wo

    def _L0_ffn_ref(input, SU_ug, SU_dp, Wscale_ug, Wscale_dp, W_up, W_gate, W_down):
        import jax, jax.numpy as jnp
        import numpy as np
        HIDDEN = 512
        INTER = 2048
        SCALE = 64.0

        def fwht(x):
            orig_shape = x.shape
            n = orig_shape[-1]
            x = x.reshape(-1, n)
            h = 1
            while h < n:
                x = x.reshape(-1, n // (2 * h), 2, h)
                a, b = (x[:, :, 0, :], x[:, :, 1, :])
                x = jnp.stack([a + b, a - b], axis=2).reshape(-1, n)
                h *= 2
            return (x / jnp.sqrt(jnp.asarray(n, x.dtype))).reshape(orig_shape)
        n = SU_ug.shape[0]
        x = input.reshape(-1, n)
        x = fwht(x * SU_ug) / SCALE
        x_up = x @ W_up.T * (Wscale_ug[:INTER] * SCALE)
        x_gate = x @ W_gate.T * (Wscale_ug[INTER:] * SCALE)
        x = jax.nn.silu(x_gate) * x_up
        x = fwht(x * SU_dp) / SCALE
        x = x @ W_down.T * (Wscale_dp * SCALE)
        return x.reshape(input.shape)
    x = L0_attn_x
    x = _layernorm(x + _L0_attn_ref(x, L0_attn_Wq_sem, L0_attn_Wk_sem, L0_attn_Wq_geo, L0_attn_Wk_geo, L0_attn_Wv, L0_attn_Wo, L0_attn_logit_scale), axis=-1)
    x = _layernorm(x + _L0_ffn_ref(x, L0_ffn_SU_ug, L0_ffn_SU_dp, L0_ffn_Wscale_ug, L0_ffn_Wscale_dp, L0_ffn_W_up, L0_ffn_W_gate, L0_ffn_W_down), axis=-1)
    return x

_drawn_inputs = setup_inputs


def setup_inputs(seed=0):
    import zlib

    import numpy as np

    out = dict(_drawn_inputs(seed))
    spreads = {'L0_attn_logit_scale': (0.0, 2.0)}
    factors = {'L0_attn_Wq_sem': 8.0, 'L0_attn_Wk_sem': 8.0, 'L0_attn_Wq_geo': 8.0, 'L0_attn_Wk_geo': 8.0}
    for name, (base, spread) in spreads.items():
        noise = np.random.default_rng([zlib.crc32(name.encode()), seed]).standard_normal(out[name].shape)
        drawn = base * np.exp(spread * noise) if base else spread * noise
        out[name] = jnp.asarray(drawn.astype(out[name].dtype))
    for name, factor in factors.items():
        out[name] = (out[name] * factor).astype(out[name].dtype)
    return out
```

```python
from contextlib import ExitStack

import concourse.bass as bass
from concourse import mybir

F32 = mybir.dt.float32
F32R = mybir.dt.float32r
ACT = mybir.ActivationFunctionType
ALU = mybir.AluOpType
AX = mybir.AxisListType

P = 128
B, T, D = 4, 1024, 512
H, HKV, DS, DG, DV = 16, 4, 32, 32, 64
REP = H // HKV
MB, LW = 64, 256
REMOTE = T - LW
NB = REMOTE // MB
NK = NB + 1
HALF = DG // 2
INTER = 2048
DC = D // P
IC = INTER // P
RT = REMOTE // P
LT = LW // P
TILES = RT + LT
QB = 256
RB = REMOTE // QB
NEG = -1.0e9
EPS = 1e-5
KEYS = NB + LW
HK = H // 2 * NK
HB = H // 2 * NB
FB = 512
FBLK = B * T // FB
FT = FB // P


class Signal:

    def __init__(self, ctx, nc, name, per):
        self.sem, self.per = ctx.enter_context(nc.semaphore(name)), per

    def now(self, i, k):
        return self.sem, (i + 1) * self.per + k

    def last(self, i, k):
        return self.sem, i * self.per + k


def tools(nc, ctx, sems, tag):
    def sb(name, shape, dt=F32):
        return ctx.enter_context(nc.sbuf_tensor(f"{tag}_{name}", shape, dt))

    def ps(name, shape):
        return ctx.enter_context(nc.psum_tensor(f"{tag}_{name}", shape, F32))

    def signal(name, per):
        return Signal(sems, nc, f"{tag}_{name}", per)

    def sem(name):
        return sems.enter_context(nc.semaphore(f"{tag}_{name}"))

    return sb, ps, signal, sem


def three_passes(pe, out, lhs_hi, lhs_lo, rhs_hi, rhs_lo, first, last):
    pe.matmul(out, lhs_hi, rhs_hi, start=first, stop=False)
    pe.matmul(out, lhs_hi, rhs_lo, start=False, stop=False)
    return pe.matmul(out, lhs_lo, rhs_hi, start=False, stop=last)


def bc(ap, axis, n):
    wide = ap.unsqueeze(axis)
    shape = list(wide.shape)
    shape[axis] = n
    return wide.broadcast_to(shape)


def attention_block(nc, sems, io, x1_dram, x1t_dram):
    ctx = ExitStack()
    with ctx:
        sb, ps, signal, sem = tools(nc, ctx, sems, "at")
        wq_hi, wq_lo = sb("wq_hi", [P, DC, 2 * D], F32R), sb("wq_lo", [P, DC, 2 * D], F32R)
        wo_hi, wo_lo = sb("wo_hi", [P, 8, D], F32R), sb("wo_lo", [P, 8, D], F32R)
        wkv = sb("wkv", [P, DC, D])
        wqs = sb("wqs", [P, DC, D])
        ident = sb("ident", [P, P])
        cos_t, sin_t = sb("cos_t", [P, REMOTE]), sb("sin_t", [P, REMOTE])
        rope = sb("rope", [P, TILES, 2, HALF])
        small = sb("small", [P, 4 * NB + 8 * NB + 2 * NK + RT * NB * 3 + 2 * RT + P])
        o = 0
        def table(*shape):
            nonlocal o
            n = 1
            for s in shape:
                n *= s
            v = small[:, o:o + n]
            o += n
            if len(shape) == 2:
                v = v.rearrange("p (a b) -> p a b", a=shape[0])
            return v
        own_sem = table(4, NB)
        own_geo = table(8, NB)
        own_v = table(2, NK)
        pool_w = table(RT, NB)
        keep = table(RT, NB)
        hide = table(RT, NB)
        spread = table(RT)
        rest_p = table(RT)
        causal = table(P)
        scales = sb("scales", [P, H + DC])
        power = sb("power", [P, 2])
        xt = sb("xt", [P, DC, T])
        xn = sb("xn", [P, 2, D])
        xs_hi, xs_lo = sb("xs_hi", [P, 2, DC, QB], F32R), sb("xs_lo", [P, 2, DC, QB], F32R)
        xpool = sb("xpool", [P, DC, NK])
        krot = sb("krot", [P, LT, HKV, 2 * DS])
        v_hi, v_lo = sb("v_hi", [P, LT, HKV * DV], F32R), sb("v_lo", [P, LT, HKV * DV], F32R)
        kp = sb("kp", [NK, D])
        kt_hi, kt_lo = sb("kt_hi", [P, 2, KEYS], F32R), sb("kt_lo", [P, 2, KEYS], F32R)
        ks_bd = sb("ks_bd", [P, 4, 4 * NB])
        kg_bd = sb("kg_bd", [P, 4, 8 * NB])
        m_sb = sb("m_sb", [P, DC, H * NB])
        vwo_hi, vwo_lo = sb("vwo_hi", [HK, 2, D], F32R), sb("vwo_lo", [HK, 2, D], F32R)
        union = sb("union", [P, H * KEYS])
        q_rem = union[:, 0:RB * 4 * QB].rearrange("p (n r c) -> p n r c", n=RB, r=2)
        rt1, rt2 = union[:, 3072:3584], union[:, 3584:4096]
        vbd = union[:, 0:8 * HK]
        kr = union[0:NK, 1024:2304]
        kt1, kt2 = union[:, 2304:2688], union[:, 2688:3072]
        kgr = union[:, 3072:3840].rearrange("p (t e) -> p t e", t=RT)
        probs_l = union[:, :].rearrange("p (h k) -> p h k", h=H)
        sm = sb("sm", [P, 2, H * NB])
        pr = sb("pr", [P, 2, H, NK])
        stat = sb("stat", [P, 2, 4, H])
        pt_hi, pt_lo = sb("pt_hi", [HK, 2, P], F32R), sb("pt_lo", [HK, 2, P], F32R)
        qrot = sb("qrot", [P, 8, 2, DV])
        lt1, lt2 = sb("lt1", [P, H * HALF]), sb("lt2", [P, H * HALF])
        qo_hi, qo_lo = sb("qo_hi", [P, 8, P], F32R), sb("qo_lo", [P, 8, P], F32R)
        tp_hi, tp_lo = sb("tp_hi", [P, 2, 4 * P], F32R), sb("tp_lo", [P, 2, 4 * P], F32R)
        vb_hi = tp_hi[:, :, :].rearrange("p a b -> p (a b)")[:, 0:8 * HK]
        vb_lo = tp_lo[:, :, :].rearrange("p a b -> p (a b)")[:, 0:8 * HK]
        x1, x1t = sb("x1", [P, 2, D]), sb("x1t", [P, 2, D])
        bn, mv, rstd = sb("bn", [P, 2, 6]), sb("mv", [P, 2, 2]), sb("rstd", [P, 2, 1])

        big = ps("big", [P, 4, 512])
        mid = ps("mid", [P, 2, 512])
        tr = ps("tr", [P, 512])
        acc = ps("acc", [P, 512])

        wq_in, wo_in, wkv_in, wqs_in, tab_in, ls_in = (sem(n) for n in ("wq_in", "wo_in", "wkv_in", "wqs_in", "tab_in", "ls_in"))
        scale_exp, scale_done, wq_scaled, wqs_scaled, wq_split, wo_split, power_set, zeroed = (
            sem(n) for n in ("scale_exp", "scale_done", "wq_scaled", "wqs_scaled", "wq_split", "wo_split", "power_set", "zeroed"))
        dve_past, pe_past = sem("dve_past"), sem("pe_past")
        xt_in = signal("xt_in", 16)
        xn_in = [signal(f"xn_in{i}", 16 * TILES // 2) for i in range(2)]
        xs_hi_s, xs_lo_s = signal("xs_hi_s", RB + 1), signal("xs_lo_s", RB + 1)
        kgeo_ps, kv_ps = signal("kgeo_ps", 1), signal("kv_ps", LT)
        xsum, xpool_s = signal("xsum", 2), signal("xpool_s", 1)
        krope = signal("krope", 12)
        krot_sem, v_hi_s, v_lo_s = signal("krot_sem", 1), signal("v_hi_s", 1), signal("v_lo_s", 1)
        kp_ps, kp_s, kr_s = signal("kp_ps", 1), signal("kp_s", 2), signal("kr_s", 6)
        ktr_ps, klt_ps = signal("ktr_ps", 1), signal("klt_ps", 1)
        kt_hi_s, kt_lo_s = signal("kt_hi_s", 2), signal("kt_lo_s", 2)
        bd_s, vbd_s, vb_hi_s, vb_lo_s = signal("bd_s", 2), signal("vbd_s", 2), signal("vb_hi_s", 1), signal("vb_lo_s", 1)
        m_ps, m_s = signal("m_ps", 1), signal("m_s", 1)
        vwo_ps, vwo_hi_s, vwo_lo_s = signal("vwo_ps", 2), signal("vwo_hi_s", 2), signal("vwo_lo_s", 2)
        qg_ps, qrope = signal("qg_ps", RB), signal("qrope", 6 * RB)
        s_ps, masked, shifted = signal("s_ps", RT), signal("masked", 2 * RT), signal("shifted", 2 * RT)
        exp_s, summed, probs_s = signal("exp_s", RT), signal("summed", 3 * RT), signal("probs_s", TILES)
        pt_ps, pt_hi_s, pt_lo_s = signal("pt_ps", TILES), signal("pt_hi_s", TILES), signal("pt_lo_s", TILES)
        out_ps, added, normed = signal("out_ps", TILES), signal("added", TILES), signal("normed", TILES)
        bn_s, var_s, rstd_s = signal("bn_s", 2 * TILES), signal("var_s", TILES), signal("rstd_s", TILES)
        x1t_ps, x1t_s = signal("x1t_ps", TILES), signal("x1t_s", TILES)
        x1_out = [signal(f"x1_out{i}", 16 * TILES // 2) for i in range(2)]
        x1t_out = [signal(f"x1t_out{i}", 16 * TILES // 2) for i in range(2)]
        qp_ps, qsem_s, lrope = signal("qp_ps", LT), signal("qsem_s", LT), signal("lrope", 6 * LT)
        qt_ps, qt_hi_s, qt_lo_s = signal("qt_ps", LT), signal("qt_hi_s", LT), signal("qt_lo_s", LT)
        ls_ps, lmasked, lmax, lexp = signal("ls_ps", 8 * LT), signal("lmasked", 8 * LT), signal("lmax", 8 * LT), signal("lexp", 8 * LT)
        lnorm = signal("lnorm", 3 * LT)
        NPT = [HKV * (tt + 1) for tt in range(LT)]
        tp_ps, tp_hi_s, tp_lo_s = signal("tp_ps", sum(NPT)), signal("tp_hi_s", sum(NPT)), signal("tp_lo_s", sum(NPT))
        pv_ps, o_hi_s, o_lo_s = signal("pv_ps", sum(NPT)), signal("o_hi_s", HKV * LT), signal("o_lo_s", HKV * LT)

        def prime(eng, *signals):
            for s in signals:
                eng.sem_inc(s.sem, s.per)

        def flat(t):
            return t[:, :, :].rearrange("p a b -> p (a b)")

        qf = flat(big)

        def own_columns(a, s):
            n = HK + NK
            j, r = divmod(4 * a * HK + 4 * s * NK, n)
            return union[:, 0:8 * n].rearrange("p (j n) -> p j n", n=n)[:, j:j + 4, r:r + NK]

        block = ctx.enter_context(nc.Block())

        @block.sync
        def _(sp):
            prime(sp, xt_in, *xn_in, *x1_out, *x1t_out)
            sp.dma_start(xt[:, :, :], io["xt"][0]).then_inc(xt_in.sem, 16)
            sp.dma_start(wkv[:, :, :], io["wkv"]).then_inc(wkv_in, 16)
            for t, n in ((ident, "ident"), (cos_t, "cos_t"), (sin_t, "sin_t"), (rope, "rope"), (small, "small")):
                sp.dma_start(t[:], io[n]).then_inc(tab_in, 16)

            def tiles(b, fetch):
                def load(t):
                    sp.wait_ge(*(added.now(b, t - 1) if t >= 2 else added.last(b, TILES - 1 + t)))
                    sp.dma_start(xn[:, t % 2, :], io["x"][b, t]).then_inc(xn_in[t % 2].sem, 16)

                load(0)
                for t in range(TILES):
                    if t + 1 < TILES:
                        load(t + 1)
                    if fetch and t == RT:
                        sp.wait_ge(*xs_hi_s.now(b, RB + 1))
                        sp.wait_ge(*xs_lo_s.now(b, RB + 1))
                        sp.wait_ge(*s_ps.now(b, RT))
                        sp.dma_start(xt[:, :, :], io["xt"][b + 1]).then_inc(xt_in.sem, 16)
                    sp.wait_ge(*normed.now(b, t + 1))
                    sp.dma_start(x1_dram[b, t], x1[:, t % 2, :]).then_inc(x1_out[t % 2].sem, 16)
                    sp.wait_ge(*x1t_s.now(b, t + 1))
                    sp.dma_start(x1t_dram[b, t], x1t[:, t % 2, :]).then_inc(x1t_out[t % 2].sem, 16)

            with sp.Fori(0, B - 1) as b:
                tiles(b, True)
            tiles(B - 1, False)
            for s in (*x1_out, *x1t_out):
                sp.wait_ge(*s.now(B - 1, 16 * TILES // 2))

        @block.gpsimd
        def _(pool):
            prime(pool, var_s, rstd_s)
            pool.dma_start(scales[:, :], io["logit_scale"]).then_inc(ls_in, 16)
            pool.dma_start(union[:, 0:DC * 2 * D].rearrange("p (c n) -> p c n", c=DC), io["wq"]).then_inc(wq_in, 16)
            pool.dma_start(wqs[:, :, :], io["wqs"]).then_inc(wqs_in, 16)
            pool.memset(power[:, 0:1], -0.5).then_inc(power_set, 1)
            pool.memset(power[:, 1:2], EPS).then_inc(power_set, 1)
            pool.wait_ge(power_set, 2)
            with pool.Fori(0, B) as b:
                for t in range(TILES):
                    pool.wait_ge(*bn_s.now(b, 2 * t + 2))
                    pool.wait_ge(*(normed.now(b, t - 1) if t >= 2 else normed.last(b, TILES - 1 + t)))
                    pool.tensor_tensor(rstd[:, t % 2, :], mv[:, t % 2, 1:2], power[:, 1:2], ALU.add).then_inc(var_s.sem, 1)
                    pool.wait_ge(*var_s.now(b, t + 1))
                    pool.tensor_tensor(rstd[:, t % 2, :], rstd[:, t % 2, :], power[:, 0:1], ALU.pow).then_inc(rstd_s.sem, 1)

        @block.scalar
        def _(act):
            prime(act, xs_hi_s, krot_sem, v_hi_s, kp_s, kt_hi_s, vb_hi_s, m_s, vwo_hi_s, exp_s, pt_hi_s, x1t_s,
                  qsem_s, qt_hi_s, lexp, tp_hi_s, o_hi_s)
            act.wait_ge(ls_in, 16)
            act.activation(scales[:, :], scales[:, :], ACT.Exp).then_inc(scale_exp, 1)
            act.wait_ge(wq_scaled, 3)
            act.activation(wq_hi[:, :, :], union[:, 0:DC * 2 * D].rearrange("p (c n) -> p c n", c=DC), ACT.Copy).then_inc(wq_split, 1)
            act.wait_ge(wq_split, 2)
            act.dma_start(union[:, 0:8 * D].rearrange("p (c n) -> p c n", c=8), io["wo"]).then_inc(wo_in, 16)
            act.wait_ge(wo_in, 16)
            act.activation(wo_hi[:, :, :], union[:, 0:8 * D].rearrange("p (c n) -> p c n", c=8), ACT.Copy).then_inc(wo_split, 1)

            def split_x(b, n):
                act.wait_ge(*xt_in.now(b, 16))
                if n < 2:
                    act.wait_ge(*(qg_ps.last(b, RB) if n == 0 else qp_ps.last(b, LT)))
                else:
                    act.wait_ge(*qg_ps.now(b, n - 1))
                act.activation(xs_hi[:, n % 2, :, :], xt[:, :, n * QB:(n + 1) * QB], ACT.Copy).then_inc(xs_hi_s.sem, 1)

            def pooled_hi(b, t):
                act.wait_ge(*pt_ps.now(b, t + 1))
                act.wait_ge(*(out_ps.now(b, t) if t else out_ps.last(b, TILES)))
                act.activation(pt_hi[:, :, :], tr[0:HK, 0:2 * P].rearrange("p (a q) -> p a q", a=2), ACT.Copy).then_inc(pt_hi_s.sem, 1)

            def x1t_copy(b, t):
                act.wait_ge(*x1t_ps.now(b, t + 1))
                act.wait_ge(*(x1t_out[t % 2].now(b, 16 * (t // 2)) if t >= 2 else x1t_out[t % 2].last(b, 16 * (TILES // 2))))
                act.activation(x1t[:, t % 2, :], tr[:, :], ACT.Copy).then_inc(x1t_s.sem, 1)

            with act.Fori(0, B) as b:
                split_x(b, 0)
                split_x(b, 1)
                act.wait_ge(*kv_ps.now(b, 2))
                act.wait_ge(*klt_ps.last(b, 1))
                act.wait_ge(*pv_ps.last(b, sum(NPT)))
                act.activation(krot[:, :, :, 0:DS], big[:, 2:4, 128:256].rearrange("p t (g e) -> p t g e", g=HKV), ACT.Copy).then_inc(krot_sem.sem, 1)
                act.activation(v_hi[:, :, :], big[:, 2:4, 256:512], ACT.Copy).then_inc(v_hi_s.sem, 1)
                act.wait_ge(*kp_ps.now(b, 1))
                act.wait_ge(*ktr_ps.last(b, 1))
                act.activation(kp[:, 128:512], acc[0:NK, 128:512], ACT.Copy).then_inc(kp_s.sem, 1)
                act.activation(kp[0:NB, 0:128], acc[0:NB, 0:128], ACT.Copy).then_inc(kp_s.sem, 1)
                act.wait_ge(*klt_ps.now(b, 1))
                act.wait_ge(*ls_ps.last(b, 8 * LT))
                act.activation(kt_hi[:, :, NB:KEYS], mid[:, 1, :].rearrange("p (a k) -> p a k", a=2), ACT.Copy).then_inc(kt_hi_s.sem, 1)
                act.wait_ge(*ktr_ps.now(b, 1))
                act.activation(kt_hi[:, :, 0:NB], tr[:, 160:192].rearrange("p (a k) -> p a k", a=2)[:, :, 0:NB], ACT.Copy).then_inc(kt_hi_s.sem, 1)
                act.wait_ge(*vbd_s.now(b, 2))
                act.activation(vb_hi, vbd, ACT.Copy).then_inc(vb_hi_s.sem, 1)
                act.wait_ge(*m_ps.now(b, 1))
                act.activation(m_sb[:, :, :].rearrange("p (u v) n -> p u (v n)", u=2), big[:, 0:2, 0:2 * H * NB], ACT.Copy).then_inc(m_s.sem, 1)
                for a in range(2):
                    act.wait_ge(*vwo_ps.now(b, a + 1))
                    act.activation(vwo_hi[:, a, :], big[0:HK, 2 + a, :], ACT.Copy).then_inc(vwo_hi_s.sem, 1)
                split_x(b, 2)
                for t in range(RT + 3):
                    if t == 1:
                        split_x(b, 3)
                    if t < RT:
                        act.wait_ge(*shifted.now(b, 2 * t + 2))
                        act.activation(pr[:, t % 2, :, 0:NB], sm[:, t % 2, :].rearrange("p (h k) -> p h k", h=H), ACT.Exp).then_inc(exp_s.sem, 1)
                    if 1 <= t <= RT:
                        pooled_hi(b, t - 1)
                    if t >= 3:
                        x1t_copy(b, t - 3)
                n0 = 0
                for tt in range(LT):
                    t = RT + tt
                    keys = NB + P * (tt + 1)
                    act.wait_ge(*qp_ps.now(b, tt + 1))
                    act.wait_ge(*(qt_ps.now(b, tt) if tt else qt_ps.last(b, LT)))
                    for a in range(2):
                        i = act.activation(qrot[:, 4 * a:4 * a + 4, :, 0:DS].rearrange("p j s e -> p s j e"),
                                           mid[:, 0, 256 * a:256 * a + 256].rearrange("p (s j e) -> p s j e", s=2, j=4), ACT.Copy)
                    i.then_inc(qsem_s.sem, 1)
                    act.wait_ge(*qt_ps.now(b, tt + 1))
                    act.wait_ge(*(out_ps.now(b, t)))
                    act.activation(qo_hi[:, :, :].rearrange("p c q -> p (c q)"), flat(mid), ACT.Copy).then_inc(qt_hi_s.sem, 1)
                    for p in range(8):
                        act.wait_ge(*lmax.now(b, 8 * tt + p + 1))
                        for h in (2 * p, 2 * p + 1):
                            i = act.activation(probs_l[:, h, 0:keys], big[:, 2 * (p % 2) + h % 2, 0:keys], ACT.Exp,
                                               bias=stat[:, tt, 0, h:h + 1], accum_out=stat[:, tt, 1, h:h + 1])
                        i.then_inc(lexp.sem, 1)
                    pooled_hi(b, t)
                    for n in range(NPT[tt] + 1):
                        if n < NPT[tt]:
                            act.wait_ge(*tp_ps.now(b, n0 + n + 1))
                            act.wait_ge(*(pv_ps.now(b, n0 + n - 1) if tt or n >= 2 else vwo_ps.now(b, 2)))
                            act.activation(tp_hi[:, n % 2, :], mid[:, n % 2, :], ACT.Copy).then_inc(tp_hi_s.sem, 1)
                        g = (n - 1) // (tt + 1)
                        if n >= 1 and n % (tt + 1) == 0:
                            act.wait_ge(*pv_ps.now(b, n0 + n))
                            r = slice(64 * (g % 2), 64 * (g % 2) + 64)
                            act.activation(qo_hi[r, 4 * (g // 2):4 * (g // 2) + 4, :].rearrange("p j q -> p (j q)"),
                                           big[r, g, :], ACT.Copy).then_inc(o_hi_s.sem, 1)
                    n0 += NPT[tt]
                    x1t_copy(b, t)

        @block.vector
        def _(dve):
            prime(dve, xs_lo_s, xsum, xpool_s, krope, v_lo_s, kr_s, kt_lo_s, bd_s, vbd_s, vb_lo_s, vwo_lo_s, qrope,
                  masked, shifted, summed, probs_s, pt_lo_s, added, normed, bn_s, lrope, qt_lo_s, lmasked, lmax,
                  lnorm, tp_lo_s, o_lo_s)
            dve.wait_ge(scale_exp, 1)
            dve.tensor_scalar(scales[:, :], scales[:, :], float(DS) ** -0.5, None, ALU.mult).then_inc(scale_done, 1)
            dve.wait_ge(scale_done, 1)
            dve.wait_ge(wq_in, 16)
            raw = union[:, 0:DC * 2 * D].rearrange("p (c n) -> p c n", c=DC)
            for c0, c1, w in ((0, 512, DS), (512, 768, HALF), (768, 1024, HALF)):
                v = raw[:, :, c0:c1].rearrange("p c (h e) -> p c h e", h=H)
                s = bc(bc(scales[:, 0:H], 1, DC), 3, w)
                dve.tensor_tensor(v, v, s, ALU.mult).then_inc(wq_scaled, 1)
            dve.wait_ge(wqs_in, 16)
            for c in range(DC):
                dve.tensor_scalar(wqs[:, c, :], wqs[:, c, :], scales[:, H + c:H + c + 1], None, ALU.mult).then_inc(wqs_scaled, 1)
            dve.memset(pr[:, :, :, :], 0.0).then_inc(zeroed, 1)
            dve.wait_ge(wq_scaled, 3)
            dve.wait_ge(wq_split, 1)
            dve.tensor_tensor(wq_lo[:, :, :], raw, wq_hi[:, :, :].bitcast(F32), ALU.subtract).then_inc(wq_split, 1)
            dve.wait_ge(wo_split, 1)
            dve.tensor_tensor(wo_lo[:, :, :], union[:, 0:8 * D].rearrange("p (c n) -> p c n", c=8),
                              wo_hi[:, :, :].bitcast(F32), ALU.subtract).then_inc(wo_split, 1)
            dve.wait_ge(wo_split, 2)
            dve.wait_ge(zeroed, 1)
            dve.wait_ge(tab_in, 16 * 5)

            def split_x(b, n):
                dve.wait_ge(*xs_hi_s.now(b, n + 1))
                dve.tensor_tensor(xs_lo[:, n % 2, :, :], xt[:, :, n * QB:(n + 1) * QB],
                                  xs_hi[:, n % 2, :, :].bitcast(F32), ALU.subtract).then_inc(xs_lo_s.sem, 1)

            def pooled_lo(b, t):
                dve.wait_ge(*pt_hi_s.now(b, t + 1))
                dve.tensor_tensor(pt_lo[:, :, :], tr[0:HK, 0:2 * P].rearrange("p (a q) -> p a q", a=2),
                                  pt_hi[:, :, :].bitcast(F32), ALU.subtract).then_inc(pt_lo_s.sem, 1)

            def rotate(b, sig, k, in1, in2, cos, sin, out1, out2, u, v):
                dve.tensor_tensor(u, in1, cos, ALU.mult).then_inc(sig.sem, 1)
                dve.tensor_tensor(v, in2, sin, ALU.mult).then_inc(sig.sem, 1)
                dve.wait_ge(*sig.now(b, k + 2))
                dve.tensor_tensor(out1, u, v, ALU.subtract).then_inc(sig.sem, 1)
                dve.wait_ge(*sig.now(b, k + 3))
                dve.tensor_tensor(u, in2, cos, ALU.mult).then_inc(sig.sem, 1)
                dve.tensor_tensor(v, in1, sin, ALU.mult).then_inc(sig.sem, 1)
                dve.wait_ge(*sig.now(b, k + 5))
                dve.tensor_tensor(out2, u, v, ALU.add).then_inc(sig.sem, 1)

            def residual_norm(b, t):
                dve.wait_ge(*out_ps.now(b, t + 1))
                dve.wait_ge(*xn_in[t % 2].now(b, 16 * (t // 2 + 1)))
                dve.wait_ge(*(x1_out[t % 2].now(b, 16 * (t // 2)) if t >= 2 else x1_out[t % 2].last(b, 16 * (TILES // 2))))
                dve.wait_ge(*(x1t_ps.now(b, t - 1) if t >= 2 else x1t_ps.last(b, TILES - 1 + t)))
                dve.tensor_tensor(x1[:, t % 2, :], acc[:, :], xn[:, t % 2, :], ALU.add).then_inc(added.sem, 1)
                dve.wait_ge(*added.now(b, t + 1))
                dve.bn_stats(bn[:, t % 2, :], x1[:, t % 2, :]).then_inc(bn_s.sem, 1)
                dve.wait_ge(*bn_s.now(b, 2 * t + 1))
                dve.sem_inc(dve_past, 1)
                dve.bn_aggr(mv[:, t % 2, :], bn[:, t % 2, :]).then_inc(bn_s.sem, 1)

            def scale_x1(b, t):
                dve.wait_ge(*rstd_s.now(b, t + 1))
                dve.tensor_scalar(x1[:, t % 2, :], x1[:, t % 2, :], mv[:, t % 2, 0:1], rstd[:, t % 2, :],
                                  ALU.subtract, ALU.mult).then_inc(normed.sem, 1)

            with dve.Fori(0, B) as b:
                dve.wait_ge(*xt_in.now(b, 16))
                dve.wait_ge(*kp_ps.last(b, 1))
                for c, (c0, c1, n) in enumerate(((0, REMOTE, NB), (REMOTE, T, 1))):
                    dve.tensor_reduce(xpool[:, :, NB * c:NB * c + n], xt[:, :, c0:c1].rearrange("p c (n m) -> p c n m", n=n),
                                      AX.X, ALU.add).then_inc(xsum.sem, 1)
                dve.wait_ge(*xsum.now(b, 2))
                dve.tensor_scalar(xpool[:, :, 0:NB], xpool[:, :, 0:NB], 1.0 / MB, None, ALU.mult).then_inc(xpool_s.sem, 1)
                split_x(b, 0)
                dve.wait_ge(*kgeo_ps.now(b, 1))
                r6 = lambda c: qf[:, 0:RT * P].rearrange("p (t e) -> p t e", t=RT)[:, :, c:c + 64].rearrange("p t (g f) -> p t g f", g=HKV)
                o6 = lambda c: kgr[:, :, c:c + 64].rearrange("p t (g f) -> p t g f", g=HKV)
                u6 = lambda t: t[:, 0:RT * 64].rearrange("p (t g f) -> p t g f", t=RT, g=HKV)
                rotate(b, krope, 0, r6(0), r6(64), bc(rope[:, 0:RT, 0, :], 2, HKV), bc(rope[:, 0:RT, 1, :], 2, HKV),
                       o6(0), o6(64), u6(kt1), u6(kt2))
                dve.wait_ge(*v_hi_s.now(b, 1))
                dve.wait_ge(*krope.now(b, 6))
                r2 = lambda c: big[:, 2:4, c:c + 64].rearrange("p t (g f) -> p t g f", g=HKV)
                u2 = lambda t: t[:, 0:LT * 64].rearrange("p (t g f) -> p t g f", t=LT, g=HKV)
                rotate(b, krope, 6, r2(0), r2(64), bc(rope[:, RT:TILES, 0, :], 2, HKV), bc(rope[:, RT:TILES, 1, :], 2, HKV),
                       krot[:, :, :, DS:DS + HALF], krot[:, :, :, DS + HALF:DS + DG], u2(kt1), u2(kt2))
                dve.tensor_tensor(v_lo[:, :, :], big[:, 2:4, 256:512], v_hi[:, :, :].bitcast(F32), ALU.subtract).then_inc(v_lo_s.sem, 1)
                dve.wait_ge(*kp_s.now(b, 2))
                for c in range(2):
                    dve.tensor_copy(kr[0:NB, 256 * c:256 * c + 256].rearrange("k (g r f) -> k g r f", g=HKV, r=REP),
                                    bc(kp[0:NB, 64 * c:64 * c + 64].rearrange("k (g f) -> k g f", g=HKV), 2, REP)).then_inc(kr_s.sem, 1)
                dve.tensor_copy(kr[0:NB, 512:1024].rearrange("k (g r f) -> k g r f", g=HKV, r=REP),
                                bc(kp[0:NB, 128:256].rearrange("k (g f) -> k g f", g=HKV), 2, REP)).then_inc(kr_s.sem, 1)
                by_head = kr[0:NB, 1024:1280].rearrange("k (g e) -> k g e", g=HKV)
                for e0, w, c0 in ((0, DS, 128), (DS, HALF, 0), (DS + HALF, HALF, 64)):
                    dve.tensor_copy(by_head[:, :, e0:e0 + w], kp[0:NB, c0:c0 + HKV * w].rearrange("k (g f) -> k g f", g=HKV)).then_inc(kr_s.sem, 1)
                split_x(b, 1)
                dve.wait_ge(*kt_hi_s.now(b, 1))
                dve.tensor_tensor(kt_lo[:, :, NB:KEYS], mid[:, 1, :].rearrange("p (a k) -> p a k", a=2),
                                  kt_hi[:, :, NB:KEYS].bitcast(F32), ALU.subtract).then_inc(kt_lo_s.sem, 1)
                dve.wait_ge(*kt_hi_s.now(b, 2))
                slots = tr[:, 0:192].rearrange("p (s k) -> p s k", k=16)
                dve.tensor_tensor(kg_bd[:, :, :].rearrange("p c (h k) -> p c h k", h=8), bc(slots[:, 0:4, 0:NB], 2, 8),
                                  bc(own_geo, 1, 4), ALU.mult).then_inc(bd_s.sem, 1)
                dve.tensor_tensor(ks_bd[:, :, :].rearrange("p c (h k) -> p c h k", h=4), bc(slots[:, 4:8, 0:NB], 2, 4),
                                  bc(own_sem, 1, 4), ALU.mult).then_inc(bd_s.sem, 1)
                dve.memset(vbd, 0.0).then_inc(zeroed, 1)
                dve.wait_ge(zeroed, b + 2)
                for a in range(2):
                    for s in range(2):
                        i = dve.tensor_tensor(own_columns(a, s), bc(slots[:, 8 + a, 0:NK], 1, 4), bc(own_v[:, s, :], 1, 4), ALU.mult)
                    i.then_inc(vbd_s.sem, 1)
                dve.tensor_tensor(kt_lo[:, :, 0:NB], tr[:, 160:192].rearrange("p (a k) -> p a k", a=2)[:, :, 0:NB],
                                  kt_hi[:, :, 0:NB].bitcast(F32), ALU.subtract).then_inc(kt_lo_s.sem, 1)
                dve.wait_ge(*vb_hi_s.now(b, 1))
                dve.tensor_tensor(vb_lo, vbd, vb_hi.bitcast(F32), ALU.subtract).then_inc(vb_lo_s.sem, 1)
                for a in range(2):
                    dve.wait_ge(*vwo_hi_s.now(b, a + 1))
                    dve.tensor_tensor(vwo_lo[:, a, :], big[0:HK, 2 + a, :], vwo_hi[:, a, :].bitcast(F32), ALU.subtract).then_inc(vwo_lo_s.sem, 1)

                def rotate_queries(n):
                    dve.wait_ge(*qg_ps.now(b, n + 1))
                    dve.wait_ge(*(qrope.now(b, 6 * n) if n else vb_lo_s.now(b, 1)))
                    f = lambda v: v.rearrange("p (a q) -> p a q", a=2)
                    rotate(b, qrope, 6 * n, f(big[:, 2 * (n % 2), :]), f(big[:, 2 * (n % 2) + 1, :]),
                           bc(cos_t[:, n * QB:(n + 1) * QB], 1, 2), bc(sin_t[:, n * QB:(n + 1) * QB], 1, 2),
                           f(q_rem[:, n, 0, :]), f(q_rem[:, n, 1, :]), f(rt1), f(rt2))

                def softmax_in(t):
                    s3 = sm[:, t % 2, :].rearrange("p (h k) -> p h k", h=H)
                    dve.wait_ge(*s_ps.now(b, t + 1))
                    dve.wait_ge(*(exp_s.now(b, t - 1) if t >= 2 else exp_s.last(b, RT)))
                    dve.tensor_tensor(s3, mid[:, t % 2, 0:H * NB].rearrange("p (h k) -> p h k", h=H),
                                      bc(keep[:, t, :], 1, H), ALU.mult).then_inc(masked.sem, 1)
                    dve.wait_ge(*masked.now(b, 2 * t + 1))
                    dve.tensor_tensor(s3, s3, bc(hide[:, t, :], 1, H), ALU.add).then_inc(masked.sem, 1)
                    dve.wait_ge(*masked.now(b, 2 * t + 2))
                    dve.tensor_reduce(stat[:, t % 2, 0, :], s3, AX.X, ALU.max).then_inc(shifted.sem, 1)
                    dve.wait_ge(*shifted.now(b, 2 * t + 1))
                    dve.wait_ge(*(pt_ps.now(b, t - 1) if t >= 2 else pt_ps.last(b, TILES - 1 + t)))
                    dve.tensor_tensor(s3, s3, bc(stat[:, t % 2, 0, :], 2, NB), ALU.subtract).then_inc(shifted.sem, 1)

                def softmax_out(t):
                    p3 = pr[:, t % 2, :, 0:NB]
                    dve.wait_ge(*exp_s.now(b, t + 1))
                    dve.tensor_reduce(stat[:, t % 2, 1, :], p3, AX.X, ALU.add).then_inc(summed.sem, 1)
                    dve.wait_ge(*summed.now(b, 3 * t + 1))
                    dve.tensor_scalar(stat[:, t % 2, 2, :], stat[:, t % 2, 1, :], spread[:, t:t + 1], None, ALU.mult).then_inc(summed.sem, 1)
                    dve.wait_ge(*summed.now(b, 3 * t + 2))
                    dve.reciprocal(stat[:, t % 2, 3, :], stat[:, t % 2, 2, :]).then_inc(summed.sem, 1)
                    dve.wait_ge(*summed.now(b, 3 * t + 3))
                    dve.tensor_copy(pr[:, t % 2, :, NB:NK], bc(rest_p[:, t:t + 1], 1, H))
                    dve.tensor_tensor(p3, p3, bc(stat[:, t % 2, 3, :], 2, NB), ALU.mult).then_inc(probs_s.sem, 1)

                rotate_queries(0)
                split_x(b, 2)
                rotate_queries(1)
                for t in range(RT + 3):
                    if t == 1:
                        rotate_queries(2)
                    if t == 1:
                        split_x(b, 3)
                    if t < RT:
                        softmax_in(t)
                    if 1 <= t <= RT:
                        pooled_lo(b, t - 1)
                    if t < RT:
                        softmax_out(t)
                    if 2 <= t < RT + 2:
                        residual_norm(b, t - 2)
                        scale_x1(b, t - 2)
                for tt in range(LT):
                    t = RT + tt
                    keys = NB + P * (tt + 1)
                    dve.wait_ge(*qp_ps.now(b, tt + 1))
                    dve.wait_ge(*(qt_ps.now(b, tt) if tt else qt_ps.last(b, LT)))
                    if tt:
                        dve.wait_ge(*lrope.now(b, 6 * tt))
                    q_out = lambda e0: qrot[:, :, :, e0:e0 + HALF].rearrange("p (a j) s e -> p a s j e", a=2)
                    head = lambda v: v.rearrange("p (h f) -> p h f", h=H)
                    cos, sin = bc(rope[:, t, 0, :], 1, H), bc(rope[:, t, 1, :], 1, H)
                    in1, in2 = head(mid[:, 1, 0:256]), head(mid[:, 1, 256:512])
                    dve.tensor_tensor(head(lt1[:, :]), in1, cos, ALU.mult).then_inc(lrope.sem, 1)
                    dve.tensor_tensor(head(lt2[:, :]), in2, sin, ALU.mult).then_inc(lrope.sem, 1)
                    dve.wait_ge(*lrope.now(b, 6 * tt + 2))
                    parts = lambda v, a: v[:, 128 * a:128 * a + 128].rearrange("p (s j f) -> p s j f", s=2, j=4)
                    dve.tensor_tensor(q_out(DS)[:, 0], parts(lt1, 0), parts(lt2, 0), ALU.subtract)
                    dve.tensor_tensor(q_out(DS)[:, 1], parts(lt1, 1), parts(lt2, 1), ALU.subtract).then_inc(lrope.sem, 1)
                    dve.wait_ge(*lrope.now(b, 6 * tt + 3))
                    dve.tensor_tensor(head(lt1[:, :]), in2, cos, ALU.mult).then_inc(lrope.sem, 1)
                    dve.tensor_tensor(head(lt2[:, :]), in1, sin, ALU.mult).then_inc(lrope.sem, 1)
                    dve.wait_ge(*lrope.now(b, 6 * tt + 5))
                    dve.tensor_tensor(q_out(DS + HALF)[:, 0], parts(lt1, 0), parts(lt2, 0), ALU.add)
                    dve.tensor_tensor(q_out(DS + HALF)[:, 1], parts(lt1, 1), parts(lt2, 1), ALU.add).then_inc(lrope.sem, 1)
                    dve.wait_ge(*qt_hi_s.now(b, tt + 1))
                    dve.tensor_tensor(qo_lo[:, :, :].rearrange("p c q -> p (c q)"), flat(mid),
                                      qo_hi[:, :, :].rearrange("p c q -> p (c q)").bitcast(F32), ALU.subtract).then_inc(qt_lo_s.sem, 1)
                    for p in range(8):
                        dve.wait_ge(*ls_ps.now(b, 8 * tt + p + 1))
                        pair = big[:, 2 * (p % 2):2 * (p % 2) + 2, :]
                        dve.tensor_tensor(pair[:, :, keys - P:keys], pair[:, :, keys - P:keys], bc(causal, 1, 2), ALU.add).then_inc(lmasked.sem, 1)
                        dve.wait_ge(*lmasked.now(b, 8 * tt + p + 1))
                        dve.tensor_reduce(stat[:, tt, 0, 2 * p:2 * p + 2], pair[:, :, 0:keys], AX.X, ALU.max, negate=True).then_inc(lmax.sem, 1)
                    dve.wait_ge(*lexp.now(b, 8 * tt + 8))
                    dve.reciprocal(stat[:, tt, 3, :], stat[:, tt, 1, :]).then_inc(lnorm.sem, 1)
                    dve.wait_ge(*lnorm.now(b, 3 * tt + 1))
                    dve.wait_ge(*(pt_ps.now(b, t - 1)))
                    dve.memset(pr[:, t % 2, :, NB:NK], 0.0)
                    dve.tensor_tensor(pr[:, t % 2, :, 0:NB], probs_l[:, :, 0:NB], bc(stat[:, tt, 3, :], 2, NB), ALU.mult).then_inc(probs_s.sem, 1)
                    for a in range(2):
                        v = probs_l[:, 8 * a:8 * a + 8, NB:keys]
                        dve.tensor_tensor(v, v, bc(stat[:, tt, 3, 8 * a:8 * a + 8], 2, keys - NB), ALU.mult).then_inc(lnorm.sem, 1)
                    pooled_lo(b, t)
                    n0 = NPT[0] * tt
                    for n in range(NPT[tt] + 1):
                        if n < NPT[tt]:
                            dve.wait_ge(*tp_hi_s.now(b, n0 + n + 1))
                            dve.tensor_tensor(tp_lo[:, n % 2, :], mid[:, n % 2, :], tp_hi[:, n % 2, :].bitcast(F32), ALU.subtract).then_inc(tp_lo_s.sem, 1)
                        g = (n - 1) // (tt + 1)
                        if n >= 1 and n % (tt + 1) == 0:
                            dve.wait_ge(*o_hi_s.now(b, HKV * tt + g + 1))
                            r = slice(64 * (g % 2), 64 * (g % 2) + 64)
                            v = lambda q: q[r, 4 * (g // 2):4 * (g // 2) + 4, :].rearrange("p j q -> p (j q)")
                            dve.tensor_tensor(v(qo_lo), big[r, g, :], v(qo_hi).bitcast(F32), ALU.subtract).then_inc(o_lo_s.sem, 1)
                    residual_norm(b, t)
                    scale_x1(b, t)

        @block.tensor
        def _(pe):
            prime(pe, kgeo_ps, kv_ps, kp_ps, ktr_ps, klt_ps, m_ps, vwo_ps, qg_ps, s_ps, pt_ps, out_ps, x1t_ps, qp_ps,
                  qt_ps, ls_ps, tp_ps, pv_ps)
            pe.wait_ge(tab_in, 16 * 5)
            pe.wait_ge(wkv_in, 16)
            pe.wait_ge(wqs_scaled, DC)
            pe.wait_ge(wq_split, 2)
            pe.wait_ge(wo_split, 2)

            def transpose_probs(b, t):
                pe.wait_ge(*probs_s.now(b, t + 1))
                if t == 0:
                    pe.wait_ge(*kt_hi_s.now(b, 2))
                    pe.wait_ge(*kt_lo_s.now(b, 2))
                    pe.wait_ge(*vbd_s.now(b, 2))
                else:
                    pe.wait_ge(*pt_lo_s.now(b, t))
                    if t > 2:
                        pe.wait_ge(*x1t_s.now(b, t - 2 if t < RT else t))
                p = pr[:, t % 2, :, :].rearrange("p (a h) k -> p a (h k)", a=2)
                for a in range(2):
                    i = pe.transpose(tr[0:HK, P * a:P * a + P], p[:, a, :], ident[:, :])
                i.then_inc(pt_ps.sem, 1)

            def attend_pooled(b, t, last):
                pe.wait_ge(*pt_lo_s.now(b, t + 1))
                pe.wait_ge(*(added.now(b, t) if t else vwo_lo_s.now(b, 2)))
                for a in range(2):
                    i = three_passes(pe, acc[:, :], pt_hi[:, a, :], pt_lo[:, a, :], vwo_hi[:, a, :], vwo_lo[:, a, :],
                                     a == 0, last and a == 1)
                return i

            def transpose_x1(b, t):
                pe.wait_ge(*normed.now(b, t + 1))
                pe.wait_ge(*pt_lo_s.now(b, min(t + 3, RT) if t < RT else t + 1))
                if t:
                    pe.wait_ge(*x1t_s.now(b, t))
                for c in range(DC):
                    i = pe.transpose(tr[:, P * c:P * c + P], x1[:, t % 2, P * c:P * c + P], ident[:, :])
                i.then_inc(x1t_ps.sem, 1)

            with pe.Fori(0, B) as b:
                pe.wait_ge(*xt_in.now(b, 16))
                pe.wait_ge(*o_lo_s.last(b, HKV * LT))
                for t in range(RT):
                    for c in range(DC):
                        i = pe.matmul(qf[:, P * t:P * t + P], xt[:, c, P * t:P * t + P], wkv[:, c, 0:128],
                                      start=(c == 0), stop=(c == DC - 1))
                i.then_inc(kgeo_ps.sem, 1)
                for t in range(LT):
                    for c in range(DC):
                        i = pe.matmul(big[:, 2 + t, :], xt[:, c, REMOTE + P * t:REMOTE + P * t + P], wkv[:, c, :],
                                      start=(c == 0), stop=(c == DC - 1))
                    i.then_inc(kv_ps.sem, 1)
                pe.wait_ge(*xpool_s.now(b, 1))
                pe.wait_ge(*added.last(b, TILES))
                for c in range(DC):
                    pe.matmul(acc[0:NK, 128:512], xpool[:, c, :], wkv[:, c, 128:512], start=(c == 0), stop=(c == DC - 1))
                pe.wait_ge(*krope.now(b, 6))
                for t in range(RT):
                    i = pe.matmul(acc[0:NB, 0:128], pool_w[:, t, :], kgr[:, t, :], start=(t == 0), stop=(t == RT - 1))
                i.then_inc(kp_ps.sem, 1)
                pe.wait_ge(*krot_sem.now(b, 1))
                pe.wait_ge(*krope.now(b, 12))
                pe.wait_ge(*tp_lo_s.last(b, sum(NPT)))
                for a in range(2):
                    for t in range(LT):
                        i = pe.transpose(mid[:, 1, 256 * a + P * t:256 * a + P * t + P],
                                         krot[:, t, 2 * a:2 * a + 2, :].rearrange("p g e -> p (g e)"), ident[:, :])
                i.then_inc(klt_ps.sem, 1)
                pe.wait_ge(*kr_s.now(b, 6))
                pe.wait_ge(*x1t_s.last(b, TILES))
                pe.sem_inc(pe_past, 1)
                for s in range(8):
                    pe.transpose(tr[:, 16 * s:16 * s + NB], kr[0:NB, P * s:P * s + P], ident[0:NB, 0:NB])
                for a in range(2):
                    pe.transpose(tr[:, 16 * (8 + a):16 * (8 + a) + NK], kp[:, 256 + P * a:256 + P * a + P], ident[0:NK, 0:NK])
                for a in range(2):
                    i = pe.transpose(tr[:, 16 * (10 + a):16 * (10 + a) + NB], kr[0:NB, 1024 + P * a:1024 + P * a + P], ident[0:NB, 0:NB])
                i.then_inc(ktr_ps.sem, 1)
                pe.wait_ge(*bd_s.now(b, 2))
                for c in range(DC):
                    for g in range(HKV):
                        i = pe.matmul(big[:, c // 2, H * NB * (c % 2) + 4 * NB * g:H * NB * (c % 2) + 4 * NB * (g + 1)],
                                      wqs[:, g, P * c:P * c + P], ks_bd[:, g, :], start=True, stop=True)
                i.then_inc(m_ps.sem, 1)
                pe.wait_ge(*vb_lo_s.now(b, 1))
                pe.wait_ge(*v_lo_s.now(b, 1))
                for a in range(2):
                    for j in range(4):
                        o = (4 * a + j) * HK
                        i = three_passes(pe, big[0:HK, 2 + a, :], vb_hi[:, o:o + HK], vb_lo[:, o:o + HK],
                                         wo_hi[:, 4 * a + j, :], wo_lo[:, 4 * a + j, :], j == 0, j == 3)
                    i.then_inc(vwo_ps.sem, 1)

                def project_geo(n):
                    pe.wait_ge(*xs_lo_s.now(b, n + 1))
                    if n == 0:
                        pe.wait_ge(*m_s.now(b, 1))
                    elif n == 1:
                        pe.wait_ge(*vwo_lo_s.now(b, 2))
                    else:
                        pe.wait_ge(*qrope.now(b, 6 * (n - 1)))
                    for r in range(2):
                        for a in range(2):
                            for c in range(DC):
                                w = slice(512 + 256 * r + 128 * a, 512 + 256 * r + 128 * a + 128)
                                i = three_passes(pe, big[:, 2 * (n % 2) + r, QB * a:QB * a + QB], wq_hi[:, c, w], wq_lo[:, c, w],
                                                 xs_hi[:, n % 2, c, :], xs_lo[:, n % 2, c, :], c == 0, c == DC - 1)
                    i.then_inc(qg_ps.sem, 1)

                def scores(t):
                    pe.wait_ge(*qrope.now(b, 6 * (t // 2 + 1)))
                    pe.wait_ge(*m_s.now(b, 1))
                    if t >= 2:
                        pe.wait_ge(*masked.now(b, 2 * (t - 2) + 1))
                    else:
                        pe.wait_ge(*kt_lo_s.now(b, 1))
                    plain = lambda c: pe.matmul(mid[:, t % 2, 0:H * NB], xt[:, c, P * t:P * t + P], m_sb[:, c, :],
                                                start=(c == 0), stop=(c == DC - 1))
                    for c in range(DC - 1):
                        plain(c)
                    for a in range(2):
                        for r in range(2):
                            q = q_rem[:, t // 2, r, QB * a + P * (t % 2):QB * a + P * (t % 2) + P]
                            pe.matmul(mid[:, t % 2, HB * a:HB * a + HB], q, kg_bd[:, 2 * r + a, :],
                                      start=False, stop=False, skip_group_check=True)
                    plain(DC - 1).then_inc(s_ps.sem, 1)

                project_geo(0)
                project_geo(1)
                for t in range(RT + 3):
                    if t < RT:
                        scores(t)
                    if t == 0:
                        project_geo(2)
                    if 1 <= t <= RT:
                        transpose_probs(b, t - 1)
                    if 2 <= t < RT + 2:
                        attend_pooled(b, t - 2, True).then_inc(out_ps.sem, 1)
                    if t >= 3:
                        transpose_x1(b, t - 3)
                n0 = 0
                for tt in range(LT):
                    t = RT + tt
                    keys = NB + P * (tt + 1)
                    pe.wait_ge(*xs_lo_s.now(b, RB + 1))
                    if tt == 0:
                        pe.wait_ge(*masked.now(b, 2 * RT - 1))
                    else:
                        pe.wait_ge(*tp_lo_s.now(b, n0))
                    for s in range(2):
                        for c in range(DC):
                            k = slice(P * tt, P * tt + P)
                            i = three_passes(pe, mid[:, s, :], xs_hi[:, 1, c, k], xs_lo[:, 1, c, k],
                                             wq_hi[:, c, 512 * s:512 * s + 512], wq_lo[:, c, 512 * s:512 * s + 512], c == 0, c == DC - 1)
                    i.then_inc(qp_ps.sem, 1)
                    pe.wait_ge(*qsem_s.now(b, tt + 1))
                    pe.wait_ge(*lrope.now(b, 6 * tt + 6))
                    for c in range(8):
                        i = pe.transpose(mid[:, c // 4, P * (c % 4):P * (c % 4) + P], qrot[:, c, :, :].rearrange("p s e -> p (s e)"), ident[:, :])
                    i.then_inc(qt_ps.sem, 1)
                    pe.wait_ge(*qt_lo_s.now(b, tt + 1))
                    pe.wait_ge(*kt_lo_s.now(b, 2))
                    for p in range(8):
                        if p >= 2:
                            pe.wait_ge(*lexp.now(b, 8 * tt + p - 1))
                        elif tt:
                            pe.wait_ge(*o_lo_s.now(b, HKV * tt))
                        else:
                            pe.wait_ge(*qrope.now(b, 6 * RB))
                        for h in (2 * p, 2 * p + 1):
                            a, s, j = h // 8, h // 4 % 2, h % 4
                            r = slice(64 * s, 64 * s + 64)
                            i = three_passes(pe, big[:, 2 * (p % 2) + h % 2, 0:keys], qo_hi[r, 4 * a + j, :], qo_lo[r, 4 * a + j, :],
                                             kt_hi[r, a, 0:keys], kt_lo[r, a, 0:keys], True, True)
                        i.then_inc(ls_ps.sem, 1)
                    transpose_probs(b, t)
                    for n in range(NPT[tt] + 1):
                        if n < NPT[tt]:
                            g, k = divmod(n, tt + 1)
                            if n == 0:
                                pe.wait_ge(*lnorm.now(b, 3 * tt + 3))
                            if n >= 2:
                                pe.wait_ge(*tp_lo_s.now(b, n0 + n - 1))
                            for j in range(4):
                                i = pe.transpose(mid[:, n % 2, P * j:P * j + P], probs_l[:, 4 * g + j, NB + P * k:NB + P * k + P], ident[:, :])
                            i.then_inc(tp_ps.sem, 1)
                        if n >= 1:
                            g, k = divmod(n - 1, tt + 1)
                            pe.wait_ge(*tp_lo_s.now(b, n0 + n))
                            w = slice(P * (g // 2), P * (g // 2) + P)
                            m = (n - 1) % 2
                            i = three_passes(pe, big[:, g, :], v_hi[:, k, w], v_lo[:, k, w], tp_hi[:, m, :], tp_lo[:, m, :], k == 0, k == tt)
                            i.then_inc(pv_ps.sem, 1)
                    n0 += NPT[tt]
                    attend_pooled(b, t, False)
                    pe.wait_ge(*o_lo_s.now(b, HKV * (tt + 1)))
                    for c in range(8):
                        i = three_passes(pe, acc[:, :], qo_hi[:, c, :], qo_lo[:, c, :], wo_hi[:, c, :], wo_lo[:, c, :], False, c == 7)
                    i.then_inc(out_ps.sem, 1)
                    transpose_x1(b, t)


def weights_block(nc, sems, io, ctx):
    keep, _, _, _ = tools(nc, ctx, sems, "w")
    wg, wu, wd = keep("wg", [P, DC, INTER]), keep("wu", [P, DC, INTER]), keep("wd", [P, IC, D])
    ug_scale = keep("ug_scale", [P, 2, IC])
    inner = ExitStack()
    with inner:
        sb, ps, _, sem = tools(nc, inner, sems, "wp")
        had = sb("had", [P, 2, P])
        hr = sb("hr", [P, 2, P], F32R)
        su = sb("su", [P, DC])
        sd = sb("sd", [P, IC])
        dps = sb("dps", [P, D])
        hi, lo = sb("hi", [P, 2, 4, 512], F32R), sb("lo", [P, 2, 4, 512], F32R)
        out = ps("out", [P, 8, 512])
        had_in, hr_s, sc_in, sc_s = sem("had_in"), sem("hr_s"), sem("sc_in"), sem("sc_s")
        piece_in, hi_s, lo_s, mm_s, ev_s = [sem(f"piece_in{i}") for i in range(2)], sem("hi_s"), sem("lo_s"), sem("mm_s"), sem("ev_s")
        pieces = [("g", n) for n in range(4)] + [("u", n) for n in range(4)] + [("d", n) for n in range(4)]
        stage = sb("stage", [P, 2, 4, 512])
        dn = sb("dn", [P, IC, D])
        dn_in, outer_s = sem("dn_in"), sem("outer_s")
        block = inner.enter_context(nc.Block())

        @block.sync
        def _(sp):
            sp.dma_start(had[:, :, :], io["had"]).then_inc(had_in, 16)
            for t, n in ((su, "su"), (sd, "sd"), (dps, "dps"), (ug_scale, "ug_scale")):
                sp.dma_start(t[:], io[n]).then_inc(sc_in, 16)
            for i, (m, n) in enumerate(pieces[0:8]):
                if i >= 2:
                    sp.wait_ge(lo_s, i - 1)
                sp.dma_start(stage[:, i % 2, :, :], io["wg" if m == "g" else "wu"][:, :, 512 * n:512 * n + 512]).then_inc(piece_in[i % 2], 16)

        @block.gpsimd
        def _(pool):
            pool.dma_start(dn[:, :, :], io["wd"]).then_inc(dn_in, 16)

        def source(i):
            return stage[:, i % 2, :, :] if i < 8 else dn[:, 4 * (i - 8):4 * (i - 8) + 4, :]

        @block.scalar
        def _(act):
            act.wait_ge(had_in, 16)
            act.activation(hr[:, :, :], had[:, :, :], ACT.Copy).then_inc(hr_s, 1)
            for i, (m, n) in enumerate(pieces):
                if i < 8:
                    act.wait_ge(piece_in[i % 2], 16 * (i // 2 + 1))
                else:
                    act.wait_ge(outer_s, 1)
                if i >= 2:
                    act.wait_ge(mm_s, 4 * (i - 1))
                act.activation(hi[:, i % 2, :, :], source(i), ACT.Copy).then_inc(hi_s, 1)

        @block.vector
        def _(dve):
            dve.wait_ge(sc_in, 64)
            dve.tensor_scalar(ug_scale[:, :, :], ug_scale[:, :, :], float(D) ** -0.5, None, ALU.mult).then_inc(sc_s, 1)
            dve.tensor_scalar(dps[:, :], dps[:, :], float(INTER) ** -0.5, None, ALU.mult).then_inc(sc_s, 1)
            dve.wait_ge(sc_s, 2)

            def evacuate(i):
                m, n = pieces[i]
                for c in range(4):
                    dve.wait_ge(mm_s, 4 * i + c + 1)
                    src = out[:, (4 * i + c) % 8, :]
                    if m == "d":
                        k = 4 * n + c
                        dve.scalar_tensor_tensor(wd[:, k, :], src, sd[:, k:k + 1], dps[:, :], ALU.mult, ALU.mult).then_inc(ev_s, 1)
                    else:
                        dst = (wg if m == "g" else wu)[:, c, 512 * n:512 * n + 512]
                        dve.tensor_scalar(dst, src, su[:, c:c + 1], None, ALU.mult).then_inc(ev_s, 1)

            def outer():
                dve.wait_ge(dn_in, 16)
                v = lambda t, a: t[:, :, :].rearrange("p (g c) n -> p g (c n)", g=4)[:, a, :]
                w = lambda a: v(dn, a)
                for op, (x, y), d in ((ALU.add, (0, 2), 0), (ALU.subtract, (0, 2), 2), (ALU.add, (1, 3), 1), (ALU.subtract, (1, 3), 3)):
                    i = dve.tensor_tensor(v(wd, d), w(x), w(y), op)
                i.then_inc(sc_s, 1)
                dve.wait_ge(sc_s, 3)
                for k, (op, (x, y), d) in enumerate(((ALU.add, (0, 1), 0), (ALU.subtract, (0, 1), 1), (ALU.add, (2, 3), 2), (ALU.subtract, (2, 3), 3))):
                    i = dve.tensor_tensor(w(d), v(wd, x), v(wd, y), op)
                i.then_inc(outer_s, 1)

            for i in range(len(pieces)):
                if i == 2:
                    outer()
                dve.wait_ge(hi_s, i + 1)
                if i >= 2:
                    dve.wait_ge(mm_s, 4 * (i - 1))
                if i == 8:
                    dve.wait_ge(outer_s, 1)
                dve.tensor_tensor(lo[:, i % 2, :, :], source(i), hi[:, i % 2, :, :].bitcast(F32), ALU.subtract).then_inc(lo_s, 1)
                if i:
                    evacuate(i - 1)
            evacuate(len(pieces) - 1)

        @block.tensor
        def _(pe):
            pe.wait_ge(hr_s, 1)
            for i in range(len(pieces)):
                pe.wait_ge(lo_s, i + 1)
                for c in range(4):
                    k = 4 * i + c
                    if k >= 8:
                        pe.wait_ge(ev_s, k - 7)
                    for s in range(4):
                        sign = bin(c & s).count("1") % 2
                        pe.matmul(out[:, k % 8, :], hr[:, sign, :], hi[:, i % 2, s, :], start=(s == 0), stop=False)
                        j = pe.matmul(out[:, k % 8, :], hr[:, sign, :], lo[:, i % 2, s, :], start=False, stop=(s == 3))
                    j.then_inc(mm_s, 1)
    return wg, wu, wd, ug_scale


def ffn_block(nc, sems, x1_dram, x1t_dram, out_dram, wg, wu, wd, ug_scale):
    ctx = ExitStack()
    with ctx:
        sb, ps, signal, sem = tools(nc, ctx, sems, "ff")
        gu_hi = [sb(f"gu_hi{i}", [P, 2, DC, P], F32R) for i in range(2)]
        gu_lo = [sb(f"gu_lo{i}", [P, 2, DC, P], F32R) for i in range(2)]
        d_hi = [sb(f"d_hi{i}", [P, D], F32R) for i in range(2)]
        d_lo = [sb(f"d_lo{i}", [P, D], F32R) for i in range(2)]
        xraw = sb("xraw", [P, FT, DC, P])
        x_hi = [sb(f"x_hi{i}", [P, DC, FB], F32R) for i in range(2)]
        x_lo = [sb(f"x_lo{i}", [P, DC, FB], F32R) for i in range(2)]
        sg, hf = [sb(f"sg{i}", [P, FB]) for i in range(2)], [sb(f"hf{i}", [P, FB]) for i in range(2)]
        h_hi = [sb(f"h_hi{i}", [P, FB], F32R) for i in range(2)]
        h_lo = [sb(f"h_lo{i}", [P, FB], F32R) for i in range(2)]
        y = sb("y", [P, FT, D])
        bn, mv, rstd, power = sb("bn", [P, FT, 6]), sb("mv", [P, FT, 2]), sb("rstd", [P, FT]), sb("power", [P, 2, FT])
        acc = ps("acc", [P, FT, 512])
        g_ps, u_ps = ps("g_ps", [P, 512]), ps("u_ps", [P, 512])

        gate_s, up_s, down_s = signal("gate_s", 1), signal("up_s", 1), signal("down_s", 1)
        silu_s, prod_s, h_hi_s, h_lo_s = signal("silu_s", 1), signal("prod_s", 1), signal("h_hi_s", 1), signal("h_lo_s", 1)
        gu_hi_s, gu_lo_s, d_hi_s, d_lo_s = signal("gu_hi_s", 1), signal("gu_lo_s", 1), signal("d_hi_s", 1), signal("d_lo_s", 1)
        xraw_in, x1_in, x_hi_s, x_lo_s = signal("xraw_in", 16), signal("x1_in", 16), signal("x_hi_s", 1), signal("x_lo_s", 1)
        added, bn_s, var_s, rstd_s, normed, stored = (signal("added", FT), signal("bn_s", 2 * FT), signal("var_s", 1),
                                                      signal("rstd_s", 1), signal("normed", 1), signal("stored", 16))
        power_set, dve_past = sem("power_set"), sem("dve_past")

        def prime(eng, *signals):
            for s in signals:
                eng.sem_inc(s.sem, s.per)

        def blocks(eng, body):
            with eng.Fori(0, FBLK // 2 - 1) as pair:
                body(pair * 2, 0, False)
                body(pair * 2 + 1, 1, False)
            body(FBLK - 2, 0, False)
            body(FBLK - 1, 1, True)

        def steps(eng, step):
            step(1, 1, False)
            with eng.Fori(0, (IC - 4) // 2) as j:
                step(j * 2 + 2, 0, False)
                step(j * 2 + 3, 1, False)
            step(IC - 2, 0, False)
            step(IC - 1, 1, False)
            step(IC, 0, True)

        block = ctx.enter_context(nc.Block())

        @block.sync
        def _(sp):
            prime(sp, xraw_in, x1_in, stored)

            def load(blk):
                sp.wait_ge(*x_lo_s.last(blk, 1))
                sp.wait_ge(*x_hi_s.last(blk, 1))
                sp.dma_start(xraw[:, :, :, :], x1t_dram[blk]).then_inc(xraw_in.sem, 16)

            def body(blk, parity, last):
                if not last:
                    load(blk + 1)
                sp.wait_ge(*stored.last(blk, 16))
                sp.dma_start(y[:, :, :], x1_dram[blk]).then_inc(x1_in.sem, 16)
                sp.wait_ge(*normed.now(blk, 1))
                sp.dma_start(out_dram[blk], y[:, :, :]).then_inc(stored.sem, 16)

            load(0)
            blocks(sp, body)
            sp.wait_ge(*stored.now(FBLK - 1, 16))

        @block.gpsimd
        def _(pool):
            prime(pool, var_s, rstd_s)
            pool.memset(power[:, 0, :], -0.5).then_inc(power_set, 1)
            pool.memset(power[:, 1, :], EPS).then_inc(power_set, 1)
            pool.wait_ge(power_set, 2)
            with pool.Fori(0, FBLK) as blk:
                pool.wait_ge(*bn_s.now(blk, 2 * FT))
                pool.wait_ge(*normed.last(blk, 1))
                pool.tensor_tensor(rstd[:, :], mv[:, :, 1], power[:, 1, :], ALU.add).then_inc(var_s.sem, 1)
                pool.wait_ge(*var_s.now(blk, 1))
                pool.tensor_tensor(rstd[:, :], rstd[:, :], power[:, 0, :], ALU.pow).then_inc(rstd_s.sem, 1)

        def gate_up_chunk(w, i):
            return w[:, :, bass.ds(i * P, P)]

        @block.scalar
        def _(act):
            prime(act, silu_s, h_hi_s, gu_hi_s, d_hi_s, x_hi_s)

            def split_x(blk, p):
                act.wait_ge(*xraw_in.now(blk, 16))
                act.activation(x_hi[p][:, :, :].rearrange("p c (t q) -> p t c q", t=FT), xraw[:, :, :, :], ACT.Copy).then_inc(x_hi_s.sem, 1)

            def split_gu(s, i, q):
                act.wait_ge(up_s.sem, s)
                act.activation(gu_hi[q][:, 0, :, :], gate_up_chunk(wg, i), ACT.Copy)
                act.activation(gu_hi[q][:, 1, :, :], gate_up_chunk(wu, i), ACT.Copy).then_inc(gu_hi_s.sem, 1)

            def chunk_work(s, i, q):
                act.wait_ge(*gate_s.now(s, 1))
                if not isinstance(s, int) or s > 0:
                    act.wait_ge(prod_s.sem, s)
                act.activation(sg[q][:, :], g_ps[:, :], ACT.Silu, scale=ug_scale[:, 1, bass.ds(i, 1)]).then_inc(silu_s.sem, 1)
                if not isinstance(s, int) or s > 0:
                    act.wait_ge(down_s.sem, s)
                act.activation(d_hi[q][:, :], wd[:, bass.ds(i, 1), :].rearrange("p a n -> p (a n)"), ACT.Copy).then_inc(d_hi_s.sem, 1)

            def round_h(s, q):
                act.wait_ge(*prod_s.now(s, 1))
                act.activation(h_hi[q][:, :], hf[q][:, :], ACT.Copy).then_inc(h_hi_s.sem, 1)

            def body(blk, parity, last):
                def step(i, q, wrap):
                    s = blk * IC + i
                    if wrap and last:
                        return
                    if wrap:
                        chunk_work(s, 0, q)
                        split_gu(s + 1, 1, 1 - q)
                        round_h(s, q)
                        return
                    chunk_work(s, i, q)
                    if isinstance(i, int) and i == IC - 1:
                        if not last:
                            split_gu(s + 1, 0, 1 - q)
                    else:
                        split_gu(s + 1, i + 1, 1 - q)
                    round_h(s, q)
                    if isinstance(i, int) and i == 1 and not last:
                        split_x(blk + 1, 1 - parity)

                steps(act, step)

            split_x(0, 0)
            act.activation(gu_hi[0][:, 0, :, :], wg[:, :, 0:P], ACT.Copy)
            act.activation(gu_hi[0][:, 1, :, :], wu[:, :, 0:P], ACT.Copy).then_inc(gu_hi_s.sem, 1)
            chunk_work(0, 0, 0)
            split_gu(1, 1, 1)
            round_h(0, 0)
            blocks(act, body)

        @block.vector
        def _(dve):
            prime(dve, prod_s, h_lo_s, gu_lo_s, d_lo_s, x_lo_s, added, bn_s, normed)

            def split_x(blk, p):
                dve.wait_ge(*x_hi_s.now(blk, 1))
                v = lambda t: t[:, :, :].rearrange("p c (t q) -> p t c q", t=FT)
                for t in range(FT):
                    i = dve.tensor_tensor(v(x_lo[p])[:, t], xraw[:, t, :, :], v(x_hi[p])[:, t].bitcast(F32), ALU.subtract)
                i.then_inc(x_lo_s.sem, 1)

            def split_gu(s, i, q):
                dve.wait_ge(*gu_hi_s.now(s, 1))
                dve.tensor_tensor(gu_lo[q][:, 0, :, :], gate_up_chunk(wg, i), gu_hi[q][:, 0, :, :].bitcast(F32), ALU.subtract)
                dve.tensor_tensor(gu_lo[q][:, 1, :, :], gate_up_chunk(wu, i), gu_hi[q][:, 1, :, :].bitcast(F32), ALU.subtract).then_inc(gu_lo_s.sem, 1)

            def chunk_work(s, i, q):
                dve.wait_ge(*d_hi_s.now(s, 1))
                dve.tensor_tensor(d_lo[q][:, :], wd[:, bass.ds(i, 1), :].rearrange("p a n -> p (a n)"), d_hi[q][:, :].bitcast(F32),
                                  ALU.subtract).then_inc(d_lo_s.sem, 1)
                dve.wait_ge(*up_s.now(s, 1))
                dve.wait_ge(*silu_s.now(s, 1))
                dve.scalar_tensor_tensor(hf[q][:, :], u_ps[:, :], ug_scale[:, 0, bass.ds(i, 1)], sg[q][:, :], ALU.mult, ALU.mult).then_inc(prod_s.sem, 1)

            def lower_h(s, q):
                dve.wait_ge(*h_hi_s.now(s, 1))
                dve.wait_ge(*prod_s.now(s, 1))
                dve.tensor_tensor(h_lo[q][:, :], hf[q][:, :], h_hi[q][:, :].bitcast(F32), ALU.subtract).then_inc(h_lo_s.sem, 1)

            def finish(blk):
                dve.wait_ge(*x1_in.now(blk, 16))
                for t in range(FT):
                    dve.wait_ge(down_s.sem, (blk + 1) * IC + 1)
                    dve.tensor_tensor(y[:, t, :], acc[:, t, :], y[:, t, :], ALU.add).then_inc(added.sem, 1)
                for t in range(FT):
                    dve.wait_ge(*added.now(blk, t + 1))
                    dve.bn_stats(bn[:, t, :], y[:, t, :]).then_inc(bn_s.sem, 1)
                dve.wait_ge(*bn_s.now(blk, FT))
                dve.sem_inc(dve_past, 1)
                for t in range(FT):
                    dve.bn_aggr(mv[:, t, :], bn[:, t, :]).then_inc(bn_s.sem, 1)

            def normalise(blk):
                dve.wait_ge(*rstd_s.now(blk, 1))
                for t in range(FT):
                    i = dve.tensor_scalar(y[:, t, :], y[:, t, :], mv[:, t, 0:1], rstd[:, t:t + 1], ALU.subtract, ALU.mult)
                i.then_inc(normed.sem, 1)

            def body(blk, parity, last):
                def step(i, q, wrap):
                    s = blk * IC + i
                    if wrap and last:
                        return
                    nxt = 0 if isinstance(i, int) and i == IC - 1 else (1 if wrap else i + 1)
                    if not (last and isinstance(i, int) and i == IC - 1):
                        split_gu(s + 1, nxt, 1 - q)
                    chunk_work(s, 0 if wrap else i, q)
                    lower_h(s, q)
                    if isinstance(i, int) and i == 1 and not last:
                        split_x(blk + 1, 1 - parity)

                steps(dve, step)
                finish(blk)
                normalise(blk)

            split_x(0, 0)
            split_gu(0, 0, 0)
            split_gu(1, 1, 1)
            chunk_work(0, 0, 0)
            lower_h(0, 0)
            blocks(dve, body)

        @block.tensor
        def _(pe):
            prime(pe, gate_s, up_s, down_s)

            def gate_up(s, q, p):
                pe.wait_ge(*gu_lo_s.now(s, 1))
                for m, bank, free, done in ((0, g_ps, silu_s, gate_s), (1, u_ps, prod_s, up_s)):
                    pe.wait_ge(free.sem, s + 1)
                    for c in range(DC):
                        i = three_passes(pe, bank[:, :], gu_hi[q][:, m, c, :], gu_lo[q][:, m, c, :], x_hi[p][:, c, :], x_lo[p][:, c, :],
                                         c == 0, c == DC - 1)
                    i.then_inc(done.sem, 1)

            def down(s, q, first, last):
                pe.wait_ge(*h_lo_s.now(s, 1))
                pe.wait_ge(*d_lo_s.now(s, 1))
                for t in range(FT):
                    k = slice(P * t, P * t + P)
                    i = three_passes(pe, acc[:, t, :], h_hi[q][:, k], h_lo[q][:, k], d_hi[q][:, :], d_lo[q][:, :], first, last)
                i.then_inc(down_s.sem, 1)

            def body(blk, parity, last):
                def step(i, q, wrap):
                    s = blk * IC + i
                    if wrap:
                        if not last:
                            pe.wait_ge(*x_lo_s.now(blk + 1, 1))
                            gate_up(s, q, 1 - parity)
                        down(s - 1, 1 - q, False, True)
                        return
                    gate_up(s, q, parity)
                    first = isinstance(i, int) and i == 1
                    if first:
                        pe.wait_ge(*added.last(blk, FT))
                    down(s - 1, 1 - q, first, False)

                steps(pe, step)

            pe.wait_ge(*x_lo_s.now(0, 1))
            gate_up(0, 0, 0)
            blocks(pe, body)


def layer_kernel(nc, io, out):
    x1_dram = nc.dram_tensor("x1_scratch", [B * T, D], F32, kind="Internal").ap()
    x1t_dram = nc.dram_tensor("x1t_scratch", [B * TILES, P, D], F32, kind="Internal").ap()
    io["x"] = io["x"].rearrange("b (t p) d -> b t p d", p=P)
    sems = ExitStack()
    with sems:
        whole_layer(nc, sems, io, x1_dram, x1t_dram, out)


def whole_layer(nc, sems, io, x1_dram, x1t_dram, out):
    attention_block(nc, sems, io, x1_dram.rearrange("(b t p) d -> b t p d", t=TILES, p=P),
                    x1t_dram.rearrange("(b t) p d -> b t p d", t=TILES))
    ctx = ExitStack()
    with ctx:
        folded = weights_block(nc, sems, io, ctx)
        ffn_block(nc, sems, x1_dram.rearrange("(n t p) d -> n p t d", t=FT, p=P),
                  x1t_dram.rearrange("(n t) p (c q) -> n p t c q", t=FT, c=DC),
                  out.rearrange("b (m t p) d -> (b m) p t d", t=FT, p=P), *folded)


def shape_tables():
    import numpy as np
    f = np.float32
    p = np.arange(P)
    inv = f(1.0) / (f(10000.0) ** (np.arange(0, DG, 2, dtype=f) / f(DG)))
    ang = np.arange(T, dtype=f)[:, None] * inv.astype(f)[None, :]
    cos, sin = np.cos(ang).astype(f), np.sin(ang).astype(f)
    rope = np.stack([cos, sin], 1).reshape(TILES, P, 2, HALF).transpose(1, 0, 2, 3)
    own = lambda n, w, k: np.repeat((p[:, None] // w == np.arange(n)[None, :]).astype(f), k, axis=1)
    pos = np.arange(REMOTE).reshape(RT, P).T[:, :, None]
    k = np.arange(NB)[None, None, :]
    pool_w = np.where(pos // MB == k, f(1.0 / MB), f(0)).astype(f)
    sees = MB * k + MB - 1 <= pos
    keep, hide = sees.astype(f), np.where(sees, f(0), f(NEG)).astype(f)
    none = ~sees.any(-1)
    spread, rest = np.where(none, f(KEYS / NB), f(1)).astype(f), np.where(none, f(1.0 / KEYS), f(0)).astype(f)
    causal = np.where(p[None, :] <= p[:, None], f(0), f(NEG)).astype(f)
    small = np.concatenate([own(4, DS, NB), own(8, HALF, NB), own(2, DV, NK), pool_w.reshape(P, -1), keep.reshape(P, -1),
                            hide.reshape(P, -1), spread, rest, causal], axis=1)
    had = np.array([[1 - 2 * (bin(i & j).count("1") % 2) for j in range(P)] for i in range(P)], f)
    return {"ident": np.eye(P, dtype=f), "cos_t": np.tile(cos[:REMOTE].T, (P // HALF, 1)), "sin_t": np.tile(sin[:REMOTE].T, (P // HALF, 1)),
            "rope": rope, "small": small, "had": np.stack([had, -had], 1)}


def kernel(**inputs):
    import numpy as np
    import concourse.bacc as bacc
    from concourse.bass_utils import run_bass_kernel_spmd as run

    a = {n: np.asarray(v) for n, v in inputs.items()}
    x = a["L0_attn_x"]
    rows = lambda w: w.reshape(w.shape[0] // P, P, -1).transpose(1, 0, 2)
    halves = lambda w, h: w.reshape(D, h, 2, HALF).transpose(0, 2, 1, 3).reshape(D, -1)
    ls = a["L0_attn_logit_scale"]
    chunk_rows = np.repeat(ls, DS).reshape(DC, P).T
    wo = a["L0_attn_Wo"].reshape(2, 2, 4, DV, D).transpose(1, 3, 0, 2, 4).reshape(P, 8, D)
    arrays = {
        "x": x,
        "xt": x.transpose(0, 2, 1).reshape(B, DC, P, T).transpose(0, 2, 1, 3),
        "wq": rows(np.concatenate([a["L0_attn_Wq_sem"], halves(a["L0_attn_Wq_geo"], H)], 1)),
        "wqs": rows(a["L0_attn_Wq_sem"].T),
        "wkv": rows(np.concatenate([halves(a["L0_attn_Wk_geo"], HKV), a["L0_attn_Wk_sem"], a["L0_attn_Wv"]], 1)),
        "wo": wo,
        "logit_scale": np.concatenate([np.broadcast_to(ls, (P, H)), chunk_rows], 1),
        "wg": rows(a["L0_ffn_W_gate"].T), "wu": rows(a["L0_ffn_W_up"].T), "wd": rows(a["L0_ffn_W_down"].T),
        "su": a["L0_ffn_SU_ug"].reshape(DC, P).T, "sd": a["L0_ffn_SU_dp"].reshape(IC, P).T,
        "dps": np.broadcast_to(a["L0_ffn_Wscale_dp"], (P, D)),
        "ug_scale": a["L0_ffn_Wscale_ug"].reshape(2, IC, P).transpose(2, 0, 1),
        **shape_tables(),
    }
    arrays = {f"in_{n}": np.ascontiguousarray(v) for n, v in arrays.items()}
    nc = bacc.Bacc("TRN2", target_bir_lowering=False, num_devices=1)
    io = {n[3:]: nc.dram_tensor(n, v.shape, mybir.dt.from_np(v.dtype), kind="ExternalInput").ap() for n, v in arrays.items()}
    out = nc.dram_tensor("out", (B, T, D), F32, kind="ExternalOutput").ap()
    layer_kernel(nc, io, out)
    return run(nc, [arrays], core_ids=[0]).results[0]["out"]
```

```python
from contextlib import ExitStack

import concourse.bass as bass
from concourse import mybir

F32 = mybir.dt.float32
F32R = mybir.dt.float32r
ACT = mybir.ActivationFunctionType
ALU = mybir.AluOpType
AX = mybir.AxisListType

P = 128
B, T, D = 4, 1024, 512
H, HKV, DS, DG, DV = 16, 4, 32, 32, 64
REP = H // HKV
MB, LW = 64, 256
REMOTE = T - LW
NB = REMOTE // MB
NK = NB + 1
HALF = DG // 2
INTER = 2048
DC = D // P
IC = INTER // P
RT = REMOTE // P
LT = LW // P
TILES = RT + LT
QB = 256
RB = REMOTE // QB
NEG = -1.0e9
EPS = 1e-5
KEYS = NB + LW
HK = H // 2 * NK
HB = H // 2 * NB
FB = 512
FBLK = B * T // FB
FT = FB // P


class Signal:

    def __init__(self, ctx, nc, name, per):
        self.sem, self.per = ctx.enter_context(nc.semaphore(name)), per

    def now(self, i, k):
        return self.sem, (i + 1) * self.per + k

    def last(self, i, k):
        return self.sem, i * self.per + k


def tools(nc, ctx, sems, tag):
    def sb(name, shape, dt=F32):
        return ctx.enter_context(nc.sbuf_tensor(f"{tag}_{name}", shape, dt))

    def ps(name, shape):
        return ctx.enter_context(nc.psum_tensor(f"{tag}_{name}", shape, F32))

    def signal(name, per):
        return Signal(sems, nc, f"{tag}_{name}", per)

    def sem(name):
        return sems.enter_context(nc.semaphore(f"{tag}_{name}"))

    return sb, ps, signal, sem


def three_passes(pe, out, lhs_hi, lhs_lo, rhs_hi, rhs_lo, first, last):
    pe.matmul(out, lhs_hi, rhs_hi, start=first, stop=False)
    pe.matmul(out, lhs_hi, rhs_lo, start=False, stop=False)
    return pe.matmul(out, lhs_lo, rhs_hi, start=False, stop=last)


def bc(ap, axis, n):
    wide = ap.unsqueeze(axis)
    shape = list(wide.shape)
    shape[axis] = n
    return wide.broadcast_to(shape)


def attention_block(nc, sems, io, x1_dram, x1t_dram):
    ctx = ExitStack()
    with ctx:
        sb, ps, signal, sem = tools(nc, ctx, sems, "at")
        wq_hi, wq_lo = sb("wq_hi", [P, DC, 2 * D], F32R), sb("wq_lo", [P, DC, 2 * D], F32R)
        wo_hi, wo_lo = sb("wo_hi", [P, 8, D], F32R), sb("wo_lo", [P, 8, D], F32R)
        wkv = sb("wkv", [P, DC, D])
        wqs = sb("wqs", [P, DC, D])
        ident = sb("ident", [P, P])
        cos_t, sin_t = sb("cos_t", [P, REMOTE]), sb("sin_t", [P, REMOTE])
        rope = sb("rope", [P, TILES, 2, HALF])
        small = sb("small", [P, 4 * NB + 8 * NB + 2 * NK + RT * NB * 3 + 2 * RT + P])
        o = 0
        def table(*shape):
            nonlocal o
            n = 1
            for s in shape:
                n *= s
            v = small[:, o:o + n]
            o += n
            if len(shape) == 2:
                v = v.rearrange("p (a b) -> p a b", a=shape[0])
            return v
        own_sem = table(4, NB)
        own_geo = table(8, NB)
        own_v = table(2, NK)
        pool_w = table(RT, NB)
        keep = table(RT, NB)
        hide = table(RT, NB)
        spread = table(RT)
        rest_p = table(RT)
        causal = table(P)
        scales = sb("scales", [P, H + DC])
        power = sb("power", [P, 3])
        xt = sb("xt", [P, DC, T])
        xn = sb("xn", [P, 2, D])
        xs_hi, xs_lo = sb("xs_hi", [P, 2, DC, QB], F32R), sb("xs_lo", [P, 2, DC, QB], F32R)
        xpool = sb("xpool", [P, DC, NK])
        krot = sb("krot", [P, LT, HKV, 2 * DS])
        v_hi, v_lo = sb("v_hi", [P, LT, HKV * DV], F32R), sb("v_lo", [P, LT, HKV * DV], F32R)
        kt_hi, kt_lo = sb("kt_hi", [P, 2, 2, KEYS], F32R), sb("kt_lo", [P, 2, 2, KEYS], F32R)
        ks_bd = sb("ks_bd", [P, 4, 4 * NB])
        kg_bd = sb("kg_bd", [P, 4, 8 * NB])
        m_sb = sb("m_sb", [P, DC, H * NB])
        vwo_hi, vwo_lo = sb("vwo_hi", [HK, 2, D], F32R), sb("vwo_lo", [HK, 2, D], F32R)
        union = sb("union", [P, H * KEYS])
        q_rem = union[:, 0:RB * 4 * QB].rearrange("p (n r c) -> p n r c", n=RB, r=2)
        rt1, rt2 = union[:, 3072:3584], union[:, 3584:4096]
        kgr = union[:, 0:768].rearrange("p (t e) -> p t e", t=RT)
        kt1, kt2 = union[:, 768:1152], union[:, 1152:1536]
        kp = union[0:NK, 1536:1536 + D]
        VB = 2 * 4 * QB
        vbd = union[:, VB:VB + 8 * HK]
        probs_l = union[:, :].rearrange("p (h k) -> p h k", h=H)
        sm = sb("sm", [P, 2, H * NB])
        pr = sb("pr", [P, 2, H, NK])
        stat = sb("stat", [P, 2, 4, H])
        pt_hi, pt_lo = sb("pt_hi", [HK, 2, P], F32R), sb("pt_lo", [HK, 2, P], F32R)
        qrot = sb("qrot", [P, 8, 2, DV])
        lt1, lt2 = sb("lt1", [P, H * HALF]), sb("lt2", [P, H * HALF])
        kr = qrot[0:NK, :, :, :].rearrange("p c s e -> p (c s e)")
        kr_by_head = lt1[0:NK, :]
        qo_hi, qo_lo = sb("qo_hi", [P, 8, P], F32R), sb("qo_lo", [P, 8, P], F32R)
        q_hi = [qo_hi[:, :, :], xs_hi[:, 0, :, :].rearrange("p c (u q) -> p (c u) q", q=P)]
        q_lo = [qo_lo[:, :, :], xs_lo[:, 0, :, :].rearrange("p c (u q) -> p (c u) q", q=P)]
        tp_hi, tp_lo = sb("tp_hi", [P, 2, 4 * P], F32R), sb("tp_lo", [P, 2, 4 * P], F32R)
        vb_hi = tp_hi[:, :, :].rearrange("p a b -> p (a b)")[:, 0:8 * HK]
        vb_lo = tp_lo[:, :, :].rearrange("p a b -> p (a b)")[:, 0:8 * HK]
        x1, x1t = sb("x1", [P, 2, D]), sb("x1t", [P, 2, D])
        bn, mv, rstd = sb("bn", [P, 2, 6]), sb("mv", [P, 2, 2]), sb("rstd", [P, 2, 2])

        big = ps("big", [P, 4, 512])
        mid = ps("mid", [P, 2, 512])
        tr = ps("tr", [P, 512])
        acc = ps("acc", [P, 512])

        wq_raw = [union[:, 2 * D * c:2 * D * (c + 1)] for c in range(DC)]
        qr_flat = qrot[:, :, :, :].rearrange("p c s e -> p (c s e)")
        wo_raw = [x1[:, 0, :], x1[:, 1, :], x1t[:, 0, :], x1t[:, 1, :], qr_flat[:, 0:D], qr_flat[:, D:2 * D],
                  m_sb[:, :, :].rearrange("p c n -> p (c n)")[:, 0:D], krot[:, :, :, :].rearrange("p t g e -> p (t g e)")]

        wkv_in, wqs_in, tab_in, ls_in = (sem(n) for n in ("wkv_in", "wqs_in", "tab_in", "ls_in"))
        wq_in, wo_in = [sem(f"wq_in{c}") for c in range(DC)], [sem(f"wo_in{c}") for c in range(8)]
        scale_exp, scale_done, wq_scaled, wqs_scaled, power_set, zeroed = (
            sem(n) for n in ("scale_exp", "scale_done", "wq_scaled", "wqs_scaled", "power_set", "zeroed"))
        wq_hi_s, wq_lo_s, wo_hi_s, wo_lo_s = (sem(n) for n in ("wq_hi_s", "wq_lo_s", "wo_hi_s", "wo_lo_s"))
        dve_past, pe_past = sem("dve_past"), sem("pe_past")
        xt_in = signal("xt_in", 16)
        xn_in = [signal(f"xn_in{i}", 16 * TILES // 2) for i in range(2)]
        xs_hi_s, xs_lo_s = signal("xs_hi_s", RB + 1), signal("xs_lo_s", RB + 1)
        kgeo_ps, kv_ps = signal("kgeo_ps", 1), signal("kv_ps", LT)
        xsum, xpool_s = signal("xsum", 2), signal("xpool_s", 1)
        krope = signal("krope", 12)
        krot_sem, v_hi_s, v_lo_s = signal("krot_sem", 1), signal("v_hi_s", 1), signal("v_lo_s", 1)
        kp_ps, kp_s, kr_s = signal("kp_ps", 1), signal("kp_s", 2), signal("kr_s", 6)
        ktr_ps, klt_ps = signal("ktr_ps", 1), signal("klt_ps", 1)
        kt_hi_s, kt_lo_s = signal("kt_hi_s", 2), signal("kt_lo_s", 2)
        bd_s, vbd_s, vb_hi_s, vb_lo_s = signal("bd_s", 2), signal("vbd_s", 2), signal("vb_hi_s", 1), signal("vb_lo_s", 1)
        m_ps, m_s = signal("m_ps", 1), signal("m_s", 1)
        vwo_ps, vwo_hi_s, vwo_lo_s = signal("vwo_ps", 2), signal("vwo_hi_s", 2), signal("vwo_lo_s", 2)
        qg_ps, qrope = signal("qg_ps", RB), signal("qrope", 6 * RB)
        s_ps, masked, shifted = signal("s_ps", RT), signal("masked", RT + 1), signal("shifted", 2 * RT)
        exp_s, summed, probs_s = signal("exp_s", RT), signal("summed", 3 * RT), signal("probs_s", TILES)
        pt_ps, pt_hi_s, pt_lo_s = signal("pt_ps", TILES), signal("pt_hi_s", TILES), signal("pt_lo_s", TILES)
        out_ps, added, normed = signal("out_ps", TILES), signal("added", TILES), signal("normed", TILES)
        bn_s, var_s, pow_s, rstd_s = signal("bn_s", 2 * TILES), signal("var_s", TILES), signal("pow_s", TILES), signal("rstd_s", 2 * TILES)
        x1t_ps, x1t_s = signal("x1t_ps", TILES), signal("x1t_s", TILES)
        x1_out = [signal(f"x1_out{i}", 16 * TILES // 2) for i in range(2)]
        x1t_out = [signal(f"x1t_out{i}", 16 * TILES // 2) for i in range(2)]
        qp_ps, qsem_s, lrope = signal("qp_ps", 2 * LT), signal("qsem_s", LT), signal("lrope", 6 * LT)
        qt_ps, qt_hi_s, qt_lo_s = signal("qt_ps", LT), signal("qt_hi_s", LT), signal("qt_lo_s", LT)
        ls_ps, lmasked, lmax, lexp = signal("ls_ps", 8 * LT), signal("lmasked", 8 * LT), signal("lmax", 8 * LT), signal("lexp", 8 * LT)
        lrecip, lnorm = signal("lrecip", 8 * LT), signal("lnorm", 8 * LT)
        NPT = [HKV * (tt + 1) for tt in range(LT)]
        tp_ps, tp_hi_s, tp_lo_s = signal("tp_ps", sum(NPT)), signal("tp_hi_s", sum(NPT)), signal("tp_lo_s", sum(NPT))
        pv_ps, o_hi_s, o_lo_s = signal("pv_ps", sum(NPT)), signal("o_hi_s", HKV * LT), signal("o_lo_s", HKV * LT)

        def prime(eng, *signals):
            for s in signals:
                eng.sem_inc(s.sem, s.per)

        def flat(t):
            return t[:, :, :].rearrange("p a b -> p (a b)")

        qf = flat(big)

        def own_columns(a, s):
            n = HK + NK
            j, r = divmod(4 * a * HK + 4 * s * NK, n)
            return union[:, VB:VB + 8 * n].rearrange("p (j n) -> p j n", n=n)[:, j:j + 4, r:r + NK]

        block = ctx.enter_context(nc.Block())

        @block.sync
        def _(sp):
            prime(sp, xt_in, *xn_in, *x1_out, *x1t_out)
            sp.dma_start(xt[:, :, :], io["xt"][0]).then_inc(xt_in.sem, 16)
            for c in range(8):
                sp.dma_start(wo_raw[c], io["wo"][:, c, :]).then_inc(wo_in[c], 16)
            for t, n in ((ident, "ident"), (cos_t, "cos_t"), (sin_t, "sin_t"), (rope, "rope"), (small, "small")):
                sp.dma_start(t[:], io[n]).then_inc(tab_in, 16)

            def tiles(b, fetch):
                def load(t):
                    sp.wait_ge(*(added.now(b, t - 1) if t >= 2 else added.last(b, TILES - 1 + t)))
                    sp.dma_start(xn[:, t % 2, :], io["x"][b, t]).then_inc(xn_in[t % 2].sem, 16)

                def store_transposed(t):
                    sp.wait_ge(*x1t_s.now(b, t + 1))
                    sp.dma_start(x1t_dram[b, t], x1t[:, t % 2, :]).then_inc(x1t_out[t % 2].sem, 16)

                load(0)
                load(1)
                for t in range(TILES):
                    sp.wait_ge(*normed.now(b, t + 1))
                    sp.dma_start(x1_dram[b, t], x1[:, t % 2, :]).then_inc(x1_out[t % 2].sem, 16)
                    if t + 2 < TILES:
                        load(t + 2)
                    if fetch and t == RT - 1:
                        sp.wait_ge(*xs_hi_s.now(b, RB + 1))
                        sp.wait_ge(*xs_lo_s.now(b, RB + 1))
                        sp.wait_ge(*s_ps.now(b, RT))
                        sp.dma_start(xt[:, :, :], io["xt"][b + 1]).then_inc(xt_in.sem, 16)
                    if t:
                        store_transposed(t - 1)
                store_transposed(TILES - 1)

            with sp.Fori(0, B - 1) as b:
                tiles(b, True)
            tiles(B - 1, False)
            for s in (*x1_out, *x1t_out):
                sp.wait_ge(*s.now(B - 1, 16 * TILES // 2))

        @block.gpsimd
        def _(pool):
            prime(pool, var_s, pow_s, rstd_s, lnorm, xs_lo_s)
            pool.dma_start(scales[:, :], io["logit_scale"]).then_inc(ls_in, 16)
            pool.dma_start(wkv[:, :, :], io["wkv"]).then_inc(wkv_in, 16)
            pool.dma_start(wqs[:, :, :], io["wqs"]).then_inc(wqs_in, 16)
            for i, v in enumerate((-0.5, EPS, -1.0)):
                pool.memset(power[:, i:i + 1], v).then_inc(power_set, 1)
            for c in range(8):
                pool.wait_ge(wo_hi_s, c + 1)
                pool.tensor_tensor(wo_lo[:, c, :], wo_raw[c], wo_hi[:, c, :].bitcast(F32), ALU.subtract).then_inc(wo_lo_s, 1)
            pool.wait_ge(power_set, 3)

            def inverse_deviation(b, t):
                pool.wait_ge(*bn_s.now(b, 2 * t + 2))
                pool.wait_ge(*(normed.now(b, t - 1) if t >= 2 else normed.last(b, TILES - 1 + t)))
                r, m = rstd[:, t % 2, 0:1], rstd[:, t % 2, 1:2]
                pool.tensor_tensor(r, mv[:, t % 2, 1:2], power[:, 1:2], ALU.add).then_inc(var_s.sem, 1)
                pool.wait_ge(*var_s.now(b, t + 1))
                pool.tensor_tensor(r, r, power[:, 0:1], ALU.pow).then_inc(pow_s.sem, 1)
                pool.tensor_tensor(m, mv[:, t % 2, 0:1], power[:, 2:3], ALU.mult).then_inc(rstd_s.sem, 1)
                pool.wait_ge(*pow_s.now(b, t + 1))
                pool.wait_ge(*rstd_s.now(b, 2 * t + 1))
                pool.tensor_tensor(m, m, r, ALU.mult).then_inc(rstd_s.sem, 1)

            def split_x(b, n):
                pool.wait_ge(*xs_hi_s.now(b, n + 1))
                pool.tensor_tensor(xs_lo[:, n % 2, :, :], xt[:, :, n * QB:(n + 1) * QB],
                                   xs_hi[:, n % 2, :, :].bitcast(F32), ALU.subtract).then_inc(xs_lo_s.sem, 1)

            def normalise(b, tt, p):
                keys = NB + P * (tt + 1)
                pool.wait_ge(*lrecip.now(b, 8 * tt + p + 1))
                v = probs_l[:, 2 * p:2 * p + 2, 0:keys]
                pool.tensor_tensor(v, v, bc(stat[:, tt, 3, 2 * p:2 * p + 2], 2, keys), ALU.mult).then_inc(lnorm.sem, 1)

            with pool.Fori(0, B) as b:
                split_x(b, 0)
                split_x(b, 1)
                split_x(b, 2)
                split_x(b, 3)
                for t in range(RT):
                    inverse_deviation(b, t)
                for tt in range(LT):
                    for p in range(8):
                        normalise(b, tt, p)
                        if tt and p == 5:
                            inverse_deviation(b, TILES - 2)
                inverse_deviation(b, TILES - 1)

        @block.scalar
        def _(act):
            prime(act, xs_hi_s, krot_sem, v_hi_s, kp_s, kt_hi_s, vb_hi_s, m_s, vwo_hi_s, exp_s, pt_hi_s, x1t_s,
                  qsem_s, qt_hi_s, lexp, tp_hi_s, o_hi_s, normed)
            for c in range(DC):
                act.dma_start(wq_raw[c], io["wq"][:, c, :]).then_inc(wq_in[c], 16)
            act.wait_ge(ls_in, 16)
            act.activation(scales[:, :], scales[:, :], ACT.Exp).then_inc(scale_exp, 1)

            def round_wo(c):
                act.wait_ge(wo_in[c], 16)
                act.activation(wo_hi[:, c, :], wo_raw[c], ACT.Copy).then_inc(wo_hi_s, 1)

            for c in range(DC):
                round_wo(c)
                act.wait_ge(wq_scaled, 3 * c + 3)
                act.activation(wq_hi[:, c, :], wq_raw[c], ACT.Copy).then_inc(wq_hi_s, 1)
            for c in range(DC, 8):
                round_wo(c)

            def split_x(b, n):
                act.wait_ge(*xt_in.now(b, 16))
                if n < 2:
                    act.wait_ge(*(ls_ps.last(b, 8 * LT) if n == 0 else qp_ps.last(b, 2 * LT)))
                else:
                    act.wait_ge(*qg_ps.now(b, n - 1))
                act.activation(xs_hi[:, n % 2, :, :], xt[:, :, n * QB:(n + 1) * QB], ACT.Copy).then_inc(xs_hi_s.sem, 1)

            def pooled_hi(b, t):
                act.wait_ge(*pt_ps.now(b, t + 1))
                act.wait_ge(*(out_ps.now(b, t) if t else out_ps.last(b, TILES)))
                act.activation(pt_hi[:, :, :], mid[0:HK, 1, 0:2 * P].rearrange("p (a q) -> p a q", a=2), ACT.Copy).then_inc(pt_hi_s.sem, 1)

            def scale_x1(b, t):
                act.wait_ge(*rstd_s.now(b, 2 * t + 2))
                act.activation(x1[:, t % 2, :], x1[:, t % 2, :], ACT.Identity, bias=rstd[:, t % 2, 1:2],
                               scale=rstd[:, t % 2, 0:1]).then_inc(normed.sem, 1)

            def x1t_copy(b, t):
                act.wait_ge(*x1t_ps.now(b, t + 1))
                act.wait_ge(*(x1t_out[t % 2].now(b, 16 * (t // 2)) if t >= 2 else x1t_out[t % 2].last(b, 16 * (TILES // 2))))
                act.activation(x1t[:, t % 2, :], (tr if t < RT else acc)[:, :], ACT.Copy).then_inc(x1t_s.sem, 1)

            def plain_queries(b, tt):
                act.wait_ge(*qp_ps.now(b, 2 * tt + 1))
                act.wait_ge(*(qt_ps.now(b, tt) if tt else ktr_ps.now(b, 1)))
                for a in range(2):
                    i = act.activation(qrot[:, 4 * a:4 * a + 4, :, 0:DS].rearrange("p j s e -> p s j e"),
                                       big[:, 2, 256 * a:256 * a + 256].rearrange("p (s j e) -> p s j e", s=2, j=4), ACT.Copy)
                i.then_inc(qsem_s.sem, 1)

            def transposed_queries(b, tt):
                act.wait_ge(*qt_ps.now(b, tt + 1))
                act.wait_ge(*out_ps.last(b, TILES))
                act.activation(q_hi[tt], flat(big[:, 0:2, :]).rearrange("p (c q) -> p c q", q=P), ACT.Copy).then_inc(qt_hi_s.sem, 1)

            with act.Fori(0, B) as b:
                split_x(b, 0)
                split_x(b, 1)
                act.wait_ge(*kv_ps.now(b, 2))
                act.wait_ge(*klt_ps.last(b, 1))
                act.wait_ge(*pv_ps.last(b, sum(NPT)))
                act.wait_ge(wo_lo_s, 8)
                act.activation(krot[:, :, :, 0:DS], big[:, 2:4, 128:256].rearrange("p t (g e) -> p t g e", g=HKV), ACT.Copy).then_inc(krot_sem.sem, 1)
                act.activation(v_hi[:, :, :], big[:, 2:4, 256:512], ACT.Copy).then_inc(v_hi_s.sem, 1)
                act.wait_ge(*kp_ps.now(b, 1))
                act.wait_ge(*ktr_ps.last(b, 1))
                act.activation(kp[:, 128:512], acc[0:NK, 128:512], ACT.Copy).then_inc(kp_s.sem, 1)
                act.activation(kp[0:NB, 0:128], acc[0:NB, 0:128], ACT.Copy).then_inc(kp_s.sem, 1)
                act.wait_ge(*klt_ps.now(b, 1))
                act.wait_ge(*ls_ps.last(b, 8 * LT))
                for s in range(2):
                    r = slice(64 * s, 64 * s + 64)
                    i = act.activation(kt_hi[r, :, s, NB:KEYS], mid[r, 1, :].rearrange("p (a k) -> p a k", a=2), ACT.Copy)
                i.then_inc(kt_hi_s.sem, 1)
                act.wait_ge(*ktr_ps.now(b, 1))
                for s in range(2):
                    r = slice(64 * s, 64 * s + 64)
                    i = act.activation(kt_hi[r, :, s, 0:NB], tr[r, 160:192].rearrange("p (a k) -> p a k", a=2)[:, :, 0:NB], ACT.Copy)
                i.then_inc(kt_hi_s.sem, 1)
                split_x(b, 2)
                act.wait_ge(*vbd_s.now(b, 2))
                act.activation(vb_hi, vbd, ACT.Copy).then_inc(vb_hi_s.sem, 1)
                act.wait_ge(*m_ps.now(b, 1))
                act.activation(m_sb[:, :, :].rearrange("p (u v) n -> p u (v n)", u=2), mid[:, :, 0:2 * H * NB], ACT.Copy).then_inc(m_s.sem, 1)
                for a in range(2):
                    act.wait_ge(*vwo_ps.now(b, a + 1))
                    act.activation(vwo_hi[:, a, :], (acc, tr)[a][0:HK, :], ACT.Copy).then_inc(vwo_hi_s.sem, 1)
                split_x(b, 3)
                for t in range(RT + 3):
                    if t >= 3:
                        scale_x1(b, t - 3)
                    if t < RT:
                        act.wait_ge(*shifted.now(b, 2 * t + 2))
                        act.activation(pr[:, t % 2, :, 0:NB], sm[:, t % 2, :].rearrange("p (h k) -> p h k", h=H), ACT.Exp).then_inc(exp_s.sem, 1)
                    if 1 <= t <= RT:
                        pooled_hi(b, t - 1)
                    if t == 3 or t == 6:
                        plain_queries(b, t // 3 - 1)
                    if t == 6 or t == 8:
                        transposed_queries(b, t // 2 - 3)
                    if t >= 3:
                        x1t_copy(b, t - 3)
                n0 = 0
                for tt in range(LT):
                    t = RT + tt
                    keys = NB + P * (tt + 1)
                    for g in range(HKV + 2):
                        if g >= 2:
                            for k in range(tt + 1):
                                n = (g - 2) * (tt + 1) + k
                                act.wait_ge(*tp_ps.now(b, n0 + n + 1))
                                act.wait_ge(*(pv_ps.now(b, n0 + n - 1) if tt or n >= 2 else vwo_ps.now(b, 2)))
                                act.activation(tp_hi[:, n % 2, :], mid[:, n % 2, :], ACT.Copy).then_inc(tp_hi_s.sem, 1)
                        if g < HKV:
                            for p in (2 * g, 2 * g + 1):
                                act.wait_ge(*lmax.now(b, 8 * tt + p + 1))
                                for h in (2 * p, 2 * p + 1):
                                    i = act.activation(probs_l[:, h, 0:keys], big[:, 2 * ((p + 1) % 2) + h % 2, 0:keys], ACT.Exp,
                                                       bias=stat[:, tt, 0, h:h + 1], accum_out=stat[:, tt, 1, h:h + 1])
                                i.then_inc(lexp.sem, 1)
                        if g >= 2:
                            act.wait_ge(*pv_ps.now(b, n0 + n + 1))
                            if tt == 1:
                                act.wait_ge(*out_ps.now(b, t))
                            r, c = slice(64 * (g % 2), 64 * (g % 2) + 64), 4 * ((g - 2) // 2)
                            act.activation(qo_hi[r, c:c + 4, :].rearrange("p j q -> p (j q)"), tr[r, :], ACT.Copy).then_inc(o_hi_s.sem, 1)
                        if tt == 1 and g == 3:
                            scale_x1(b, t - 1)
                        if tt == 1 and g == 4:
                            x1t_copy(b, t - 1)
                    pooled_hi(b, t)
                    n0 += NPT[tt]
                scale_x1(b, TILES - 1)
                x1t_copy(b, TILES - 1)

        @block.vector
        def _(dve):
            prime(dve, xsum, xpool_s, krope, v_lo_s, kr_s, kt_lo_s, bd_s, vbd_s, vb_lo_s, vwo_lo_s, qrope,
                  masked, shifted, summed, probs_s, pt_lo_s, added, bn_s, lrope, qt_lo_s, lmasked, lmax,
                  lrecip, tp_lo_s, o_lo_s)
            dve.wait_ge(scale_exp, 1)
            dve.tensor_scalar(scales[:, :], scales[:, :], float(DS) ** -0.5, None, ALU.mult).then_inc(scale_done, 1)
            dve.wait_ge(scale_done, 1)
            dve.memset(pr[:, :, :, :], 0.0)
            for k in (kt_hi, kt_lo):
                for s in range(2):
                    i = dve.memset(k[64 * (1 - s):64 * (1 - s) + 64, :, s, :].bitcast(F32), 0.0)
            i.then_inc(zeroed, 1)

            def lower_wq(c):
                dve.wait_ge(wq_hi_s, c + 1)
                dve.tensor_tensor(wq_lo[:, c, :], wq_raw[c], wq_hi[:, c, :].bitcast(F32), ALU.subtract).then_inc(wq_lo_s, 1)

            for c in range(DC):
                dve.wait_ge(wq_in[c], 16)
                for c0, c1, w in ((0, 512, DS), (512, 768, HALF), (768, 1024, HALF)):
                    v = wq_raw[c][:, c0:c1].rearrange("p (h e) -> p h e", h=H)
                    dve.tensor_tensor(v, v, bc(scales[:, 0:H], 2, w), ALU.mult).then_inc(wq_scaled, 1)
                if c:
                    lower_wq(c - 1)
            lower_wq(DC - 1)
            dve.wait_ge(wqs_in, 16)
            for c in range(DC):
                dve.tensor_scalar(wqs[:, c, :], wqs[:, c, :], scales[:, H + c:H + c + 1], None, ALU.mult).then_inc(wqs_scaled, 1)
            dve.wait_ge(zeroed, 1)
            dve.wait_ge(tab_in, 16 * 5)

            def pooled_lo(b, t):
                dve.wait_ge(*pt_hi_s.now(b, t + 1))
                dve.tensor_tensor(pt_lo[:, :, :], mid[0:HK, 1, 0:2 * P].rearrange("p (a q) -> p a q", a=2),
                                  pt_hi[:, :, :].bitcast(F32), ALU.subtract).then_inc(pt_lo_s.sem, 1)

            def rotate(b, sig, k, in1, in2, cos, sin, out1, out2, u, v):
                dve.tensor_tensor(u, in1, cos, ALU.mult).then_inc(sig.sem, 1)
                dve.tensor_tensor(v, in2, sin, ALU.mult).then_inc(sig.sem, 1)
                dve.wait_ge(*sig.now(b, k + 2))
                dve.tensor_tensor(out1, u, v, ALU.subtract).then_inc(sig.sem, 1)
                dve.wait_ge(*sig.now(b, k + 3))
                dve.tensor_tensor(u, in2, cos, ALU.mult).then_inc(sig.sem, 1)
                dve.tensor_tensor(v, in1, sin, ALU.mult).then_inc(sig.sem, 1)
                dve.wait_ge(*sig.now(b, k + 5))
                dve.tensor_tensor(out2, u, v, ALU.add).then_inc(sig.sem, 1)

            def residual(b, t):
                dve.wait_ge(*out_ps.now(b, t + 1))
                dve.wait_ge(*xn_in[t % 2].now(b, 16 * (t // 2 + 1)))
                dve.wait_ge(*(x1_out[t % 2].now(b, 16 * (t // 2)) if t >= 2 else x1_out[t % 2].last(b, 16 * (TILES // 2))))
                dve.wait_ge(*(x1t_ps.now(b, t - 1) if t >= 2 else x1t_ps.last(b, TILES - 1 + t)))
                dve.tensor_tensor(x1[:, t % 2, :], acc[:, :], xn[:, t % 2, :], ALU.add).then_inc(added.sem, 1)
                dve.wait_ge(*added.now(b, t + 1))
                dve.bn_stats(bn[:, t % 2, :], x1[:, t % 2, :]).then_inc(bn_s.sem, 1)
                dve.wait_ge(*bn_s.now(b, 2 * t + 1))
                dve.sem_inc(dve_past, 1)
                dve.bn_aggr(mv[:, t % 2, :], bn[:, t % 2, :]).then_inc(bn_s.sem, 1)

            with dve.Fori(0, B) as b:
                dve.wait_ge(*xt_in.now(b, 16))
                dve.wait_ge(*kp_ps.last(b, 1))
                for c, (c0, c1, n) in enumerate(((0, REMOTE, NB), (REMOTE, T, 1))):
                    dve.tensor_reduce(xpool[:, :, NB * c:NB * c + n], xt[:, :, c0:c1].rearrange("p c (n m) -> p c n m", n=n),
                                      AX.X, ALU.add).then_inc(xsum.sem, 1)
                dve.wait_ge(*xsum.now(b, 2))
                dve.tensor_scalar(xpool[:, :, 0:NB], xpool[:, :, 0:NB], 1.0 / MB, None, ALU.mult).then_inc(xpool_s.sem, 1)
                dve.wait_ge(*kgeo_ps.now(b, 1))
                r6 = lambda c: qf[:, 0:RT * P].rearrange("p (t e) -> p t e", t=RT)[:, :, c:c + 64].rearrange("p t (g f) -> p t g f", g=HKV)
                o6 = lambda c: kgr[:, :, c:c + 64].rearrange("p t (g f) -> p t g f", g=HKV)
                u6 = lambda t: t[:, 0:RT * 64].rearrange("p (t g f) -> p t g f", t=RT, g=HKV)
                rotate(b, krope, 0, r6(0), r6(64), bc(rope[:, 0:RT, 0, :], 2, HKV), bc(rope[:, 0:RT, 1, :], 2, HKV),
                       o6(0), o6(64), u6(kt1), u6(kt2))
                dve.wait_ge(*v_hi_s.now(b, 1))
                dve.wait_ge(*krope.now(b, 6))
                r2 = lambda c: big[:, 2:4, c:c + 64].rearrange("p t (g f) -> p t g f", g=HKV)
                u2 = lambda t: t[:, 0:LT * 64].rearrange("p (t g f) -> p t g f", t=LT, g=HKV)
                rotate(b, krope, 6, r2(0), r2(64), bc(rope[:, RT:TILES, 0, :], 2, HKV), bc(rope[:, RT:TILES, 1, :], 2, HKV),
                       krot[:, :, :, DS:DS + HALF], krot[:, :, :, DS + HALF:DS + DG], u2(kt1), u2(kt2))
                dve.tensor_tensor(v_lo[:, :, :], big[:, 2:4, 256:512], v_hi[:, :, :].bitcast(F32), ALU.subtract).then_inc(v_lo_s.sem, 1)
                dve.wait_ge(wo_lo_s, 8)
                dve.wait_ge(*kp_s.now(b, 2))
                for c in range(2):
                    dve.tensor_copy(kr[0:NB, 256 * c:256 * c + 256].rearrange("k (g r f) -> k g r f", g=HKV, r=REP),
                                    bc(kp[0:NB, 64 * c:64 * c + 64].rearrange("k (g f) -> k g f", g=HKV), 2, REP)).then_inc(kr_s.sem, 1)
                dve.tensor_copy(kr[0:NB, 512:1024].rearrange("k (g r f) -> k g r f", g=HKV, r=REP),
                                bc(kp[0:NB, 128:256].rearrange("k (g f) -> k g f", g=HKV), 2, REP)).then_inc(kr_s.sem, 1)
                by_head = kr_by_head[0:NB, :].rearrange("k (g e) -> k g e", g=HKV)
                for e0, w, c0 in ((0, DS, 128), (DS, HALF, 0), (DS + HALF, HALF, 64)):
                    dve.tensor_copy(by_head[:, :, e0:e0 + w], kp[0:NB, c0:c0 + HKV * w].rearrange("k (g f) -> k g f", g=HKV)).then_inc(kr_s.sem, 1)
                dve.memset(vbd, 0.0).then_inc(zeroed, 1)
                dve.wait_ge(*kt_hi_s.now(b, 1))
                for s in range(2):
                    r = slice(64 * s, 64 * s + 64)
                    i = dve.tensor_tensor(kt_lo[r, :, s, NB:KEYS], mid[r, 1, :].rearrange("p (a k) -> p a k", a=2),
                                          kt_hi[r, :, s, NB:KEYS].bitcast(F32), ALU.subtract)
                i.then_inc(kt_lo_s.sem, 1)

                def rotate_queries(n):
                    dve.wait_ge(*qg_ps.now(b, n + 1))
                    if n:
                        dve.wait_ge(*qrope.now(b, 6 * n))
                    if n == 2:
                        dve.wait_ge(*vb_lo_s.now(b, 1))
                    f = lambda v: v.rearrange("p (a q) -> p a q", a=2)
                    rotate(b, qrope, 6 * n, f(big[:, 2 * (n % 2), :]), f(big[:, 2 * (n % 2) + 1, :]),
                           bc(cos_t[:, n * QB:(n + 1) * QB], 1, 2), bc(sin_t[:, n * QB:(n + 1) * QB], 1, 2),
                           f(q_rem[:, n, 0, :]), f(q_rem[:, n, 1, :]), f(rt1), f(rt2))

                rotate_queries(0)
                dve.wait_ge(*kt_hi_s.now(b, 2))
                slots = tr[:, 0:192].rearrange("p (s k) -> p s k", k=16)
                dve.tensor_tensor(kg_bd[:, :, :].rearrange("p c (h k) -> p c h k", h=8), bc(slots[:, 0:4, 0:NB], 2, 8),
                                  bc(own_geo, 1, 4), ALU.mult).then_inc(bd_s.sem, 1)
                dve.tensor_tensor(ks_bd[:, :, :].rearrange("p c (h k) -> p c h k", h=4), bc(slots[:, 4:8, 0:NB], 2, 4),
                                  bc(own_sem, 1, 4), ALU.mult).then_inc(bd_s.sem, 1)
                dve.wait_ge(zeroed, b + 2)
                for a in range(2):
                    for s in range(2):
                        i = dve.tensor_tensor(own_columns(a, s), bc(slots[:, 8 + a, 0:NK], 1, 4), bc(own_v[:, s, :], 1, 4), ALU.mult)
                    i.then_inc(vbd_s.sem, 1)
                for s in range(2):
                    r = slice(64 * s, 64 * s + 64)
                    i = dve.tensor_tensor(kt_lo[r, :, s, 0:NB], tr[r, 160:192].rearrange("p (a k) -> p a k", a=2)[:, :, 0:NB],
                                          kt_hi[r, :, s, 0:NB].bitcast(F32), ALU.subtract)
                i.then_inc(kt_lo_s.sem, 1)
                dve.wait_ge(*vb_hi_s.now(b, 1))
                dve.tensor_tensor(vb_lo, vbd, vb_hi.bitcast(F32), ALU.subtract).then_inc(vb_lo_s.sem, 1)
                rotate_queries(1)
                for a in range(2):
                    dve.wait_ge(*vwo_hi_s.now(b, a + 1))
                    dve.tensor_tensor(vwo_lo[:, a, :], (acc, tr)[a][0:HK, :], vwo_hi[:, a, :].bitcast(F32), ALU.subtract).then_inc(vwo_lo_s.sem, 1)

                def softmax_in(t):
                    s3 = sm[:, t % 2, :].rearrange("p (h k) -> p h k", h=H)
                    s_in = mid[:, 0, 0:H * NB].rearrange("p (h k) -> p h k", h=H)
                    dve.wait_ge(*s_ps.now(b, t + 1))
                    dve.wait_ge(*(exp_s.now(b, t - 1) if t >= 2 else exp_s.last(b, RT)))
                    if t == 0:
                        dve.tensor_tensor(s3, s_in, bc(keep[:, t, :], 1, H), ALU.mult).then_inc(masked.sem, 1)
                        dve.wait_ge(*masked.now(b, 1))
                        s_in = s3
                    dve.tensor_tensor(s3, s_in, bc(hide[:, t, :], 1, H), ALU.add).then_inc(masked.sem, 1)
                    dve.wait_ge(*masked.now(b, t + 2))
                    dve.tensor_reduce(stat[:, t % 2, 0, :], s3, AX.X, ALU.max).then_inc(shifted.sem, 1)
                    dve.wait_ge(*shifted.now(b, 2 * t + 1))
                    dve.wait_ge(*(pt_ps.now(b, t - 1) if t >= 2 else pt_ps.last(b, TILES - 1 + t)))
                    dve.tensor_tensor(s3, s3, bc(stat[:, t % 2, 0, :], 2, NB), ALU.subtract).then_inc(shifted.sem, 1)

                def softmax_out(t):
                    p3 = pr[:, t % 2, :, 0:NB]
                    dve.wait_ge(*exp_s.now(b, t + 1))
                    dve.tensor_reduce(stat[:, t % 2, 1, :], p3, AX.X, ALU.add).then_inc(summed.sem, 1)
                    dve.wait_ge(*summed.now(b, 3 * t + 1))
                    dve.tensor_scalar(stat[:, t % 2, 2, :], stat[:, t % 2, 1, :], spread[:, t:t + 1], None, ALU.mult).then_inc(summed.sem, 1)
                    dve.wait_ge(*summed.now(b, 3 * t + 2))
                    dve.reciprocal(stat[:, t % 2, 3, :], stat[:, t % 2, 2, :]).then_inc(summed.sem, 1)
                    dve.wait_ge(*summed.now(b, 3 * t + 3))
                    if t in (0, 2):
                        dve.tensor_copy(pr[:, t % 2, :, NB:NK], bc(rest_p[:, t:t + 1], 1, H))
                    dve.tensor_tensor(p3, p3, bc(stat[:, t % 2, 3, :], 2, NB), ALU.mult).then_inc(probs_s.sem, 1)

                def rotate_local(tt):
                    t = RT + tt
                    dve.wait_ge(*qsem_s.now(b, tt + 1))
                    dve.wait_ge(*qp_ps.now(b, 2 * tt + 2))
                    if tt:
                        dve.wait_ge(*lrope.now(b, 6 * tt))
                    q_out = lambda e0: qrot[:, :, :, e0:e0 + HALF].rearrange("p (a j) s e -> p a s j e", a=2)
                    head = lambda v: v.rearrange("p (h f) -> p h f", h=H)
                    cos, sin = bc(rope[:, t, 0, :], 1, H), bc(rope[:, t, 1, :], 1, H)
                    in1, in2 = head(big[:, 3, 0:256]), head(big[:, 3, 256:512])
                    dve.tensor_tensor(head(lt1[:, :]), in1, cos, ALU.mult).then_inc(lrope.sem, 1)
                    dve.tensor_tensor(head(lt2[:, :]), in2, sin, ALU.mult).then_inc(lrope.sem, 1)
                    dve.wait_ge(*lrope.now(b, 6 * tt + 2))
                    parts = lambda v, a: v[:, 128 * a:128 * a + 128].rearrange("p (s j f) -> p s j f", s=2, j=4)
                    dve.tensor_tensor(q_out(DS)[:, 0], parts(lt1, 0), parts(lt2, 0), ALU.subtract)
                    dve.tensor_tensor(q_out(DS)[:, 1], parts(lt1, 1), parts(lt2, 1), ALU.subtract).then_inc(lrope.sem, 1)
                    dve.wait_ge(*lrope.now(b, 6 * tt + 3))
                    dve.tensor_tensor(head(lt1[:, :]), in2, cos, ALU.mult).then_inc(lrope.sem, 1)
                    dve.tensor_tensor(head(lt2[:, :]), in1, sin, ALU.mult).then_inc(lrope.sem, 1)
                    dve.wait_ge(*lrope.now(b, 6 * tt + 5))
                    dve.tensor_tensor(q_out(DS + HALF)[:, 0], parts(lt1, 0), parts(lt2, 0), ALU.add)
                    dve.tensor_tensor(q_out(DS + HALF)[:, 1], parts(lt1, 1), parts(lt2, 1), ALU.add).then_inc(lrope.sem, 1)

                def transposed_queries(tt):
                    dve.wait_ge(*qt_hi_s.now(b, tt + 1))
                    dve.tensor_tensor(q_lo[tt], flat(big[:, 0:2, :]).rearrange("p (c q) -> p c q", q=P), q_hi[tt].bitcast(F32),
                                      ALU.subtract).then_inc(qt_lo_s.sem, 1)

                for t in range(RT + 3):
                    if t == 1:
                        rotate_queries(2)
                    if t < RT:
                        softmax_in(t)
                    if 1 <= t <= RT:
                        pooled_lo(b, t - 1)
                    if t < RT:
                        softmax_out(t)
                    if 2 <= t < RT + 2:
                        residual(b, t - 2)
                    if t == 4 or t == 7:
                        rotate_local(t // 3 - 1)
                    if t == 6 or t == 8:
                        transposed_queries(t // 2 - 3)
                n0 = 0
                for tt in range(LT):
                    t = RT + tt
                    keys = NB + P * (tt + 1)
                    for g in range(HKV + 2):
                        if g >= 2:
                            for k in range(tt + 1):
                                n = (g - 2) * (tt + 1) + k
                                dve.wait_ge(*tp_hi_s.now(b, n0 + n + 1))
                                dve.tensor_tensor(tp_lo[:, n % 2, :], mid[:, n % 2, :], tp_hi[:, n % 2, :].bitcast(F32), ALU.subtract).then_inc(tp_lo_s.sem, 1)
                        if 1 <= g <= HKV:
                            for p in (2 * g - 2, 2 * g - 1):
                                dve.wait_ge(*lexp.now(b, 8 * tt + p + 1))
                                dve.reciprocal(stat[:, tt, 3, 2 * p:2 * p + 2], stat[:, tt, 1, 2 * p:2 * p + 2]).then_inc(lrecip.sem, 1)
                        if g < HKV:
                            for p in (2 * g, 2 * g + 1):
                                dve.wait_ge(*ls_ps.now(b, 8 * tt + p + 1))
                                m = 2 * ((p + 1) % 2)
                                pair = big[:, m:m + 2, :]
                                dve.tensor_tensor(pair[:, :, keys - P:keys], pair[:, :, keys - P:keys], bc(causal, 1, 2), ALU.add).then_inc(lmasked.sem, 1)
                                dve.wait_ge(*lmasked.now(b, 8 * tt + p + 1))
                                dve.tensor_reduce(stat[:, tt, 0, 2 * p:2 * p + 2], pair[:, :, 0:keys], AX.X, ALU.max, negate=True).then_inc(lmax.sem, 1)
                        if g >= 2:
                            dve.wait_ge(*o_hi_s.now(b, HKV * tt + g - 1))
                            r, c = slice(64 * (g % 2), 64 * (g % 2) + 64), 4 * ((g - 2) // 2)
                            v = lambda q: q[r, c:c + 4, :].rearrange("p j q -> p (j q)")
                            dve.tensor_tensor(v(qo_lo), tr[r, :], v(qo_hi).bitcast(F32), ALU.subtract).then_inc(o_lo_s.sem, 1)
                        if tt == 1 and g == 2:
                            residual(b, t - 1)
                    dve.wait_ge(*lnorm.now(b, 8 * tt + 8))
                    dve.wait_ge(*pt_ps.now(b, t - 1))
                    dve.tensor_copy(pr[:, t % 2, :, 0:NB], probs_l[:, :, 0:NB]).then_inc(probs_s.sem, 1)
                    pooled_lo(b, t)
                    n0 += NPT[tt]
                residual(b, TILES - 1)

        @block.tensor
        def _(pe):
            prime(pe, kgeo_ps, kv_ps, kp_ps, ktr_ps, klt_ps, m_ps, vwo_ps, qg_ps, s_ps, pt_ps, out_ps, x1t_ps, qp_ps,
                  qt_ps, ls_ps, tp_ps, pv_ps)
            pe.wait_ge(wkv_in, 16)

            def transpose_probs(b, t):
                pe.wait_ge(*probs_s.now(b, t + 1))
                if 0 < t < RT:
                    pe.wait_ge(*pt_lo_s.now(b, t))
                p = pr[:, t % 2, :, :].rearrange("p (a h) k -> p a (h k)", a=2)
                for a in range(2):
                    i = pe.transpose(mid[0:HK, 1, P * a:P * a + P], p[:, a, :], ident[:, :])
                i.then_inc(pt_ps.sem, 1)

            def attend_pooled(b, t, last):
                pe.wait_ge(*pt_lo_s.now(b, t + 1))
                pe.wait_ge(*(added.now(b, t) if t else vwo_lo_s.now(b, 2)))
                if t == TILES - 1:
                    pe.wait_ge(*x1t_s.now(b, t))
                for a in range(2):
                    i = three_passes(pe, acc[:, :], pt_hi[:, a, :], pt_lo[:, a, :], vwo_hi[:, a, :], vwo_lo[:, a, :],
                                     a == 0, last and a == 1)
                return i

            def transpose_x1(b, t):
                pe.wait_ge(*normed.now(b, t + 1))
                if t == 0:
                    pe.wait_ge(*vwo_lo_s.now(b, 2))
                elif t < RT:
                    pe.wait_ge(*x1t_s.now(b, t))
                for c in range(DC):
                    i = pe.transpose((tr if t < RT else acc)[:, P * c:P * c + P], x1[:, t % 2, P * c:P * c + P], ident[:, :])
                i.then_inc(x1t_ps.sem, 1)

            def project_local(b, tt, s):
                pe.wait_ge(*xs_lo_s.now(b, RB + 1))
                if s == 0:
                    if tt:
                        pe.wait_ge(*lrope.now(b, 6))
                    else:
                        pe.wait_ge(*qrope.now(b, 12))
                for c in range(DC):
                    k = slice(P * tt, P * tt + P)
                    i = three_passes(pe, big[:, 2 + s, :], xs_hi[:, 1, c, k], xs_lo[:, 1, c, k],
                                     wq_hi[:, c, 512 * s:512 * s + 512], wq_lo[:, c, 512 * s:512 * s + 512], c == 0, c == DC - 1)
                i.then_inc(qp_ps.sem, 1)

            def transpose_queries(b, tt):
                pe.wait_ge(*qsem_s.now(b, tt + 1))
                pe.wait_ge(*lrope.now(b, 6 * tt + 6))
                pe.wait_ge(*(qt_lo_s.now(b, tt) if tt else qrope.now(b, 6 * RB)))
                for c in range(8):
                    i = pe.transpose(big[:, c // 4, P * (c % 4):P * (c % 4) + P], qrot[:, c, :, :].rearrange("p s e -> p (s e)"), ident[:, :])
                i.then_inc(qt_ps.sem, 1)

            def output(b, t):
                attend_pooled(b, t, False)
                pe.wait_ge(*o_lo_s.now(b, HKV * (t - RT + 1)))
                for c in range(8):
                    i = three_passes(pe, acc[:, :], qo_hi[:, c, :], qo_lo[:, c, :], wo_hi[:, c, :], wo_lo[:, c, :], False, c == 7)
                i.then_inc(out_ps.sem, 1)

            with pe.Fori(0, B) as b:
                pe.wait_ge(*xt_in.now(b, 16))
                pe.wait_ge(*lexp.last(b, 8 * LT))
                for t in range(RT):
                    for c in range(DC):
                        i = pe.matmul(qf[:, P * t:P * t + P], xt[:, c, P * t:P * t + P], wkv[:, c, 0:128],
                                      start=(c == 0), stop=(c == DC - 1))
                i.then_inc(kgeo_ps.sem, 1)
                for t in range(LT):
                    for c in range(DC):
                        i = pe.matmul(big[:, 2 + t, :], xt[:, c, REMOTE + P * t:REMOTE + P * t + P], wkv[:, c, :],
                                      start=(c == 0), stop=(c == DC - 1))
                    i.then_inc(kv_ps.sem, 1)
                pe.wait_ge(tab_in, 16 * 5)
                pe.wait_ge(*xpool_s.now(b, 1))
                pe.wait_ge(*x1t_s.last(b, TILES))
                for c in range(DC):
                    pe.matmul(acc[0:NK, 128:512], xpool[:, c, :], wkv[:, c, 128:512], start=(c == 0), stop=(c == DC - 1))
                pe.wait_ge(*krope.now(b, 6))
                for t in range(RT):
                    i = pe.matmul(acc[0:NB, 0:128], pool_w[:, t, :], kgr[:, t, :], start=(t == 0), stop=(t == RT - 1))
                i.then_inc(kp_ps.sem, 1)

                def project_geo(n):
                    pe.wait_ge(wq_lo_s, DC)
                    pe.wait_ge(*xs_lo_s.now(b, n + 1))
                    if n == 1:
                        pe.wait_ge(*v_lo_s.now(b, 1))
                    elif n == 2:
                        pe.wait_ge(*qrope.now(b, 6))
                    for r in range(2):
                        for a in range(2):
                            for c in range(DC):
                                w = slice(512 + 256 * r + 128 * a, 512 + 256 * r + 128 * a + 128)
                                i = three_passes(pe, big[:, 2 * (n % 2) + r, QB * a:QB * a + QB], wq_hi[:, c, w], wq_lo[:, c, w],
                                                 xs_hi[:, n % 2, c, :], xs_lo[:, n % 2, c, :], c == 0, c == DC - 1)
                    i.then_inc(qg_ps.sem, 1)

                project_geo(0)
                pe.wait_ge(*krot_sem.now(b, 1))
                pe.wait_ge(*krope.now(b, 12))
                pe.wait_ge(*pt_lo_s.last(b, TILES))
                for a in range(2):
                    for t in range(LT):
                        i = pe.transpose(mid[:, 1, 256 * a + P * t:256 * a + P * t + P],
                                         krot[:, t, 2 * a:2 * a + 2, :].rearrange("p g e -> p (g e)"), ident[:, :])
                i.then_inc(klt_ps.sem, 1)
                pe.wait_ge(*kr_s.now(b, 6))
                pe.wait_ge(*o_lo_s.last(b, HKV * LT))
                pe.sem_inc(pe_past, 1)
                for s in range(8):
                    pe.transpose(tr[:, 16 * s:16 * s + NB], kr[0:NB, P * s:P * s + P], ident[0:NB, 0:NB])
                for a in range(2):
                    pe.transpose(tr[:, 16 * (8 + a):16 * (8 + a) + NK], kp[:, 256 + P * a:256 + P * a + P], ident[0:NK, 0:NK])
                for a in range(2):
                    i = pe.transpose(tr[:, 16 * (10 + a):16 * (10 + a) + NB], kr_by_head[0:NB, P * a:P * a + P], ident[0:NB, 0:NB])
                i.then_inc(ktr_ps.sem, 1)
                project_geo(1)
                pe.wait_ge(wqs_scaled, DC)
                pe.wait_ge(*bd_s.now(b, 2))
                pe.wait_ge(*kt_lo_s.now(b, 1))
                for c in range(DC):
                    for g in range(HKV):
                        i = pe.matmul(mid[:, c // 2, H * NB * (c % 2) + 4 * NB * g:H * NB * (c % 2) + 4 * NB * (g + 1)],
                                      wqs[:, g, P * c:P * c + P], ks_bd[:, g, :], start=True, stop=True)
                i.then_inc(m_ps.sem, 1)
                pe.wait_ge(wo_lo_s, 8)
                pe.wait_ge(*vb_lo_s.now(b, 1))
                pe.wait_ge(*kt_lo_s.now(b, 2))
                for a in range(2):
                    for j in range(4):
                        o = (4 * a + j) * HK
                        i = three_passes(pe, (acc, tr)[a][0:HK, :], vb_hi[:, o:o + HK], vb_lo[:, o:o + HK],
                                         wo_hi[:, 4 * a + j, :], wo_lo[:, 4 * a + j, :], j == 0, j == 3)
                    i.then_inc(vwo_ps.sem, 1)

                def scores(t):
                    pe.wait_ge(*qrope.now(b, 6 * (t // 2 + 1)))
                    if t == 0:
                        pe.wait_ge(*m_s.now(b, 1))
                    else:
                        pe.wait_ge(*masked.now(b, t + 1))
                    plain = lambda c: pe.matmul(mid[:, 0, 0:H * NB], xt[:, c, P * t:P * t + P], m_sb[:, c, :],
                                                start=(c == 0), stop=(c == DC - 1))
                    for c in range(DC - 1):
                        plain(c)
                    for a in range(2):
                        for r in range(2):
                            q = q_rem[:, t // 2, r, QB * a + P * (t % 2):QB * a + P * (t % 2) + P]
                            pe.matmul(mid[:, 0, HB * a:HB * a + HB], q, kg_bd[:, 2 * r + a, :],
                                      start=False, stop=False, skip_group_check=True)
                    plain(DC - 1).then_inc(s_ps.sem, 1)

                for t in range(RT + 3):
                    if t < RT:
                        scores(t)
                    if t == 0:
                        project_geo(2)
                    if 1 <= t <= RT:
                        transpose_probs(b, t - 1)
                    if t in (2, 3):
                        project_local(b, 0, t - 2)
                    if t in (5, 6):
                        project_local(b, 1, t - 5)
                    if 2 <= t < RT + 2:
                        attend_pooled(b, t - 2, True).then_inc(out_ps.sem, 1)
                    if t == 5 or t == 8:
                        transpose_queries(b, t // 3 - 1)
                    if t >= 3:
                        transpose_x1(b, t - 3)
                n0 = 0
                for tt in range(LT):
                    t = RT + tt
                    keys = NB + P * (tt + 1)
                    for g in range(HKV + 2):
                        if g >= 2:
                            pe.wait_ge(*lnorm.now(b, 8 * tt + 2 * (g - 2) + 2))
                            for k in range(tt + 1):
                                n = (g - 2) * (tt + 1) + k
                                if n >= 2:
                                    pe.wait_ge(*tp_lo_s.now(b, n0 + n - 1))
                                else:
                                    pe.wait_ge(*pt_lo_s.now(b, t))
                                for j in range(4):
                                    h = 4 * (g - 2) + j
                                    i = pe.transpose(mid[:, n % 2, P * j:P * j + P], probs_l[:, h, NB + P * k:NB + P * k + P], ident[:, :])
                                i.then_inc(tp_ps.sem, 1)
                        if g < HKV:
                            pe.wait_ge(*qt_lo_s.now(b, LT))
                            for p in (2 * g, 2 * g + 1):
                                if tt or p >= 2:
                                    pe.wait_ge(*lexp.now(b, 8 * tt + p - 1))
                                for h in (2 * p, 2 * p + 1):
                                    a, s, j = h // 8, h // 4 % 2, h % 4
                                    i = three_passes(pe, big[:, 2 * ((p + 1) % 2) + h % 2, 0:keys], q_hi[tt][:, 4 * a + j, :], q_lo[tt][:, 4 * a + j, :],
                                                     kt_hi[:, a, s, 0:keys], kt_lo[:, a, s, 0:keys], True, True)
                                i.then_inc(ls_ps.sem, 1)
                        if g >= 2:
                            if tt or g > 2:
                                pe.wait_ge(*o_lo_s.now(b, HKV * tt + g - 2))
                            else:
                                pe.wait_ge(*x1t_s.now(b, RT))
                            for k in range(tt + 1):
                                n = (g - 2) * (tt + 1) + k
                                pe.wait_ge(*tp_lo_s.now(b, n0 + n + 1))
                                w = slice(P * ((g - 2) // 2), P * ((g - 2) // 2) + P)
                                three_passes(pe, tr[:, :], v_hi[:, k, w], v_lo[:, k, w], tp_hi[:, n % 2, :], tp_lo[:, n % 2, :],
                                             k == 0, k == tt).then_inc(pv_ps.sem, 1)
                        if tt == 1 and g == 1:
                            output(b, t - 1)
                        if tt == 1 and g == 4:
                            transpose_x1(b, t - 1)
                    n0 += NPT[tt]
                    transpose_probs(b, t)
                output(b, TILES - 1)
                transpose_x1(b, TILES - 1)


def weights_block(nc, sems, io, x1t_dram, ctx):
    keep, _, _, _ = tools(nc, ctx, sems, "w")
    wg, wu, wd = keep("wg", [P, DC, INTER]), keep("wu", [P, DC, INTER]), keep("wd", [P, IC, D])
    ug_scale = keep("ug_scale", [P, 2, IC])
    xraw = keep("xraw", [P, FT, DC, P])
    inner = ExitStack()
    with inner:
        sb, ps, _, sem = tools(nc, inner, sems, "wp")
        had = sb("had", [P, 2, P])
        hr = sb("hr", [P, 2, P], F32R)
        su = sb("su", [P, DC])
        sd = sb("sd", [P, IC])
        dps = sb("dps", [P, D])
        stage, mixed = sb("stage", [P, 2, 4, 512]), sb("mixed", [P, 2, 4, 512])
        dn = sb("dn", [P, IC, D])
        hi, lo = sb("hi", [P, 2, 4, 512], F32R), sb("lo", [P, 2, 4, 512], F32R)
        out = ps("out", [P, 8, 512])
        had_in, hr_s, sc_in, sc_s, sub_s = (sem(n) for n in ("had_in", "hr_s", "sc_in", "sc_s", "sub_s"))
        outer_low, outer_s = sem("outer_low"), sem("outer_s")
        piece_in, mix_s, hi_s, lo_s, mm_s = [sem(f"piece_in{i}") for i in range(2)], sem("mix_s"), sem("hi_s"), sem("lo_s"), sem("mm_s")
        dn_in = [sem(f"dn_in{i}") for i in range(2)]
        ev_gu_s, ev_d_s, x_pre = sem("ev_gu_s"), sem("ev_d_s"), sem("x_pre")
        pieces = [("g", n) for n in range(4)] + [("u", n) for n in range(4)] + [("d", n) for n in range(4)]
        GU = 8
        block = inner.enter_context(nc.Block())

        @block.sync
        def _(sp):
            def load(i):
                if i >= 2:
                    sp.wait_ge(mix_s, i - 1)
                if i == 2:
                    sp.wait_ge(sub_s, 1)
                m, n = pieces[i]
                sp.dma_start(stage[:, i % 2, :, :], io["wg" if m == "g" else "wu"][:, :, 512 * n:512 * n + 512]).then_inc(piece_in[i % 2], 16)

            def load_down(n):
                sp.dma_start(dn[:, 4 * n:4 * n + 4, :], io["wd"][:, 4 * n:4 * n + 4, :]).then_inc(dn_in[n % 2], 16)

            load(0)
            sp.dma_start(had[:, :, :], io["had"]).then_inc(had_in, 16)
            load(1)
            for t, n in ((su, "su"), (sd, "sd"), (dps, "dps"), (ug_scale, "ug_scale")):
                sp.dma_start(t[:], io[n]).then_inc(sc_in, 16)
            for n, i in ((0, 2), (2, 3), (1, 4), (3, 5)):
                load_down(n)
                load(i)
            load(6)
            load(7)
            sp.dma_start(xraw[:, :, :, :], x1t_dram[0]).then_inc(x_pre, 16)
            sp.wait_ge(x_pre, 16)

        @block.gpsimd
        def _(pool):
            for i in range(len(pieces)):
                if i < GU:
                    pool.wait_ge(piece_in[i % 2], 16 * (i // 2 + 1))
                    x = stage[:, i % 2, :, :]
                else:
                    pool.wait_ge(outer_s, i - GU + 1)
                    x = dn[:, 4 * (i - GU):4 * (i - GU) + 4, :]
                if i >= 2:
                    pool.wait_ge(lo_s, i - 1)
                j = pool.tensor_tensor(mixed[:, i % 2, 0:2, :], x[:, 0:2, :], x[:, 2:4, :], ALU.add)
                if i:
                    j = pool.tensor_tensor(mixed[:, i % 2, 2:4, :], x[:, 0:2, :], x[:, 2:4, :], ALU.subtract)
                j.then_inc(mix_s, 1)

        @block.scalar
        def _(act):
            act.wait_ge(had_in, 16)
            act.activation(hr[:, :, :], had[:, :, :], ACT.Copy).then_inc(hr_s, 1)
            act.wait_ge(sc_in, 64)

            def evacuate(i):
                m, n = pieces[i]
                for c in range(4):
                    act.wait_ge(mm_s, 4 * i + c + 1)
                    dst = (wg if m == "g" else wu)[:, c, 512 * n:512 * n + 512]
                    act.activation(dst, out[:, (4 * i + c) % 8, :], ACT.Identity, scale=su[:, c:c + 1]).then_inc(ev_gu_s, 1)

            for i in range(len(pieces)):
                act.wait_ge(mix_s, i + 1)
                if i == 0:
                    act.wait_ge(sub_s, 1)
                if i >= 2:
                    act.wait_ge(mm_s, 4 * (i - 1))
                act.activation(hi[:, i % 2, :, :], mixed[:, i % 2, :, :], ACT.Copy).then_inc(hi_s, 1)
                if 1 <= i <= GU:
                    evacuate(i - 1)

        @block.vector
        def _(dve):
            dve.wait_ge(piece_in[0], 16)
            dve.tensor_tensor(mixed[:, 0, 2:4, :], stage[:, 0, 0:2, :], stage[:, 0, 2:4, :], ALU.subtract).then_inc(sub_s, 1)
            dve.wait_ge(sc_in, 64)
            dve.tensor_scalar(ug_scale[:, :, :], ug_scale[:, :, :], float(D) ** -0.5, None, ALU.mult).then_inc(sc_s, 1)
            dve.tensor_scalar(dps[:, :], dps[:, :], float(INTER) ** -0.5, None, ALU.mult).then_inc(sc_s, 1)

            def outer(k):
                v = lambda t, a: t[:, :, :].rearrange("p (g c) n -> p g (c n)", g=4)[:, a, :]
                if k in (0, 2):
                    dve.wait_ge(dn_in[k // 2], 32)
                if k == 4:
                    dve.wait_ge(outer_low, 1)
                src, dst = (dn, wd) if k < 4 else (wd, dn)
                x, y, d, op = (((0, 2, 0, ALU.add), (0, 2, 2, ALU.subtract), (1, 3, 1, ALU.add), (1, 3, 3, ALU.subtract))
                               if k < 4 else
                               ((0, 1, 0, ALU.add), (0, 1, 1, ALU.subtract), (2, 3, 2, ALU.add), (2, 3, 3, ALU.subtract)))[k % 4]
                i = dve.tensor_tensor(v(dst, d), v(src, x), v(src, y), op)
                if k == 3:
                    i.then_inc(outer_low, 1)
                if k >= 4:
                    i.then_inc(outer_s, 1)

            def evacuate(i):
                for c in range(4):
                    dve.wait_ge(mm_s, 4 * i + c + 1)
                    k = 4 * (i - GU) + c
                    dve.scalar_tensor_tensor(wd[:, k, :], out[:, (4 * i + c) % 8, :], sd[:, k:k + 1], dps[:, :], ALU.mult, ALU.mult).then_inc(ev_d_s, 1)

            dve.wait_ge(sc_s, 2)
            for i in range(len(pieces)):
                dve.wait_ge(hi_s, i + 1)
                if i >= 2:
                    dve.wait_ge(mm_s, 4 * (i - 1))
                dve.tensor_tensor(lo[:, i % 2, :, :], mixed[:, i % 2, :, :], hi[:, i % 2, :, :].bitcast(F32), ALU.subtract).then_inc(lo_s, 1)
                for k in {3: (0, 1), 4: (2,), 5: (3, 4), 6: (5, 6), 7: (7,)}.get(i, ()):
                    outer(k)
                if i > GU:
                    evacuate(i - 1)
            evacuate(len(pieces) - 1)

        @block.tensor
        def _(pe):
            pe.wait_ge(hr_s, 1)
            for i in range(len(pieces)):
                pe.wait_ge(lo_s, i + 1)
                for c in range(4):
                    if i >= 2:
                        pe.wait_ge(*((ev_gu_s, 4 * (i - 2) + c + 1) if i - 2 < GU else (ev_d_s, 4 * (i - 2 - GU) + c + 1)))
                    bank = out[:, (4 * i + c) % 8, :]
                    for low in range(2):
                        s, sign = (c & 2) + low, c & low
                        pe.matmul(bank, hr[:, sign, :], hi[:, i % 2, s, :], start=(low == 0), stop=False)
                        j = pe.matmul(bank, hr[:, sign, :], lo[:, i % 2, s, :], start=False, stop=(low == 1))
                    j.then_inc(mm_s, 1)
    return wg, wu, wd, ug_scale, xraw


def ffn_block(nc, sems, x1_dram, x1t_dram, out_dram, wg, wu, wd, ug_scale, xraw):
    ctx = ExitStack()
    with ctx:
        sb, ps, signal, sem = tools(nc, ctx, sems, "ff")
        gu_hi = [sb(f"gu_hi{i}", [P, 2, DC, P], F32R) for i in range(2)]
        gu_lo = [sb(f"gu_lo{i}", [P, 2, DC, P], F32R) for i in range(2)]
        d_hi = [sb(f"d_hi{i}", [P, D], F32R) for i in range(2)]
        d_lo = [sb(f"d_lo{i}", [P, D], F32R) for i in range(2)]
        x_hi = [sb(f"x_hi{i}", [P, DC, FB], F32R) for i in range(2)]
        x_lo = [sb(f"x_lo{i}", [P, DC, FB], F32R) for i in range(2)]
        sg, hf = [sb(f"sg{i}", [P, FB]) for i in range(2)], [sb(f"hf{i}", [P, FB]) for i in range(2)]
        h_hi = [sb(f"h_hi{i}", [P, FB], F32R) for i in range(2)]
        h_lo = [sb(f"h_lo{i}", [P, FB], F32R) for i in range(2)]
        y = sb("y", [P, FT, D])
        bn, mv, power = sb("bn", [P, FT, 6]), sb("mv", [P, FT, 2]), sb("power", [P, 3, FT])
        rstd = sb("rstd", [P, 2, FT])
        acc = ps("acc", [P, FT, 512])
        g_ps, u_ps = ps("g_ps", [P, 512]), ps("u_ps", [P, 512])

        gate_s, up_s, down_s = signal("gate_s", 1), signal("up_s", 1), signal("down_s", 1)
        silu_s, prod_s, h_hi_s, h_lo_s = signal("silu_s", 1), signal("prod_s", 1), signal("h_hi_s", 1), signal("h_lo_s", 1)
        gu_hi_s, gu_lo_s, d_hi_s, d_lo_s = signal("gu_hi_s", 1), signal("gu_lo_s", 1), signal("d_hi_s", 1), signal("d_lo_s", 1)
        xraw_in, x1_in, x_hi_s, x_lo_s = signal("xraw_in", 16), signal("x1_in", 16), signal("x_hi_s", FT), signal("x_lo_s", 1)
        added, bn_s, var_s, pow_s = signal("added", FT), signal("bn_s", 2 * FT), signal("var_s", 1), signal("pow_s", 1)
        rstd_s, normed, stored = signal("rstd_s", 2), signal("normed", 1), signal("stored", 16)
        power_set, dve_past = sem("power_set"), sem("dve_past")

        def prime(eng, *signals):
            for s in signals:
                eng.sem_inc(s.sem, s.per)

        def blocks(eng, body):
            body(0, 0, True, False)
            with eng.Fori(0, FBLK // 2 - 1) as pair:
                body(pair * 2 + 1, 1, False, False)
                body(pair * 2 + 2, 0, False, False)
            body(FBLK - 1, 1, False, True)

        def steps(eng, step):
            for i in (1, 2, 3):
                step(i, i % 2, False)
            with eng.Fori(0, (IC - 6) // 2) as j:
                step(j * 2 + 4, 0, False)
                step(j * 2 + 5, 1, False)
            step(IC - 2, 0, False)
            step(IC - 1, 1, False)
            step(IC, 0, True)

        block = ctx.enter_context(nc.Block())

        @block.sync
        def _(sp):
            prime(sp, xraw_in, x1_in, stored)

            def load(blk):
                sp.wait_ge(*x_lo_s.last(blk, 1))
                sp.wait_ge(*x_hi_s.last(blk, FT))
                sp.dma_start(xraw[:, :, :, :], x1t_dram[blk]).then_inc(xraw_in.sem, 16)

            def store(blk):
                sp.wait_ge(*normed.now(blk, 1))
                sp.dma_start(out_dram[blk], y[:, :, :]).then_inc(stored.sem, 16)

            def body(blk, parity, first, last):
                if not last:
                    load(blk + 1)
                if not first:
                    store(blk - 1)
                sp.wait_ge(*stored.last(blk, 16))
                sp.dma_start(y[:, :, :], x1_dram[blk]).then_inc(x1_in.sem, 16)

            sp.sem_inc(xraw_in.sem, 16)
            blocks(sp, body)
            store(FBLK - 1)
            sp.wait_ge(*stored.now(FBLK - 1, 16))

        @block.gpsimd
        def _(pool):
            prime(pool, var_s, pow_s, rstd_s)
            for i, v in enumerate((-0.5, EPS, -1.0)):
                pool.memset(power[:, i, :], v).then_inc(power_set, 1)
            pool.wait_ge(power_set, 3)
            with pool.Fori(0, FBLK) as blk:
                pool.wait_ge(*bn_s.now(blk, 2 * FT))
                pool.wait_ge(*normed.last(blk, 1))
                r, m = rstd[:, 0, :], rstd[:, 1, :]
                pool.tensor_tensor(r, mv[:, :, 1], power[:, 1, :], ALU.add).then_inc(var_s.sem, 1)
                pool.tensor_tensor(m, mv[:, :, 0], power[:, 2, :], ALU.mult).then_inc(rstd_s.sem, 1)
                pool.wait_ge(*var_s.now(blk, 1))
                pool.tensor_tensor(r, r, power[:, 0, :], ALU.pow).then_inc(pow_s.sem, 1)
                pool.wait_ge(*pow_s.now(blk, 1))
                pool.wait_ge(*rstd_s.now(blk, 1))
                pool.tensor_tensor(m, m, r, ALU.mult).then_inc(rstd_s.sem, 1)

        def gate_up_chunk(w, i):
            return w[:, :, bass.ds(i * P, P)]

        @block.scalar
        def _(act):
            prime(act, silu_s, h_hi_s, gu_hi_s, d_hi_s, x_hi_s, normed)

            def split_x(blk, p):
                act.wait_ge(*xraw_in.now(blk, 16))
                for t in range(FT):
                    act.activation(x_hi[p][:, :, P * t:P * t + P], xraw[:, t, :, :], ACT.Copy).then_inc(x_hi_s.sem, 1)

            def split_gu(s, i, q):
                act.wait_ge(up_s.sem, s)
                act.activation(gu_hi[q][:, 0, :, :], gate_up_chunk(wg, i), ACT.Copy)
                act.activation(gu_hi[q][:, 1, :, :], gate_up_chunk(wu, i), ACT.Copy).then_inc(gu_hi_s.sem, 1)

            def chunk_work(s, i, q):
                act.wait_ge(*gate_s.now(s, 1))
                if not isinstance(s, int) or s > 0:
                    act.wait_ge(prod_s.sem, s)
                act.activation(sg[q][:, :], g_ps[:, :], ACT.Silu, scale=ug_scale[:, 1, bass.ds(i, 1)]).then_inc(silu_s.sem, 1)
                if not isinstance(s, int) or s > 0:
                    act.wait_ge(down_s.sem, s)
                act.activation(d_hi[q][:, :], wd[:, bass.ds(i, 1), :].rearrange("p a n -> p (a n)"), ACT.Copy).then_inc(d_hi_s.sem, 1)

            def round_h(s, q):
                act.wait_ge(*prod_s.now(s, 1))
                act.activation(h_hi[q][:, :], hf[q][:, :], ACT.Copy).then_inc(h_hi_s.sem, 1)

            def normalise(blk):
                act.wait_ge(*rstd_s.now(blk, 2))
                for t in range(FT):
                    i = act.activation(y[:, t, :], y[:, t, :], ACT.Identity, bias=rstd[:, 1, t:t + 1], scale=rstd[:, 0, t:t + 1])
                i.then_inc(normed.sem, 1)

            def body(blk, parity, first, last):
                def step(i, q, wrap):
                    s = blk * IC + i
                    if wrap and last:
                        return
                    if wrap:
                        chunk_work(s, 0, q)
                        split_gu(s + 1, 1, 1 - q)
                        round_h(s, q)
                        return
                    chunk_work(s, i, q)
                    if isinstance(i, int) and i == IC - 1:
                        if not last:
                            split_gu(s + 1, 0, 1 - q)
                    else:
                        split_gu(s + 1, i + 1, 1 - q)
                    round_h(s, q)
                    if isinstance(i, int) and i == 2 and not first:
                        normalise(blk - 1)
                    if isinstance(i, int) and i == IC - 2 and not last:
                        split_x(blk + 1, 1 - parity)

                steps(act, step)

            split_x(0, 0)
            act.activation(gu_hi[0][:, 0, :, :], wg[:, :, 0:P], ACT.Copy)
            act.activation(gu_hi[0][:, 1, :, :], wu[:, :, 0:P], ACT.Copy).then_inc(gu_hi_s.sem, 1)
            chunk_work(0, 0, 0)
            split_gu(1, 1, 1)
            round_h(0, 0)
            blocks(act, body)
            normalise(FBLK - 1)

        @block.vector
        def _(dve):
            prime(dve, prod_s, h_lo_s, gu_lo_s, d_lo_s, x_lo_s, added, bn_s)

            def split_x(blk, p):
                for t in range(FT):
                    dve.wait_ge(*x_hi_s.now(blk, t + 1))
                    k = slice(P * t, P * t + P)
                    i = dve.tensor_tensor(x_lo[p][:, :, k], xraw[:, t, :, :], x_hi[p][:, :, k].bitcast(F32), ALU.subtract)
                i.then_inc(x_lo_s.sem, 1)

            def split_gu(s, i, q):
                dve.wait_ge(*gu_hi_s.now(s, 1))
                dve.tensor_tensor(gu_lo[q][:, 0, :, :], gate_up_chunk(wg, i), gu_hi[q][:, 0, :, :].bitcast(F32), ALU.subtract)
                dve.tensor_tensor(gu_lo[q][:, 1, :, :], gate_up_chunk(wu, i), gu_hi[q][:, 1, :, :].bitcast(F32), ALU.subtract).then_inc(gu_lo_s.sem, 1)

            def chunk_work(s, i, q):
                dve.wait_ge(*d_hi_s.now(s, 1))
                dve.tensor_tensor(d_lo[q][:, :], wd[:, bass.ds(i, 1), :].rearrange("p a n -> p (a n)"), d_hi[q][:, :].bitcast(F32),
                                  ALU.subtract).then_inc(d_lo_s.sem, 1)
                dve.wait_ge(*up_s.now(s, 1))
                dve.wait_ge(*silu_s.now(s, 1))
                dve.scalar_tensor_tensor(hf[q][:, :], u_ps[:, :], ug_scale[:, 0, bass.ds(i, 1)], sg[q][:, :], ALU.mult, ALU.mult).then_inc(prod_s.sem, 1)

            def lower_h(s, q):
                dve.wait_ge(*h_hi_s.now(s, 1))
                dve.wait_ge(*prod_s.now(s, 1))
                dve.tensor_tensor(h_lo[q][:, :], hf[q][:, :], h_hi[q][:, :].bitcast(F32), ALU.subtract).then_inc(h_lo_s.sem, 1)

            def residual(blk):
                dve.wait_ge(*x1_in.now(blk, 16))
                for t in range(FT):
                    dve.wait_ge(down_s.sem, (blk + 1) * IC + 1)
                    dve.tensor_tensor(y[:, t, :], acc[:, t, :], y[:, t, :], ALU.add).then_inc(added.sem, 1)

            def statistics(blk):
                dve.wait_ge(*rstd_s.last(blk, 2))
                for t in range(FT):
                    dve.wait_ge(*added.now(blk, t + 1))
                    dve.bn_stats(bn[:, t, :], y[:, t, :]).then_inc(bn_s.sem, 1)
                dve.wait_ge(*bn_s.now(blk, FT))
                dve.sem_inc(dve_past, 1)
                for t in range(FT):
                    dve.bn_aggr(mv[:, t, :], bn[:, t, :]).then_inc(bn_s.sem, 1)

            def body(blk, parity, first, last):
                def step(i, q, wrap):
                    s = blk * IC + i
                    if wrap and last:
                        residual(blk)
                        return
                    nxt = 0 if isinstance(i, int) and i == IC - 1 else (1 if wrap else i + 1)
                    if not (last and isinstance(i, int) and i == IC - 1):
                        split_gu(s + 1, nxt, 1 - q)
                    chunk_work(s, 0 if wrap else i, q)
                    lower_h(s, q)
                    if wrap:
                        residual(blk)
                    if isinstance(i, int) and i == 1 and not first:
                        statistics(blk - 1)
                    if isinstance(i, int) and i == IC - 2 and not last:
                        split_x(blk + 1, 1 - parity)

                steps(dve, step)

            split_x(0, 0)
            split_gu(0, 0, 0)
            split_gu(1, 1, 1)
            chunk_work(0, 0, 0)
            lower_h(0, 0)
            blocks(dve, body)
            statistics(FBLK - 1)

        @block.tensor
        def _(pe):
            prime(pe, gate_s, up_s, down_s)

            def gate_up(s, q, p):
                pe.wait_ge(*gu_lo_s.now(s, 1))
                for m, bank, free, done in ((0, g_ps, silu_s, gate_s), (1, u_ps, prod_s, up_s)):
                    pe.wait_ge(free.sem, s + 1)
                    for c in range(DC):
                        i = three_passes(pe, bank[:, :], gu_hi[q][:, m, c, :], gu_lo[q][:, m, c, :], x_hi[p][:, c, :], x_lo[p][:, c, :],
                                         c == 0, c == DC - 1)
                    i.then_inc(done.sem, 1)

            def down(s, q, first, last):
                pe.wait_ge(*h_lo_s.now(s, 1))
                pe.wait_ge(*d_lo_s.now(s, 1))
                for t in range(FT):
                    k = slice(P * t, P * t + P)
                    i = three_passes(pe, acc[:, t, :], h_hi[q][:, k], h_lo[q][:, k], d_hi[q][:, :], d_lo[q][:, :], first, last)
                i.then_inc(down_s.sem, 1)

            def body(blk, parity, first, last):
                def step(i, q, wrap):
                    s = blk * IC + i
                    if wrap:
                        if not last:
                            pe.wait_ge(*x_lo_s.now(blk + 1, 1))
                            gate_up(s, q, 1 - parity)
                        down(s - 1, 1 - q, False, True)
                        return
                    gate_up(s, q, parity)
                    start = isinstance(i, int) and i == 1
                    if start:
                        pe.wait_ge(*added.last(blk, FT))
                    down(s - 1, 1 - q, start, False)

                steps(pe, step)

            pe.wait_ge(*x_lo_s.now(0, 1))
            gate_up(0, 0, 0)
            blocks(pe, body)


def layer_kernel(nc, io, out):
    x1_dram = nc.dram_tensor("x1_scratch", [B * T, D], F32, kind="Internal").ap()
    x1t_dram = nc.dram_tensor("x1t_scratch", [B * TILES, P, D], F32, kind="Internal").ap()
    io["x"] = io["x"].rearrange("b (t p) d -> b t p d", p=P)
    sems = ExitStack()
    with sems:
        whole_layer(nc, sems, io, x1_dram, x1t_dram, out)


def whole_layer(nc, sems, io, x1_dram, x1t_dram, out):
    attention_block(nc, sems, io, x1_dram.rearrange("(b t p) d -> b t p d", t=TILES, p=P),
                    x1t_dram.rearrange("(b t) p d -> b t p d", t=TILES))
    ctx = ExitStack()
    with ctx:
        x1t_blocks = x1t_dram.rearrange("(n t) p (c q) -> n p t c q", t=FT, c=DC)
        folded = weights_block(nc, sems, io, x1t_blocks, ctx)
        ffn_block(nc, sems, x1_dram.rearrange("(n t p) d -> n p t d", t=FT, p=P), x1t_blocks,
                  out.rearrange("b (m t p) d -> (b m) p t d", t=FT, p=P), *folded)


def shape_tables():
    import numpy as np
    f = np.float32
    p = np.arange(P)
    inv = f(1.0) / (f(10000.0) ** (np.arange(0, DG, 2, dtype=f) / f(DG)))
    ang = np.arange(T, dtype=f)[:, None] * inv.astype(f)[None, :]
    cos, sin = np.cos(ang).astype(f), np.sin(ang).astype(f)
    rope = np.stack([cos, sin], 1).reshape(TILES, P, 2, HALF).transpose(1, 0, 2, 3)
    own = lambda n, w, k: np.repeat((p[:, None] // w == np.arange(n)[None, :]).astype(f), k, axis=1)
    pos = np.arange(REMOTE).reshape(RT, P).T[:, :, None]
    k = np.arange(NB)[None, None, :]
    pool_w = np.where(pos // MB == k, f(1.0 / MB), f(0)).astype(f)
    sees = MB * k + MB - 1 <= pos
    keep, hide = sees.astype(f), np.where(sees, f(0), f(NEG)).astype(f)
    none = ~sees.any(-1)
    spread, rest = np.where(none, f(KEYS / NB), f(1)).astype(f), np.where(none, f(1.0 / KEYS), f(0)).astype(f)
    causal = np.where(p[None, :] <= p[:, None], f(0), f(NEG)).astype(f)
    small = np.concatenate([own(4, DS, NB), own(8, HALF, NB), own(2, DV, NK), pool_w.reshape(P, -1), keep.reshape(P, -1),
                            hide.reshape(P, -1), spread, rest, causal], axis=1)
    had = np.array([[1 - 2 * (bin(i & j).count("1") % 2) for j in range(P)] for i in range(P)], f)
    return {"ident": np.eye(P, dtype=f), "cos_t": np.tile(cos[:REMOTE].T, (P // HALF, 1)), "sin_t": np.tile(sin[:REMOTE].T, (P // HALF, 1)),
            "rope": rope, "small": small, "had": np.stack([had, -had], 1)}


def kernel(**inputs):
    import numpy as np
    import concourse.bacc as bacc
    from concourse.bass_utils import run_bass_kernel_spmd as run

    a = {n: np.asarray(v) for n, v in inputs.items()}
    x = a["L0_attn_x"]
    rows = lambda w: w.reshape(w.shape[0] // P, P, -1).transpose(1, 0, 2)
    halves = lambda w, h: w.reshape(D, h, 2, HALF).transpose(0, 2, 1, 3).reshape(D, -1)
    ls = a["L0_attn_logit_scale"]
    chunk_rows = np.repeat(ls, DS).reshape(DC, P).T
    wo = a["L0_attn_Wo"].reshape(2, 2, 4, DV, D).transpose(1, 3, 0, 2, 4).reshape(P, 8, D)
    arrays = {
        "x": x,
        "xt": x.transpose(0, 2, 1).reshape(B, DC, P, T).transpose(0, 2, 1, 3),
        "wq": rows(np.concatenate([a["L0_attn_Wq_sem"], halves(a["L0_attn_Wq_geo"], H)], 1)),
        "wqs": rows(a["L0_attn_Wq_sem"].T),
        "wkv": rows(np.concatenate([halves(a["L0_attn_Wk_geo"], HKV), a["L0_attn_Wk_sem"], a["L0_attn_Wv"]], 1)),
        "wo": wo,
        "logit_scale": np.concatenate([np.broadcast_to(ls, (P, H)), chunk_rows], 1),
        "wg": rows(a["L0_ffn_W_gate"].T), "wu": rows(a["L0_ffn_W_up"].T), "wd": rows(a["L0_ffn_W_down"].T),
        "su": a["L0_ffn_SU_ug"].reshape(DC, P).T, "sd": a["L0_ffn_SU_dp"].reshape(IC, P).T,
        "dps": np.broadcast_to(a["L0_ffn_Wscale_dp"], (P, D)),
        "ug_scale": a["L0_ffn_Wscale_ug"].reshape(2, IC, P).transpose(2, 0, 1),
        **shape_tables(),
    }
    arrays = {f"in_{n}": np.ascontiguousarray(v) for n, v in arrays.items()}
    nc = bacc.Bacc("TRN2", target_bir_lowering=False, num_devices=1)
    io = {n[3:]: nc.dram_tensor(n, v.shape, mybir.dt.from_np(v.dtype), kind="ExternalInput").ap() for n, v in arrays.items()}
    out = nc.dram_tensor("out", (B, T, D), F32, kind="ExternalOutput").ap()
    layer_kernel(nc, io, out)
    return run(nc, [arrays], core_ids=[0]).results[0]["out"]
```

```python
from contextlib import ExitStack

import concourse.bass as bass
from concourse import mybir

F32 = mybir.dt.float32
F32R = mybir.dt.float32r
ACT = mybir.ActivationFunctionType
ALU = mybir.AluOpType
AX = mybir.AxisListType

P = 128
B, T, D = 4, 1024, 512
H, HKV, DS, DG, DV = 16, 4, 32, 32, 64
REP = H // HKV
MB, LW = 64, 256
REMOTE = T - LW
NB = REMOTE // MB
NK = NB + 1
HALF = DG // 2
INTER = 2048
DC = D // P
IC = INTER // P
RT = REMOTE // P
LT = LW // P
TILES = RT + LT
QB = 256
RB = REMOTE // QB
NEG = -1.0e9
EPS = 1e-5
KEYS = NB + LW
HK = H // 2 * NK
HB = H // 2 * NB
FB = 512
FBLK = B * T // FB
FT = FB // P


class Signal:

    def __init__(self, ctx, nc, name, per):
        self.sem, self.per = ctx.enter_context(nc.semaphore(name)), per

    def now(self, i, k):
        return self.sem, (i + 1) * self.per + k

    def last(self, i, k):
        return self.sem, i * self.per + k


def tools(nc, ctx, sems, tag):
    def sb(name, shape, dt=F32):
        return ctx.enter_context(nc.sbuf_tensor(f"{tag}_{name}", shape, dt))

    def ps(name, shape):
        return ctx.enter_context(nc.psum_tensor(f"{tag}_{name}", shape, F32))

    def signal(name, per):
        return Signal(sems, nc, f"{tag}_{name}", per)

    def sem(name):
        return sems.enter_context(nc.semaphore(f"{tag}_{name}"))

    return sb, ps, signal, sem


def three_passes(pe, out, lhs_hi, lhs_lo, rhs_hi, rhs_lo, first, last):
    pe.matmul(out, lhs_hi, rhs_hi, start=first, stop=False)
    pe.matmul(out, lhs_hi, rhs_lo, start=False, stop=False)
    return pe.matmul(out, lhs_lo, rhs_hi, start=False, stop=last)


def bc(ap, axis, n):
    wide = ap.unsqueeze(axis)
    shape = list(wide.shape)
    shape[axis] = n
    return wide.broadcast_to(shape)


def attention_block(nc, sems, io, x1_dram, x1t_dram):
    ctx = ExitStack()
    with ctx:
        sb, ps, signal, sem = tools(nc, ctx, sems, "at")
        wq_hi, wq_lo = sb("wq_hi", [P, DC, 2 * D], F32R), sb("wq_lo", [P, DC, 2 * D], F32R)
        wo_hi, wo_lo = sb("wo_hi", [P, 8, D], F32R), sb("wo_lo", [P, 8, D], F32R)
        wkv = sb("wkv", [P, DC, D])
        wqs = sb("wqs", [P, DC, D])
        ident = sb("ident", [P, P])
        cos_t, sin_t = sb("cos_t", [P, REMOTE]), sb("sin_t", [P, REMOTE])
        rope = sb("rope", [P, TILES, 2, HALF])
        small = sb("small", [P, 4 * NB + 8 * NB + 2 * NK + RT * NB * 3 + 2 * RT + P])
        o = 0
        def table(*shape):
            nonlocal o
            n = 1
            for s in shape:
                n *= s
            v = small[:, o:o + n]
            o += n
            if len(shape) == 2:
                v = v.rearrange("p (a b) -> p a b", a=shape[0])
            return v
        own_sem = table(4, NB)
        own_geo = table(8, NB)
        own_v = table(2, NK)
        pool_w = table(RT, NB)
        keep = table(RT, NB)
        hide = table(RT, NB)
        spread = table(RT)
        rest_p = table(RT)
        causal = table(P)
        scales = sb("scales", [P, H + DC])
        power = sb("power", [P, 3])
        xt = sb("xt", [P, DC, T])
        xn = sb("xn", [P, 2, D])
        xs_hi, xs_lo = sb("xs_hi", [P, 2, DC, QB], F32R), sb("xs_lo", [P, 2, DC, QB], F32R)
        xpool = sb("xpool", [P, DC, NK])
        krot = sb("krot", [P, LT, HKV, 2 * DS])
        v_hi, v_lo = sb("v_hi", [P, LT, HKV * DV], F32R), sb("v_lo", [P, LT, HKV * DV], F32R)
        kt_hi, kt_lo = sb("kt_hi", [P, 2, 2, KEYS], F32R), sb("kt_lo", [P, 2, 2, KEYS], F32R)
        ks_bd = sb("ks_bd", [P, 4, 4 * NB])
        kg_bd = sb("kg_bd", [P, 4, 8 * NB])
        m_sb = sb("m_sb", [P, DC, H * NB])
        vwo_hi, vwo_lo = sb("vwo_hi", [HK, 2, D], F32R), sb("vwo_lo", [HK, 2, D], F32R)
        union = sb("union", [P, H * KEYS])
        q_rem = union[:, 0:RB * 4 * QB].rearrange("p (n r c) -> p n r c", n=RB, r=2)
        q_rot = union[:, 3072:3072 + D]
        rt1, rt2 = union[:, 3072:3584], union[:, 3584:4096]
        kgr = union[:, 0:768].rearrange("p (t e) -> p t e", t=RT)
        kt1, kt2 = union[:, 768:1152], union[:, 1152:1536]
        kp = union[0:NK, 1536:1536 + D]
        VB = 2 * 4 * QB
        vbd = union[:, VB:VB + 8 * HK]
        probs_l = union[:, :].rearrange("p (h k) -> p h k", h=H)
        sm = sb("sm", [P, 2, H * NB])
        pr = sb("pr", [P, 2, H, NK])
        stat = sb("stat", [P, 2, 4, H])
        pt_hi, pt_lo = sb("pt_hi", [HK, 2, P], F32R), sb("pt_lo", [HK, 2, P], F32R)
        qrot = sb("qrot", [P, 8, 2, DV])
        lt1, lt2 = sb("lt1", [P, H * HALF]), sb("lt2", [P, H * HALF])
        kr = qrot[0:NK, :, :, :].rearrange("p c s e -> p (c s e)")
        kr_by_head = lt1[0:NK, :]
        qo_hi, qo_lo = sb("qo_hi", [P, 8, P], F32R), sb("qo_lo", [P, 8, P], F32R)
        q_hi = [qo_hi[:, :, :], xs_hi[:, 0, :, :].rearrange("p c (u q) -> p (c u) q", q=P)]
        q_lo = [qo_lo[:, :, :], xs_lo[:, 0, :, :].rearrange("p c (u q) -> p (c u) q", q=P)]
        tp_hi, tp_lo = sb("tp_hi", [P, 2, 4 * P], F32R), sb("tp_lo", [P, 2, 4 * P], F32R)
        vb_hi = tp_hi[:, :, :].rearrange("p a b -> p (a b)")[:, 0:8 * HK]
        vb_lo = tp_lo[:, :, :].rearrange("p a b -> p (a b)")[:, 0:8 * HK]
        x1, x1t = sb("x1", [P, 2, D]), sb("x1t", [P, 2, D])
        bn, mv, rstd = sb("bn", [P, 2, 6]), sb("mv", [P, 2, 2]), sb("rstd", [P, 2, 2])

        big = ps("big", [P, 4, 512])
        mid = ps("mid", [P, 2, 512])
        tr = ps("tr", [P, 512])
        acc = ps("acc", [P, 512])

        wq_raw = [union[:, 2 * D * c:2 * D * (c + 1)] for c in range(DC)]
        qr_flat = qrot[:, :, :, :].rearrange("p c s e -> p (c s e)")
        wo_raw = [x1[:, 0, :], x1[:, 1, :], x1t[:, 0, :], x1t[:, 1, :], qr_flat[:, 0:D], qr_flat[:, D:2 * D],
                  m_sb[:, :, :].rearrange("p c n -> p (c n)")[:, 0:D], krot[:, :, :, :].rearrange("p t g e -> p (t g e)")]

        wkv_in, wqs_in, tab_in, ls_in = (sem(n) for n in ("wkv_in", "wqs_in", "tab_in", "ls_in"))
        wq_in, wo_in = [sem(f"wq_in{c}") for c in range(DC)], [sem(f"wo_in{c}") for c in range(8)]
        scale_exp, scale_done, wq_scaled, wqs_scaled, power_set, zeroed = (
            sem(n) for n in ("scale_exp", "scale_done", "wq_scaled", "wqs_scaled", "power_set", "zeroed"))
        wq_hi_s, wq_lo_s, wo_hi_s, wo_lo_s = (sem(n) for n in ("wq_hi_s", "wq_lo_s", "wo_hi_s", "wo_lo_s"))
        dve_past, pe_past = sem("dve_past"), sem("pe_past")
        xt_in = signal("xt_in", 16)
        xn_in = [signal(f"xn_in{i}", 16 * TILES // 2) for i in range(2)]
        xs_hi_s, xs_lo_s = signal("xs_hi_s", RB + 1), signal("xs_lo_s", RB + 1)
        kgeo_ps, kv_ps = signal("kgeo_ps", 1), signal("kv_ps", LT)
        xsum, xpool_s = signal("xsum", 2), signal("xpool_s", 1)
        krope = signal("krope", 12)
        krot_sem, v_hi_s, v_lo_s = signal("krot_sem", 1), signal("v_hi_s", 1), signal("v_lo_s", 1)
        kp_ps, kp_s, kr_s = signal("kp_ps", 1), signal("kp_s", 2), signal("kr_s", 6)
        ktr_ps, klt_ps = signal("ktr_ps", 1), signal("klt_ps", 1)
        kt_hi_s, kt_lo_s = signal("kt_hi_s", 2), signal("kt_lo_s", 2)
        bd_s, vbd_s, vb_hi_s, vb_lo_s = signal("bd_s", 2), signal("vbd_s", 2), signal("vb_hi_s", 1), signal("vb_lo_s", 1)
        m_ps, m_s = signal("m_ps", 1), signal("m_s", 1)
        vwo_ps, vwo_hi_s, vwo_lo_s = signal("vwo_ps", 2), signal("vwo_hi_s", 2), signal("vwo_lo_s", 2)
        qg_ps, qrope = signal("qg_ps", RB), signal("qrope", 6 * RB)
        s_ps, masked, shifted = signal("s_ps", RT), signal("masked", RT + 1), signal("shifted", 2 * RT)
        exp_s, summed, probs_s = signal("exp_s", RT), signal("summed", 2 * RT + 1), signal("probs_s", RT)
        pt_ps, pt_hi_s, pt_lo_s = signal("pt_ps", TILES), signal("pt_hi_s", TILES), signal("pt_lo_s", TILES)
        out_ps, added, normed = signal("out_ps", TILES), signal("added", TILES), signal("normed", TILES)
        bn_s, var_s, pow_s, rstd_s = signal("bn_s", 2 * TILES), signal("var_s", TILES), signal("pow_s", TILES), signal("rstd_s", 2 * TILES)
        x1t_ps, x1t_s = signal("x1t_ps", TILES), signal("x1t_s", TILES)
        x1_out = [signal(f"x1_out{i}", 16 * TILES // 2) for i in range(2)]
        x1t_out = [signal(f"x1t_out{i}", 16 * TILES // 2) for i in range(2)]
        qp_ps, qsem_s, lrope = signal("qp_ps", 2 * LT), signal("qsem_s", LT), signal("lrope", 6 * LT)
        lcopy = signal("lcopy", LT)
        qt_ps, qt_hi_s, qt_lo_s = signal("qt_ps", LT), signal("qt_hi_s", LT), signal("qt_lo_s", LT)
        ls_ps, lmasked, lmax, lexp = signal("ls_ps", 8 * LT), signal("lmasked", 8 * LT), signal("lmax", 8 * LT), signal("lexp", 8 * LT)
        lrecip, lnorm = signal("lrecip", 8 * LT), signal("lnorm", 8 * LT)
        NPT = [HKV * (tt + 1) for tt in range(LT)]
        tp_ps, tp_hi_s, tp_lo_s = signal("tp_ps", sum(NPT)), signal("tp_hi_s", sum(NPT)), signal("tp_lo_s", sum(NPT))
        pv_ps, o_hi_s, o_lo_s = signal("pv_ps", sum(NPT)), signal("o_hi_s", HKV * LT), signal("o_lo_s", HKV * LT)

        GROUPS = LT * HKV
        ROUNDS = GROUPS + 2
        BLOCKS = {i: [sum(NPT[:i // HKV]) + (i % HKV) * (i // HKV + 1) + k for k in range(i // HKV + 1)] for i in range(GROUPS)}

        def pair_scores(tt, p):
            if tt == 0:
                return big[:, p % 2, :].rearrange("p (u k) -> p u k", u=2)
            m = 2 * ((p + 1) % 2)
            return big[:, m:m + 2, :]

        def x1t_bank(t):
            return (big[:, 2] if t == RT else tr)[:, :]

        def prime(eng, *signals):
            for s in signals:
                eng.sem_inc(s.sem, s.per)

        def flat(t):
            return t[:, :, :].rearrange("p a b -> p (a b)")

        qf = flat(big)

        def own_columns(a, s):
            n = HK + NK
            j, r = divmod(4 * a * HK + 4 * s * NK, n)
            return union[:, VB:VB + 8 * n].rearrange("p (j n) -> p j n", n=n)[:, j:j + 4, r:r + NK]

        block = ctx.enter_context(nc.Block())

        @block.sync
        def _(sp):
            prime(sp, xt_in, *xn_in, *x1_out, *x1t_out)
            sp.dma_start(xt[:, :, :], io["xt"][0]).then_inc(xt_in.sem, 16)
            for c in range(8):
                sp.dma_start(wo_raw[c], io["wo"][:, c, :]).then_inc(wo_in[c], 16)
            for t, n in ((ident, "ident"), (cos_t, "cos_t"), (sin_t, "sin_t"), (rope, "rope"), (small, "small")):
                sp.dma_start(t[:], io[n]).then_inc(tab_in, 16)

            def tiles(b, fetch):
                def load(t):
                    sp.wait_ge(*(added.now(b, t - 1) if t >= 2 else added.last(b, TILES - 1 + t)))
                    sp.dma_start(xn[:, t % 2, :], io["x"][b, t]).then_inc(xn_in[t % 2].sem, 16)

                def store_transposed(t):
                    sp.wait_ge(*x1t_s.now(b, t + 1))
                    sp.dma_start(x1t_dram[b, t], x1t[:, t % 2, :]).then_inc(x1t_out[t % 2].sem, 16)

                load(0)
                load(1)
                for t in range(TILES):
                    sp.wait_ge(*normed.now(b, t + 1))
                    sp.dma_start(x1_dram[b, t], x1[:, t % 2, :]).then_inc(x1_out[t % 2].sem, 16)
                    if t + 2 < TILES:
                        load(t + 2)
                    if fetch and t == RT - 1:
                        sp.wait_ge(*xs_hi_s.now(b, RB + 1))
                        sp.wait_ge(*xs_lo_s.now(b, RB + 1))
                        sp.wait_ge(*s_ps.now(b, RT))
                        sp.dma_start(xt[:, :, :], io["xt"][b + 1]).then_inc(xt_in.sem, 16)
                    if t:
                        store_transposed(t - 1)
                store_transposed(TILES - 1)

            with sp.Fori(0, B - 1) as b:
                tiles(b, True)
            tiles(B - 1, False)
            for s in (*x1_out, *x1t_out):
                sp.wait_ge(*s.now(B - 1, 16 * TILES // 2))

        @block.gpsimd
        def _(pool):
            prime(pool, var_s, pow_s, rstd_s, lnorm, xs_lo_s, lrope)
            pool.dma_start(scales[:, :], io["logit_scale"]).then_inc(ls_in, 16)
            pool.dma_start(wkv[:, :, :], io["wkv"]).then_inc(wkv_in, 16)
            pool.dma_start(wqs[:, :, :], io["wqs"]).then_inc(wqs_in, 16)
            for i, v in enumerate((-0.5, EPS, -1.0)):
                pool.memset(power[:, i:i + 1], v).then_inc(power_set, 1)
            for c in range(8):
                pool.wait_ge(wo_hi_s, c + 1)
                pool.tensor_tensor(wo_lo[:, c, :], wo_raw[c], wo_hi[:, c, :].bitcast(F32), ALU.subtract).then_inc(wo_lo_s, 1)
            pool.wait_ge(power_set, 3)

            def inverse_deviation(b, t):
                pool.wait_ge(*bn_s.now(b, 2 * t + 2))
                pool.wait_ge(*(normed.now(b, t - 1) if t >= 2 else normed.last(b, TILES - 1 + t)))
                r, m = rstd[:, t % 2, 0:1], rstd[:, t % 2, 1:2]
                pool.tensor_tensor(r, mv[:, t % 2, 1:2], power[:, 1:2], ALU.add).then_inc(var_s.sem, 1)
                pool.wait_ge(*var_s.now(b, t + 1))
                pool.tensor_tensor(r, r, power[:, 0:1], ALU.pow).then_inc(pow_s.sem, 1)
                pool.tensor_tensor(m, mv[:, t % 2, 0:1], power[:, 2:3], ALU.mult).then_inc(rstd_s.sem, 1)
                pool.wait_ge(*pow_s.now(b, t + 1))
                pool.wait_ge(*rstd_s.now(b, 2 * t + 1))
                pool.tensor_tensor(m, m, r, ALU.mult).then_inc(rstd_s.sem, 1)

            def split_x(b, n):
                pool.wait_ge(*xs_hi_s.now(b, n + 1))
                pool.tensor_tensor(xs_lo[:, n % 2, :, :], xt[:, :, n * QB:(n + 1) * QB],
                                   xs_hi[:, n % 2, :, :].bitcast(F32), ALU.subtract).then_inc(xs_lo_s.sem, 1)

            def normalise(b, tt, p):
                t, n, h = RT + tt, P * (tt + 1), slice(2 * p, 2 * p + 2)
                pool.wait_ge(*lrecip.now(b, 8 * tt + p + 1))
                if p == 0:
                    pool.wait_ge(*pt_ps.now(b, t - 1))
                v = probs_l[:, h, NB:NB + n]
                pool.tensor_tensor(pr[:, t % 2, h, 0:NB], probs_l[:, h, 0:NB], bc(stat[:, tt, 3, h], 2, NB), ALU.mult)
                pool.tensor_tensor(v, v, bc(stat[:, tt, 3, h], 2, n), ALU.mult).then_inc(lnorm.sem, 1)

            def rotate_local(b, tt):
                t = RT + tt
                pool.wait_ge(*qsem_s.now(b, tt + 1))
                pool.wait_ge(*lcopy.now(b, tt + 1))
                if tt:
                    pool.wait_ge(*lrope.now(b, 6 * tt))
                q_out = lambda e0: qrot[:, :, :, e0:e0 + HALF].rearrange("p (a j) s e -> p a s j e", a=2)
                head = lambda v: v.rearrange("p (h f) -> p h f", h=H)
                cos, sin = bc(rope[:, t, 0, :], 1, H), bc(rope[:, t, 1, :], 1, H)
                in1, in2 = head(q_rot[:, 0:256]), head(q_rot[:, 256:512])
                pool.tensor_tensor(head(lt1[:, :]), in1, cos, ALU.mult).then_inc(lrope.sem, 1)
                pool.tensor_tensor(head(lt2[:, :]), in2, sin, ALU.mult).then_inc(lrope.sem, 1)
                pool.wait_ge(*lrope.now(b, 6 * tt + 2))
                parts = lambda v, a: v[:, 128 * a:128 * a + 128].rearrange("p (s j f) -> p s j f", s=2, j=4)
                pool.tensor_tensor(q_out(DS)[:, 0], parts(lt1, 0), parts(lt2, 0), ALU.subtract)
                pool.tensor_tensor(q_out(DS)[:, 1], parts(lt1, 1), parts(lt2, 1), ALU.subtract).then_inc(lrope.sem, 1)
                pool.wait_ge(*lrope.now(b, 6 * tt + 3))
                pool.tensor_tensor(head(lt1[:, :]), in2, cos, ALU.mult).then_inc(lrope.sem, 1)
                pool.tensor_tensor(head(lt2[:, :]), in1, sin, ALU.mult).then_inc(lrope.sem, 1)
                pool.wait_ge(*lrope.now(b, 6 * tt + 5))
                pool.tensor_tensor(q_out(DS + HALF)[:, 0], parts(lt1, 0), parts(lt2, 0), ALU.add)
                pool.tensor_tensor(q_out(DS + HALF)[:, 1], parts(lt1, 1), parts(lt2, 1), ALU.add).then_inc(lrope.sem, 1)

            with pool.Fori(0, B) as b:
                split_x(b, 0)
                split_x(b, 1)
                split_x(b, 2)
                split_x(b, 3)
                for t in range(RT):
                    inverse_deviation(b, t)
                    if t in (1, 4):
                        rotate_local(b, t // 4)
                for tt in range(LT):
                    for p in range(8):
                        normalise(b, tt, p)
                        if tt and p == 5:
                            inverse_deviation(b, TILES - 2)
                inverse_deviation(b, TILES - 1)

        @block.scalar
        def _(act):
            prime(act, xs_hi_s, krot_sem, v_hi_s, kp_s, kt_hi_s, vb_hi_s, m_s, vwo_hi_s, exp_s, pt_hi_s, x1t_s,
                  qsem_s, lcopy, qt_hi_s, lexp, tp_hi_s, o_hi_s, normed)
            for c in range(DC):
                act.dma_start(wq_raw[c], io["wq"][:, c, :]).then_inc(wq_in[c], 16)
            act.wait_ge(ls_in, 16)
            act.activation(scales[:, :], scales[:, :], ACT.Exp).then_inc(scale_exp, 1)

            def round_wo(c):
                act.wait_ge(wo_in[c], 16)
                act.activation(wo_hi[:, c, :], wo_raw[c], ACT.Copy).then_inc(wo_hi_s, 1)

            for c in range(DC):
                round_wo(c)
                if c == 2:
                    act.wait_ge(wqs_in, 16)
                    act.wait_ge(scale_done, 1)
                    for k in range(DC):
                        act.activation(wqs[:, k, :], wqs[:, k, :], ACT.Identity, scale=scales[:, H + k:H + k + 1]).then_inc(wqs_scaled, 1)
                act.wait_ge(wq_scaled, 3 * c + 3)
                act.activation(wq_hi[:, c, :], wq_raw[c], ACT.Copy).then_inc(wq_hi_s, 1)
            for c in range(DC, 8):
                round_wo(c)

            def split_x(b, n):
                act.wait_ge(*xt_in.now(b, 16))
                if n < 2:
                    act.wait_ge(*(ls_ps.last(b, 8 * LT) if n == 0 else qp_ps.last(b, 2 * LT)))
                else:
                    act.wait_ge(*qg_ps.now(b, n - 1))
                act.activation(xs_hi[:, n % 2, :, :], xt[:, :, n * QB:(n + 1) * QB], ACT.Copy).then_inc(xs_hi_s.sem, 1)

            def pooled_hi(b, t):
                act.wait_ge(*pt_ps.now(b, t + 1))
                act.wait_ge(*(out_ps.now(b, t) if t else out_ps.last(b, TILES)))
                act.activation(pt_hi[:, :, :], mid[0:HK, 1 if t < RT else 0, 0:2 * P].rearrange("p (a q) -> p a q", a=2), ACT.Copy).then_inc(pt_hi_s.sem, 1)

            def scale_x1(b, t):
                act.wait_ge(*rstd_s.now(b, 2 * t + 2))
                act.activation(x1[:, t % 2, :], x1[:, t % 2, :], ACT.Identity, bias=rstd[:, t % 2, 1:2],
                               scale=rstd[:, t % 2, 0:1]).then_inc(normed.sem, 1)

            def x1t_copy(b, t):
                act.wait_ge(*x1t_ps.now(b, t + 1))
                act.wait_ge(*(x1t_out[t % 2].now(b, 16 * (t // 2)) if t >= 2 else x1t_out[t % 2].last(b, 16 * (TILES // 2))))
                act.activation(x1t[:, t % 2, :], x1t_bank(t), ACT.Copy).then_inc(x1t_s.sem, 1)

            def plain_queries(b, tt):
                act.wait_ge(*qp_ps.now(b, 2 * tt + 1))
                act.wait_ge(*(qt_ps.now(b, tt) if tt else ktr_ps.now(b, 1)))
                for a in range(2):
                    i = act.activation(qrot[:, 4 * a:4 * a + 4, :, 0:DS].rearrange("p j s e -> p s j e"),
                                       big[:, 2, 256 * a:256 * a + 256].rearrange("p (s j e) -> p s j e", s=2, j=4), ACT.Copy)
                i.then_inc(qsem_s.sem, 1)

            def rotary_queries(b, tt):
                act.wait_ge(*qp_ps.now(b, 2 * tt + 2))
                act.wait_ge(*(lrope.now(b, 6) if tt else qrope.now(b, 6 * RB)))
                act.activation(q_rot, big[:, 3, :], ACT.Copy).then_inc(lcopy.sem, 1)

            def transposed_queries(b, tt):
                act.wait_ge(*qt_ps.now(b, tt + 1))
                act.wait_ge(*out_ps.last(b, TILES))
                act.activation(q_hi[tt], flat(big[:, 2 * tt:2 * tt + 2, :]).rearrange("p (c q) -> p c q", q=P), ACT.Copy).then_inc(qt_hi_s.sem, 1)

            with act.Fori(0, B) as b:
                split_x(b, 0)
                split_x(b, 1)
                act.wait_ge(*kv_ps.now(b, 2))
                act.wait_ge(*klt_ps.last(b, 1))
                act.wait_ge(*pv_ps.last(b, sum(NPT)))
                act.wait_ge(wo_lo_s, 8)
                act.activation(krot[:, :, :, 0:DS], big[:, 2:4, 128:256].rearrange("p t (g e) -> p t g e", g=HKV), ACT.Copy).then_inc(krot_sem.sem, 1)
                act.activation(v_hi[:, :, :], big[:, 2:4, 256:512], ACT.Copy).then_inc(v_hi_s.sem, 1)
                act.wait_ge(*kp_ps.now(b, 1))
                act.wait_ge(*ktr_ps.last(b, 1))
                act.activation(kp[:, 128:512], acc[0:NK, 128:512], ACT.Copy).then_inc(kp_s.sem, 1)
                act.activation(kp[0:NB, 0:128], acc[0:NB, 0:128], ACT.Copy).then_inc(kp_s.sem, 1)
                act.wait_ge(*klt_ps.now(b, 1))
                act.wait_ge(*ls_ps.last(b, 8 * LT))
                for s in range(2):
                    r = slice(64 * s, 64 * s + 64)
                    i = act.activation(kt_hi[r, :, s, NB:KEYS], mid[r, 1, :].rearrange("p (a k) -> p a k", a=2), ACT.Copy)
                i.then_inc(kt_hi_s.sem, 1)
                act.wait_ge(*ktr_ps.now(b, 1))
                for s in range(2):
                    r = slice(64 * s, 64 * s + 64)
                    i = act.activation(kt_hi[r, :, s, 0:NB], tr[r, 160:192].rearrange("p (a k) -> p a k", a=2)[:, :, 0:NB], ACT.Copy)
                i.then_inc(kt_hi_s.sem, 1)
                split_x(b, 2)
                act.wait_ge(*vbd_s.now(b, 2))
                act.activation(vb_hi, vbd, ACT.Copy).then_inc(vb_hi_s.sem, 1)
                act.wait_ge(*m_ps.now(b, 1))
                act.activation(m_sb[:, :, :].rearrange("p (u v) n -> p u (v n)", u=2), mid[:, :, 0:2 * H * NB], ACT.Copy).then_inc(m_s.sem, 1)
                for a in range(2):
                    act.wait_ge(*vwo_ps.now(b, a + 1))
                    act.activation(vwo_hi[:, a, :], (acc, tr)[a][0:HK, :], ACT.Copy).then_inc(vwo_hi_s.sem, 1)
                split_x(b, 3)
                for t in range(RT + 2):
                    if t == 6:
                        transposed_queries(b, 0)
                    if t >= 3:
                        scale_x1(b, t - 3)
                    if t < RT:
                        act.wait_ge(*shifted.now(b, 2 * t + 2))
                        act.activation(pr[:, t % 2, :, 0:NB], sm[:, t % 2, :].rearrange("p (h k) -> p h k", h=H), ACT.Exp).then_inc(exp_s.sem, 1)
                    if 1 <= t <= RT:
                        pooled_hi(b, t - 1)
                    if t == 2 or t == 6:
                        plain_queries(b, t // 4)
                    if t == 3 or t == 6:
                        rotary_queries(b, t // 6)
                    if 3 <= t <= RT:
                        x1t_copy(b, t - 3)
                for i in range(ROUNDS):
                    if i >= 2:
                        for n in BLOCKS[i - 2]:
                            act.wait_ge(*tp_ps.now(b, n + 1))
                            act.wait_ge(*(pv_ps.now(b, n - 1) if n >= 2 else vwo_ps.now(b, 2)))
                            act.activation(tp_hi[:, n % 2, :], mid[:, n % 2, :], ACT.Copy).then_inc(tp_hi_s.sem, 1)
                    if i in (5, 9):
                        pooled_hi(b, RT + i // 9)
                    if i < GROUPS:
                        tt, g = divmod(i, HKV)
                        keys = NB + P * (tt + 1)
                        if tt:
                            act.wait_ge(*tp_ps.now(b, g + 1))
                        for p in (2 * g, 2 * g + 1):
                            act.wait_ge(*lmax.now(b, 8 * tt + p + 1))
                            for h in (2 * p, 2 * p + 1):
                                j = act.activation(probs_l[:, h, 0:keys], pair_scores(tt, p)[:, h % 2, 0:keys], ACT.Exp,
                                                   bias=stat[:, tt, 0, h:h + 1], accum_out=stat[:, tt, 1, h:h + 1])
                            j.then_inc(lexp.sem, 1)
                    if i == 0:
                        x1t_copy(b, RT - 2)
                        scale_x1(b, RT - 1)
                    if i == 1:
                        transposed_queries(b, 1)
                        x1t_copy(b, RT - 1)
                    if i == 7:
                        scale_x1(b, TILES - 2)
                    if i >= 2:
                        tt, g = divmod(i - 2, HKV)
                        act.wait_ge(*pv_ps.now(b, BLOCKS[i - 2][-1] + 1))
                        if tt == 1:
                            act.wait_ge(*out_ps.now(b, RT + 1))
                        r, c = slice(64 * (g % 2), 64 * (g % 2) + 64), 4 * (g // 2)
                        act.activation(qo_hi[r, c:c + 4, :].rearrange("p j q -> p (j q)"), tr[r, :], ACT.Copy).then_inc(o_hi_s.sem, 1)
                    if i == 9:
                        x1t_copy(b, TILES - 2)
                scale_x1(b, TILES - 1)
                x1t_copy(b, TILES - 1)

        @block.vector
        def _(dve):
            prime(dve, xsum, xpool_s, krope, v_lo_s, kr_s, kt_lo_s, bd_s, vbd_s, vb_lo_s, vwo_lo_s, qrope,
                  masked, shifted, summed, probs_s, pt_lo_s, added, bn_s, qt_lo_s, lmasked, lmax,
                  lrecip, tp_lo_s, o_lo_s)
            dve.wait_ge(scale_exp, 1)
            dve.tensor_scalar(scales[:, :], scales[:, :], float(DS) ** -0.5, None, ALU.mult).then_inc(scale_done, 1)
            dve.wait_ge(scale_done, 1)
            dve.memset(pr[:, :, :, :], 0.0)
            for k in (kt_hi, kt_lo):
                for s in range(2):
                    i = dve.memset(k[64 * (1 - s):64 * (1 - s) + 64, :, s, :].bitcast(F32), 0.0)
            i.then_inc(zeroed, 1)

            def lower_wq(c):
                dve.wait_ge(wq_hi_s, c + 1)
                dve.tensor_tensor(wq_lo[:, c, :], wq_raw[c], wq_hi[:, c, :].bitcast(F32), ALU.subtract).then_inc(wq_lo_s, 1)

            for c in range(DC):
                dve.wait_ge(wq_in[c], 16)
                for c0, c1, w in ((0, 512, DS), (512, 768, HALF), (768, 1024, HALF)):
                    v = wq_raw[c][:, c0:c1].rearrange("p (h e) -> p h e", h=H)
                    dve.tensor_tensor(v, v, bc(scales[:, 0:H], 2, w), ALU.mult).then_inc(wq_scaled, 1)
                if c:
                    lower_wq(c - 1)
            lower_wq(DC - 1)
            dve.wait_ge(zeroed, 1)
            dve.wait_ge(tab_in, 16 * 5)

            def pooled_lo(b, t):
                dve.wait_ge(*pt_hi_s.now(b, t + 1))
                dve.tensor_tensor(pt_lo[:, :, :], mid[0:HK, 1 if t < RT else 0, 0:2 * P].rearrange("p (a q) -> p a q", a=2),
                                  pt_hi[:, :, :].bitcast(F32), ALU.subtract).then_inc(pt_lo_s.sem, 1)

            def rotate(b, sig, k, in1, in2, cos, sin, out1, out2, u, v):
                dve.tensor_tensor(u, in1, cos, ALU.mult).then_inc(sig.sem, 1)
                dve.tensor_tensor(v, in2, sin, ALU.mult).then_inc(sig.sem, 1)
                dve.wait_ge(*sig.now(b, k + 2))
                dve.tensor_tensor(out1, u, v, ALU.subtract).then_inc(sig.sem, 1)
                dve.wait_ge(*sig.now(b, k + 3))
                dve.tensor_tensor(u, in2, cos, ALU.mult).then_inc(sig.sem, 1)
                dve.tensor_tensor(v, in1, sin, ALU.mult).then_inc(sig.sem, 1)
                dve.wait_ge(*sig.now(b, k + 5))
                dve.tensor_tensor(out2, u, v, ALU.add).then_inc(sig.sem, 1)

            def residual(b, t):
                dve.wait_ge(*out_ps.now(b, t + 1))
                dve.wait_ge(*xn_in[t % 2].now(b, 16 * (t // 2 + 1)))
                dve.wait_ge(*(x1_out[t % 2].now(b, 16 * (t // 2)) if t >= 2 else x1_out[t % 2].last(b, 16 * (TILES // 2))))
                dve.wait_ge(*(x1t_ps.now(b, t - 1) if t >= 2 else x1t_ps.last(b, TILES - 1 + t)))
                dve.tensor_tensor(x1[:, t % 2, :], acc[:, :], xn[:, t % 2, :], ALU.add).then_inc(added.sem, 1)
                dve.wait_ge(*added.now(b, t + 1))
                dve.bn_stats(bn[:, t % 2, :], x1[:, t % 2, :]).then_inc(bn_s.sem, 1)
                dve.wait_ge(*bn_s.now(b, 2 * t + 1))
                dve.sem_inc(dve_past, 1)
                dve.bn_aggr(mv[:, t % 2, :], bn[:, t % 2, :]).then_inc(bn_s.sem, 1)

            with dve.Fori(0, B) as b:
                dve.wait_ge(*xt_in.now(b, 16))
                dve.wait_ge(*kp_ps.last(b, 1))
                for c, (c0, c1, n) in enumerate(((0, REMOTE, NB), (REMOTE, T, 1))):
                    dve.tensor_reduce(xpool[:, :, NB * c:NB * c + n], xt[:, :, c0:c1].rearrange("p c (n m) -> p c n m", n=n),
                                      AX.X, ALU.add).then_inc(xsum.sem, 1)
                dve.wait_ge(*xsum.now(b, 2))
                dve.tensor_scalar(xpool[:, :, 0:NB], xpool[:, :, 0:NB], 1.0 / MB, None, ALU.mult).then_inc(xpool_s.sem, 1)
                dve.wait_ge(*kgeo_ps.now(b, 1))
                r6 = lambda c: qf[:, 0:RT * P].rearrange("p (t e) -> p t e", t=RT)[:, :, c:c + 64].rearrange("p t (g f) -> p t g f", g=HKV)
                o6 = lambda c: kgr[:, :, c:c + 64].rearrange("p t (g f) -> p t g f", g=HKV)
                u6 = lambda t: t[:, 0:RT * 64].rearrange("p (t g f) -> p t g f", t=RT, g=HKV)
                rotate(b, krope, 0, r6(0), r6(64), bc(rope[:, 0:RT, 0, :], 2, HKV), bc(rope[:, 0:RT, 1, :], 2, HKV),
                       o6(0), o6(64), u6(kt1), u6(kt2))
                dve.wait_ge(*v_hi_s.now(b, 1))
                dve.wait_ge(*krope.now(b, 6))
                r2 = lambda c: big[:, 2:4, c:c + 64].rearrange("p t (g f) -> p t g f", g=HKV)
                u2 = lambda t: t[:, 0:LT * 64].rearrange("p (t g f) -> p t g f", t=LT, g=HKV)
                rotate(b, krope, 6, r2(0), r2(64), bc(rope[:, RT:TILES, 0, :], 2, HKV), bc(rope[:, RT:TILES, 1, :], 2, HKV),
                       krot[:, :, :, DS:DS + HALF], krot[:, :, :, DS + HALF:DS + DG], u2(kt1), u2(kt2))
                dve.tensor_tensor(v_lo[:, :, :], big[:, 2:4, 256:512], v_hi[:, :, :].bitcast(F32), ALU.subtract).then_inc(v_lo_s.sem, 1)
                dve.wait_ge(wo_lo_s, 8)
                dve.wait_ge(*kp_s.now(b, 2))
                for c in range(2):
                    dve.tensor_copy(kr[0:NB, 256 * c:256 * c + 256].rearrange("k (g r f) -> k g r f", g=HKV, r=REP),
                                    bc(kp[0:NB, 64 * c:64 * c + 64].rearrange("k (g f) -> k g f", g=HKV), 2, REP)).then_inc(kr_s.sem, 1)
                dve.tensor_copy(kr[0:NB, 512:1024].rearrange("k (g r f) -> k g r f", g=HKV, r=REP),
                                bc(kp[0:NB, 128:256].rearrange("k (g f) -> k g f", g=HKV), 2, REP)).then_inc(kr_s.sem, 1)
                by_head = kr_by_head[0:NB, :].rearrange("k (g e) -> k g e", g=HKV)
                for e0, w, c0 in ((0, DS, 128), (DS, HALF, 0), (DS + HALF, HALF, 64)):
                    dve.tensor_copy(by_head[:, :, e0:e0 + w], kp[0:NB, c0:c0 + HKV * w].rearrange("k (g f) -> k g f", g=HKV)).then_inc(kr_s.sem, 1)
                dve.memset(vbd, 0.0).then_inc(zeroed, 1)
                dve.wait_ge(*kt_hi_s.now(b, 1))
                for s in range(2):
                    r = slice(64 * s, 64 * s + 64)
                    i = dve.tensor_tensor(kt_lo[r, :, s, NB:KEYS], mid[r, 1, :].rearrange("p (a k) -> p a k", a=2),
                                          kt_hi[r, :, s, NB:KEYS].bitcast(F32), ALU.subtract)
                i.then_inc(kt_lo_s.sem, 1)

                def rotate_queries(n):
                    dve.wait_ge(*qg_ps.now(b, n + 1))
                    if n:
                        dve.wait_ge(*qrope.now(b, 6 * n))
                    if n == 2:
                        dve.wait_ge(*vb_lo_s.now(b, 1))
                    f = lambda v: v.rearrange("p (a q) -> p a q", a=2)
                    rotate(b, qrope, 6 * n, f(big[:, 2 * (n % 2), :]), f(big[:, 2 * (n % 2) + 1, :]),
                           bc(cos_t[:, n * QB:(n + 1) * QB], 1, 2), bc(sin_t[:, n * QB:(n + 1) * QB], 1, 2),
                           f(q_rem[:, n, 0, :]), f(q_rem[:, n, 1, :]), f(rt1), f(rt2))

                dve.wait_ge(*kt_hi_s.now(b, 2))
                slots = tr[:, 0:192].rearrange("p (s k) -> p s k", k=16)
                dve.tensor_tensor(kg_bd[:, :, :].rearrange("p c (h k) -> p c h k", h=8), bc(slots[:, 0:4, 0:NB], 2, 8),
                                  bc(own_geo, 1, 4), ALU.mult).then_inc(bd_s.sem, 1)
                dve.tensor_tensor(ks_bd[:, :, :].rearrange("p c (h k) -> p c h k", h=4), bc(slots[:, 4:8, 0:NB], 2, 4),
                                  bc(own_sem, 1, 4), ALU.mult).then_inc(bd_s.sem, 1)
                dve.wait_ge(zeroed, b + 2)
                for a in range(2):
                    for s in range(2):
                        i = dve.tensor_tensor(own_columns(a, s), bc(slots[:, 8 + a, 0:NK], 1, 4), bc(own_v[:, s, :], 1, 4), ALU.mult)
                    i.then_inc(vbd_s.sem, 1)
                for s in range(2):
                    r = slice(64 * s, 64 * s + 64)
                    i = dve.tensor_tensor(kt_lo[r, :, s, 0:NB], tr[r, 160:192].rearrange("p (a k) -> p a k", a=2)[:, :, 0:NB],
                                          kt_hi[r, :, s, 0:NB].bitcast(F32), ALU.subtract)
                i.then_inc(kt_lo_s.sem, 1)
                dve.wait_ge(*vb_hi_s.now(b, 1))
                dve.tensor_tensor(vb_lo, vbd, vb_hi.bitcast(F32), ALU.subtract).then_inc(vb_lo_s.sem, 1)
                rotate_queries(0)
                rotate_queries(1)
                for a in range(2):
                    dve.wait_ge(*vwo_hi_s.now(b, a + 1))
                    dve.tensor_tensor(vwo_lo[:, a, :], (acc, tr)[a][0:HK, :], vwo_hi[:, a, :].bitcast(F32), ALU.subtract).then_inc(vwo_lo_s.sem, 1)

                def softmax_in(t):
                    s3 = sm[:, t % 2, :].rearrange("p (h k) -> p h k", h=H)
                    s_in = mid[:, 0, 0:H * NB].rearrange("p (h k) -> p h k", h=H)
                    dve.wait_ge(*s_ps.now(b, t + 1))
                    dve.wait_ge(*(exp_s.now(b, t - 1) if t >= 2 else exp_s.last(b, RT)))
                    if t == 0:
                        dve.tensor_tensor(s3, s_in, bc(keep[:, t, :], 1, H), ALU.mult).then_inc(masked.sem, 1)
                        dve.wait_ge(*masked.now(b, 1))
                        s_in = s3
                    dve.tensor_tensor(s3, s_in, bc(hide[:, t, :], 1, H), ALU.add).then_inc(masked.sem, 1)
                    dve.wait_ge(*masked.now(b, t + 2))
                    dve.tensor_reduce(stat[:, t % 2, 0, :], s3, AX.X, ALU.max).then_inc(shifted.sem, 1)
                    dve.wait_ge(*shifted.now(b, 2 * t + 1))
                    dve.wait_ge(*(pt_ps.now(b, t - 1) if t >= 2 else pt_ps.last(b, TILES - 1 + t)))
                    dve.tensor_tensor(s3, s3, bc(stat[:, t % 2, 0, :], 2, NB), ALU.subtract).then_inc(shifted.sem, 1)

                def softmax_out(t):
                    p3 = pr[:, t % 2, :, 0:NB]
                    dve.wait_ge(*exp_s.now(b, t + 1))
                    dve.tensor_reduce(stat[:, t % 2, 1, :], p3, AX.X, ALU.add).then_inc(summed.sem, 1)
                    total = stat[:, t % 2, 1, :]
                    dve.wait_ge(*summed.now(b, 2 * t + 1 + (t > 0)))
                    if t == 0:
                        total = stat[:, t % 2, 2, :]
                        dve.tensor_scalar(total, stat[:, t % 2, 1, :], spread[:, t:t + 1], None, ALU.mult).then_inc(summed.sem, 1)
                        dve.wait_ge(*summed.now(b, 2))
                    dve.reciprocal(stat[:, t % 2, 3, :], total).then_inc(summed.sem, 1)
                    dve.wait_ge(*summed.now(b, 2 * t + 3))
                    if t in (0, 2):
                        dve.tensor_copy(pr[:, t % 2, :, NB:NK], bc(rest_p[:, t:t + 1], 1, H))
                    dve.tensor_tensor(p3, p3, bc(stat[:, t % 2, 3, :], 2, NB), ALU.mult).then_inc(probs_s.sem, 1)

                def transposed_queries(tt):
                    dve.wait_ge(*qt_hi_s.now(b, tt + 1))
                    dve.tensor_tensor(q_lo[tt], flat(big[:, 2 * tt:2 * tt + 2, :]).rearrange("p (c q) -> p c q", q=P), q_hi[tt].bitcast(F32),
                                      ALU.subtract).then_inc(qt_lo_s.sem, 1)

                for t in range(RT + 2):
                    if t < RT:
                        softmax_in(t)
                    if t == 6:
                        transposed_queries(0)
                    if 1 <= t <= RT:
                        pooled_lo(b, t - 1)
                    if t < RT:
                        softmax_out(t)
                    if t == 1:
                        rotate_queries(2)
                    if 2 <= t <= RT:
                        residual(b, t - 2)
                for i in range(ROUNDS):
                    if i >= 2:
                        for n in BLOCKS[i - 2]:
                            dve.wait_ge(*tp_hi_s.now(b, n + 1))
                            dve.tensor_tensor(tp_lo[:, n % 2, :], mid[:, n % 2, :], tp_hi[:, n % 2, :].bitcast(F32), ALU.subtract).then_inc(tp_lo_s.sem, 1)
                    if i in (5, 9):
                        pooled_lo(b, RT + i // 9)
                    if i < GROUPS:
                        tt, g = divmod(i, HKV)
                        keys = NB + P * (tt + 1)
                        for p in (2 * g, 2 * g + 1):
                            dve.wait_ge(*ls_ps.now(b, 8 * tt + p + 1))
                            pair = pair_scores(tt, p)
                            dve.tensor_tensor(pair[:, :, keys - P:keys], pair[:, :, keys - P:keys], bc(causal, 1, 2), ALU.add).then_inc(lmasked.sem, 1)
                            dve.wait_ge(*lmasked.now(b, 8 * tt + p + 1))
                            dve.tensor_reduce(stat[:, tt, 0, 2 * p:2 * p + 2], pair[:, :, 0:keys], AX.X, ALU.max, negate=True).then_inc(lmax.sem, 1)
                        if i == 0:
                            residual(b, RT - 1)
                        for p in (2 * g, 2 * g + 1):
                            dve.wait_ge(*lexp.now(b, 8 * tt + p + 1))
                            dve.reciprocal(stat[:, tt, 3, 2 * p:2 * p + 2], stat[:, tt, 1, 2 * p:2 * p + 2]).then_inc(lrecip.sem, 1)
                    if i == 1:
                        transposed_queries(1)
                    if i == 6:
                        residual(b, TILES - 2)
                    if i >= 2:
                        tt, g = divmod(i - 2, HKV)
                        dve.wait_ge(*o_hi_s.now(b, i - 1))
                        r, c = slice(64 * (g % 2), 64 * (g % 2) + 64), 4 * (g // 2)
                        v = lambda q: q[r, c:c + 4, :].rearrange("p j q -> p (j q)")
                        dve.tensor_tensor(v(qo_lo), tr[r, :], v(qo_hi).bitcast(F32), ALU.subtract).then_inc(o_lo_s.sem, 1)
                residual(b, TILES - 1)

        @block.tensor
        def _(pe):
            prime(pe, kgeo_ps, kv_ps, kp_ps, ktr_ps, klt_ps, m_ps, vwo_ps, qg_ps, s_ps, pt_ps, out_ps, x1t_ps, qp_ps,
                  qt_ps, ls_ps, tp_ps, pv_ps)
            pe.wait_ge(wkv_in, 16)

            def transpose_probs(b, t):
                if t < RT:
                    pe.wait_ge(*probs_s.now(b, t + 1))
                    if t:
                        pe.wait_ge(*pt_lo_s.now(b, t))
                else:
                    pe.wait_ge(*lnorm.now(b, 8 * (t - RT + 1)))
                    last = BLOCKS[HKV * (t - RT + 1) - 1][-1]
                    pe.wait_ge(*tp_lo_s.now(b, last - last % 2 + 1))
                p = pr[:, t % 2, :, :].rearrange("p (a h) k -> p a (h k)", a=2)
                for a in range(2):
                    i = pe.transpose(mid[0:HK, 1 if t < RT else 0, P * a:P * a + P], p[:, a, :], ident[:, :])
                i.then_inc(pt_ps.sem, 1)

            def attend_pooled(b, t, first, last):
                pe.wait_ge(*pt_lo_s.now(b, t + 1))
                if first:
                    pe.wait_ge(*(added.now(b, t) if t else vwo_lo_s.now(b, 2)))
                for a in range(2):
                    i = three_passes(pe, acc[:, :], pt_hi[:, a, :], pt_lo[:, a, :], vwo_hi[:, a, :], vwo_lo[:, a, :],
                                     first and a == 0, last and a == 1)
                return i

            def transpose_x1(b, t):
                pe.wait_ge(*normed.now(b, t + 1))
                if t == 0:
                    pe.wait_ge(*vwo_lo_s.now(b, 2))
                elif t < RT:
                    pe.wait_ge(*x1t_s.now(b, t))
                elif t == RT:
                    pe.wait_ge(*lexp.now(b, 8 * LT - 1))
                for c in range(DC):
                    i = pe.transpose(x1t_bank(t)[:, P * c:P * c + P], x1[:, t % 2, P * c:P * c + P], ident[:, :])
                i.then_inc(x1t_ps.sem, 1)

            def project_local(b, tt, s):
                pe.wait_ge(*xs_lo_s.now(b, RB + 1))
                if s == 0:
                    if tt:
                        pe.wait_ge(*qsem_s.now(b, 1))
                        pe.wait_ge(*lcopy.now(b, 1))
                    else:
                        pe.wait_ge(*qrope.now(b, 12))
                for c in range(DC):
                    k = slice(P * tt, P * tt + P)
                    i = three_passes(pe, big[:, 2 + s, :], xs_hi[:, 1, c, k], xs_lo[:, 1, c, k],
                                     wq_hi[:, c, 512 * s:512 * s + 512], wq_lo[:, c, 512 * s:512 * s + 512], c == 0, c == DC - 1)
                i.then_inc(qp_ps.sem, 1)

            def transpose_queries(b, tt):
                pe.wait_ge(*qsem_s.now(b, tt + 1))
                pe.wait_ge(*lrope.now(b, 6 * tt + 6))
                if tt == 0:
                    pe.wait_ge(*qrope.now(b, 6 * RB))
                for c in range(8):
                    i = pe.transpose(big[:, 2 * tt + c // 4, P * (c % 4):P * (c % 4) + P], qrot[:, c, :, :].rearrange("p s e -> p (s e)"), ident[:, :])
                i.then_inc(qt_ps.sem, 1)

            def output(b, t, part):
                if part == 0:
                    pe.wait_ge(*added.now(b, t))
                else:
                    attend_pooled(b, t, False, False)
                pe.wait_ge(*o_lo_s.now(b, HKV * (t - RT) + 2 * part + 2))
                for c in range(4 * part, 4 * part + 4):
                    i = three_passes(pe, acc[:, :], qo_hi[:, c, :], qo_lo[:, c, :], wo_hi[:, c, :], wo_lo[:, c, :], c == 0, c == 7)
                if part:
                    i.then_inc(out_ps.sem, 1)

            def rotary_keys(b):
                pe.wait_ge(*xt_in.now(b, 16))
                pe.wait_ge(*lexp.last(b, 8 * LT))
                for t in range(RT):
                    for c in range(DC):
                        i = pe.matmul(qf[:, P * t:P * t + P], xt[:, c, P * t:P * t + P], wkv[:, c, 0:128],
                                      start=(c == 0), stop=(c == DC - 1))
                i.then_inc(kgeo_ps.sem, 1)

            def local_keys(b):
                pe.wait_ge(*x1t_s.last(b, TILES - 1))
                for t in range(LT):
                    for c in range(DC):
                        i = pe.matmul(big[:, 2 + t, :], xt[:, c, REMOTE + P * t:REMOTE + P * t + P], wkv[:, c, :],
                                      start=(c == 0), stop=(c == DC - 1))
                    i.then_inc(kv_ps.sem, 1)

            def batch(b, more):
                pe.wait_ge(tab_in, 16 * 5)
                pe.wait_ge(*xpool_s.now(b, 1))
                pe.wait_ge(*added.last(b, TILES))
                for c in range(DC):
                    pe.matmul(acc[0:NK, 128:512], xpool[:, c, :], wkv[:, c, 128:512], start=(c == 0), stop=(c == DC - 1))
                pe.wait_ge(*krope.now(b, 6))
                for t in range(RT):
                    i = pe.matmul(acc[0:NB, 0:128], pool_w[:, t, :], kgr[:, t, :], start=(t == 0), stop=(t == RT - 1))
                i.then_inc(kp_ps.sem, 1)

                def project_geo(n):
                    pe.wait_ge(wq_lo_s, DC)
                    pe.wait_ge(*xs_lo_s.now(b, n + 1))
                    if n == 1:
                        pe.wait_ge(*v_lo_s.now(b, 1))
                    elif n == 2:
                        pe.wait_ge(*qrope.now(b, 6))
                    for r in range(2):
                        for a in range(2):
                            for c in range(DC):
                                w = slice(512 + 256 * r + 128 * a, 512 + 256 * r + 128 * a + 128)
                                i = three_passes(pe, big[:, 2 * (n % 2) + r, QB * a:QB * a + QB], wq_hi[:, c, w], wq_lo[:, c, w],
                                                 xs_hi[:, n % 2, c, :], xs_lo[:, n % 2, c, :], c == 0, c == DC - 1)
                    i.then_inc(qg_ps.sem, 1)

                project_geo(0)
                pe.wait_ge(*krot_sem.now(b, 1))
                pe.wait_ge(*krope.now(b, 12))
                pe.wait_ge(*pt_lo_s.last(b, TILES))
                for a in range(2):
                    for t in range(LT):
                        i = pe.transpose(mid[:, 1, 256 * a + P * t:256 * a + P * t + P],
                                         krot[:, t, 2 * a:2 * a + 2, :].rearrange("p g e -> p (g e)"), ident[:, :])
                i.then_inc(klt_ps.sem, 1)
                pe.wait_ge(*kr_s.now(b, 6))
                pe.wait_ge(*o_lo_s.last(b, HKV * LT))
                pe.wait_ge(*x1t_s.last(b, TILES))
                pe.sem_inc(pe_past, 1)
                for s in range(8):
                    pe.transpose(tr[:, 16 * s:16 * s + NB], kr[0:NB, P * s:P * s + P], ident[0:NB, 0:NB])
                for a in range(2):
                    pe.transpose(tr[:, 16 * (8 + a):16 * (8 + a) + NK], kp[:, 256 + P * a:256 + P * a + P], ident[0:NK, 0:NK])
                for a in range(2):
                    i = pe.transpose(tr[:, 16 * (10 + a):16 * (10 + a) + NB], kr_by_head[0:NB, P * a:P * a + P], ident[0:NB, 0:NB])
                i.then_inc(ktr_ps.sem, 1)
                project_geo(1)
                pe.wait_ge(wqs_scaled, DC)
                pe.wait_ge(*bd_s.now(b, 2))
                pe.wait_ge(*kt_lo_s.now(b, 1))
                for c in range(DC):
                    for g in range(HKV):
                        i = pe.matmul(mid[:, c // 2, H * NB * (c % 2) + 4 * NB * g:H * NB * (c % 2) + 4 * NB * (g + 1)],
                                      wqs[:, g, P * c:P * c + P], ks_bd[:, g, :], start=True, stop=True)
                i.then_inc(m_ps.sem, 1)
                pe.wait_ge(wo_lo_s, 8)
                pe.wait_ge(*vb_lo_s.now(b, 1))
                pe.wait_ge(*kt_lo_s.now(b, 2))
                for a in range(2):
                    for j in range(4):
                        o = (4 * a + j) * HK
                        i = three_passes(pe, (acc, tr)[a][0:HK, :], vb_hi[:, o:o + HK], vb_lo[:, o:o + HK],
                                         wo_hi[:, 4 * a + j, :], wo_lo[:, 4 * a + j, :], j == 0, j == 3)
                    i.then_inc(vwo_ps.sem, 1)

                def scores(t):
                    pe.wait_ge(*qrope.now(b, 6 * (t // 2 + 1)))
                    if t == 0:
                        pe.wait_ge(*m_s.now(b, 1))
                    else:
                        pe.wait_ge(*masked.now(b, t + 1))
                    plain = lambda c: pe.matmul(mid[:, 0, 0:H * NB], xt[:, c, P * t:P * t + P], m_sb[:, c, :],
                                                start=(c == 0), stop=(c == DC - 1))
                    for c in range(DC - 1):
                        plain(c)
                    for a in range(2):
                        for r in range(2):
                            q = q_rem[:, t // 2, r, QB * a + P * (t % 2):QB * a + P * (t % 2) + P]
                            pe.matmul(mid[:, 0, HB * a:HB * a + HB], q, kg_bd[:, 2 * r + a, :],
                                      start=False, stop=False, skip_group_check=True)
                    plain(DC - 1).then_inc(s_ps.sem, 1)

                def local_scores(i):
                    tt, g = divmod(i, HKV)
                    keys = NB + P * (tt + 1)
                    pe.wait_ge(*qt_lo_s.now(b, tt + 1))
                    for p in (2 * g, 2 * g + 1):
                        if tt or p >= 2:
                            pe.wait_ge(*lexp.now(b, 8 * tt + p - 1))
                        for h in (2 * p, 2 * p + 1):
                            a, s, j = h // 8, h // 4 % 2, h % 4
                            i = three_passes(pe, pair_scores(tt, p)[:, h % 2, 0:keys], q_hi[tt][:, 4 * a + j, :], q_lo[tt][:, 4 * a + j, :],
                                             kt_hi[:, a, s, 0:keys], kt_lo[:, a, s, 0:keys], True, True)
                        i.then_inc(ls_ps.sem, 1)

                for t in range(RT + 2):
                    if t < RT:
                        scores(t)
                    if t == 0:
                        project_geo(2)
                    if t == RT + 1:
                        local_scores(0)
                    if t >= 2:
                        attend_pooled(b, t - 2, True, True).then_inc(out_ps.sem, 1)
                    if t == RT:
                        project_local(b, 1, 1)
                    if 1 <= t <= RT:
                        transpose_probs(b, t - 1)
                    if t in (1, 2):
                        project_local(b, 0, t - 1)
                    if t == RT - 1:
                        project_local(b, 1, 0)
                    if t == 5:
                        transpose_queries(b, 0)
                    if 3 <= t <= RT:
                        transpose_x1(b, t - 3)

                def local_transposes(i):
                    tt, g = divmod(i, HKV)
                    pe.wait_ge(*lnorm.now(b, 8 * tt + 2 * g + 2))
                    for k, n in enumerate(BLOCKS[i]):
                        if n >= 2:
                            pe.wait_ge(*tp_lo_s.now(b, n - 1))
                        if g == 0:
                            pe.wait_ge(*pt_lo_s.now(b, RT + tt))
                        for h in range(4 * g, 4 * g + 4):
                            i = pe.transpose(mid[:, n % 2, P * (h % 4):P * (h % 4) + P], probs_l[:, h, NB + P * k:NB + P * k + P], ident[:, :])
                        i.then_inc(tp_ps.sem, 1)

                def local_values(i):
                    g = i % HKV
                    pe.wait_ge(*(o_lo_s.now(b, i) if i else x1t_s.now(b, RT)))
                    w = slice(P * (g // 2), P * (g // 2) + P)
                    for k, n in enumerate(BLOCKS[i]):
                        pe.wait_ge(*tp_lo_s.now(b, n + 1))
                        three_passes(pe, tr[:, :], v_hi[:, k, w], v_lo[:, k, w], tp_hi[:, n % 2, :], tp_lo[:, n % 2, :],
                                     k == 0, n == BLOCKS[i][-1]).then_inc(pv_ps.sem, 1)

                for i in range(ROUNDS):
                    if i >= 2:
                        local_transposes(i - 2)
                    if i == 5:
                        transpose_probs(b, RT)
                    if i == 0:
                        transpose_x1(b, RT - 2)
                    if 1 <= i < GROUPS:
                        local_scores(i)
                    if i == 1:
                        transpose_queries(b, 1)
                        transpose_x1(b, RT - 1)
                    if i == 6:
                        output(b, RT, 1)
                    if more and i == 8:
                        rotary_keys(b + 1)
                    if i in (4, 8):
                        output(b, RT + i // 8, 0)
                    if i == 9:
                        transpose_x1(b, RT)
                        transpose_probs(b, TILES - 1)
                    if i >= 2:
                        local_values(i - 2)
                output(b, TILES - 1, 1)
                if more:
                    local_keys(b + 1)
                transpose_x1(b, TILES - 1)

            rotary_keys(0)
            local_keys(0)
            with pe.Fori(0, B - 1) as b:
                batch(b, True)
            batch(B - 1, False)


def weights_block(nc, sems, io, x1t_dram, ctx):
    keep, _, _, _ = tools(nc, ctx, sems, "w")
    wg, wu, wd = keep("wg", [P, DC, INTER]), keep("wu", [P, DC, INTER]), keep("wd", [P, IC, D])
    ug_scale = keep("ug_scale", [P, 2, IC])
    xraw = keep("xraw", [P, FT, DC, P])
    inner = ExitStack()
    with inner:
        sb, ps, _, sem = tools(nc, inner, sems, "wp")
        had = sb("had", [P, 2, P])
        hr = sb("hr", [P, 2, P], F32R)
        su = sb("su", [P, DC])
        sd = sb("sd", [P, IC])
        dps = sb("dps", [P, D])
        stage, mixed = sb("stage", [P, 2, 4, 512]), sb("mixed", [P, 2, 4, 512])
        dn = sb("dn", [P, IC, D])
        hi, lo = sb("hi", [P, 2, 4, 512], F32R), sb("lo", [P, 2, 4, 512], F32R)
        out = ps("out", [P, 8, 512])
        had_in, hr_s, sc_in, sc_s, first_s = (sem(n) for n in ("had_in", "hr_s", "sc_in", "sc_s", "first_s"))
        outer_low, outer_s = sem("outer_low"), sem("outer_s")
        piece_in, mix_s, hi_s, lo_s, mm_s = [sem(f"piece_in{i}") for i in range(2)], sem("mix_s"), sem("hi_s"), sem("lo_s"), sem("mm_s")
        dn_in = [sem(f"dn_in{i}") for i in range(2)]
        ev_gu_s, ev_d_s, x_pre = sem("ev_gu_s"), sem("ev_d_s"), sem("x_pre")
        pieces = [("g", n) for n in range(4)] + [("u", n) for n in range(4)] + [("d", n) for n in range(4)]
        GU = 8
        block = inner.enter_context(nc.Block())

        @block.sync
        def _(sp):
            def load(i):
                if i >= 2:
                    sp.wait_ge(*((mix_s, i - 2) if i > 2 else (lo_s, 1)))
                m, n = pieces[i]
                sp.dma_start(stage[:, i % 2, :, :], io["wg" if m == "g" else "wu"][:, :, 512 * n:512 * n + 512]).then_inc(piece_in[i % 2], 16)

            def load_down(n):
                sp.dma_start(dn[:, 4 * n:4 * n + 4, :], io["wd"][:, 4 * n:4 * n + 4, :]).then_inc(dn_in[n % 2], 16)

            load(0)
            sp.dma_start(had[:, :, :], io["had"]).then_inc(had_in, 16)
            load(1)
            for t, n in ((su, "su"), (sd, "sd"), (dps, "dps"), (ug_scale, "ug_scale")):
                sp.dma_start(t[:], io[n]).then_inc(sc_in, 16)
            for n, i in ((0, 2), (2, 3), (1, 4), (3, 5)):
                load_down(n)
                load(i)
            load(6)
            load(7)
            sp.dma_start(xraw[:, :, :, :], x1t_dram[0]).then_inc(x_pre, 16)
            sp.wait_ge(x_pre, 16)

        @block.gpsimd
        def _(pool):
            for i in range(1, len(pieces)):
                if i < GU:
                    pool.wait_ge(piece_in[i % 2], 16 * (i // 2 + 1))
                    x = stage[:, i % 2, :, :]
                else:
                    pool.wait_ge(outer_s, i - GU + 1)
                    x = dn[:, 4 * (i - GU):4 * (i - GU) + 4, :]
                if i >= 3:
                    pool.wait_ge(lo_s, i - 1)
                pool.tensor_tensor(mixed[:, i % 2, 0:2, :], x[:, 0:2, :], x[:, 2:4, :], ALU.add)
                pool.tensor_tensor(mixed[:, i % 2, 2:4, :], x[:, 0:2, :], x[:, 2:4, :], ALU.subtract).then_inc(mix_s, 1)

        @block.scalar
        def _(act):
            act.wait_ge(had_in, 16)
            act.activation(hr[:, :, :], had[:, :, :], ACT.Copy).then_inc(hr_s, 1)

            def evacuate(i):
                m, n = pieces[i]
                for c in range(4):
                    act.wait_ge(mm_s, 4 * i + c + 1)
                    dst = (wg if m == "g" else wu)[:, c, 512 * n:512 * n + 512]
                    act.activation(dst, out[:, (4 * i + c) % 8, :], ACT.Identity, scale=su[:, c:c + 1]).then_inc(ev_gu_s, 1)

            act.wait_ge(piece_in[0], 16)
            for c in range(4):
                act.activation(hi[:, 0, c, :], stage[:, 0, c, :], ACT.Copy).then_inc(first_s, 1)
            act.wait_ge(sc_in, 64)
            for i in range(1, len(pieces)):
                act.wait_ge(mix_s, i)
                if i >= 2:
                    act.wait_ge(mm_s, 4 * (i - 1))
                act.activation(hi[:, i % 2, :, :], mixed[:, i % 2, :, :], ACT.Copy).then_inc(hi_s, 1)
                if i <= GU:
                    evacuate(i - 1)

        @block.vector
        def _(dve):
            for c in range(4):
                dve.wait_ge(first_s, c + 1)
                j = dve.tensor_tensor(lo[:, 0, c, :], stage[:, 0, c, :], hi[:, 0, c, :].bitcast(F32), ALU.subtract)
            j.then_inc(lo_s, 1)
            dve.wait_ge(sc_in, 64)
            dve.tensor_scalar(ug_scale[:, :, :], ug_scale[:, :, :], float(D) ** -0.5, None, ALU.mult).then_inc(sc_s, 1)
            dve.tensor_scalar(dps[:, :], dps[:, :], float(INTER) ** -0.5, None, ALU.mult).then_inc(sc_s, 1)

            def outer(k):
                v = lambda t, a: t[:, :, :].rearrange("p (g c) n -> p g (c n)", g=4)[:, a, :]
                if k in (0, 2):
                    dve.wait_ge(dn_in[k // 2], 32)
                if k == 4:
                    dve.wait_ge(outer_low, 1)
                src, dst = (dn, wd) if k < 4 else (wd, dn)
                x, y, d, op = (((0, 2, 0, ALU.add), (0, 2, 2, ALU.subtract), (1, 3, 1, ALU.add), (1, 3, 3, ALU.subtract))
                               if k < 4 else
                               ((0, 1, 0, ALU.add), (0, 1, 1, ALU.subtract), (2, 3, 2, ALU.add), (2, 3, 3, ALU.subtract)))[k % 4]
                i = dve.tensor_tensor(v(dst, d), v(src, x), v(src, y), op)
                if k == 3:
                    i.then_inc(outer_low, 1)
                if k >= 4:
                    i.then_inc(outer_s, 1)

            def evacuate(i):
                for c in range(4):
                    dve.wait_ge(mm_s, 4 * i + c + 1)
                    k = 4 * (i - GU) + c
                    dve.scalar_tensor_tensor(wd[:, k, :], out[:, (4 * i + c) % 8, :], sd[:, k:k + 1], dps[:, :], ALU.mult, ALU.mult).then_inc(ev_d_s, 1)

            dve.wait_ge(sc_s, 2)
            for i in range(1, len(pieces)):
                dve.wait_ge(hi_s, i)
                if i >= 2:
                    dve.wait_ge(mm_s, 4 * (i - 1))
                dve.tensor_tensor(lo[:, i % 2, :, :], mixed[:, i % 2, :, :], hi[:, i % 2, :, :].bitcast(F32), ALU.subtract).then_inc(lo_s, 1)
                for k in {2: (0,), 3: (1,), 4: (2,), 5: (3, 4), 6: (5,), 7: (6,), 8: (7,)}.get(i, ()):
                    outer(k)
                if i > GU:
                    evacuate(i - 1)
            evacuate(len(pieces) - 1)

        @block.tensor
        def _(pe):
            pe.wait_ge(hr_s, 1)
            for i in range(len(pieces)):
                pe.wait_ge(lo_s, i + 1)
                for c in range(4):
                    if i >= 2:
                        pe.wait_ge(*((ev_gu_s, 4 * (i - 2) + c + 1) if i - 2 < GU else (ev_d_s, 4 * (i - 2 - GU) + c + 1)))
                    bank = out[:, (4 * i + c) % 8, :]
                    chunks = ((c & 2), (c & 2) + 1) if i else range(4)
                    for s in chunks:
                        sign = bin(c & s & (1 if i else 3)).count("1") % 2
                        pe.matmul(bank, hr[:, sign, :], hi[:, i % 2, s, :], start=(s == chunks[0]), stop=False)
                        j = pe.matmul(bank, hr[:, sign, :], lo[:, i % 2, s, :], start=False, stop=(s == chunks[-1]))
                    j.then_inc(mm_s, 1)
    return wg, wu, wd, ug_scale, xraw


def ffn_block(nc, sems, x1_dram, x1t_dram, out_dram, wg, wu, wd, ug_scale, xraw):
    ctx = ExitStack()
    with ctx:
        sb, ps, signal, sem = tools(nc, ctx, sems, "ff")
        gu_hi = [sb(f"gu_hi{i}", [P, 2, DC, P], F32R) for i in range(2)]
        gu_lo = [sb(f"gu_lo{i}", [P, 2, DC, P], F32R) for i in range(2)]
        d_hi = [sb(f"d_hi{i}", [P, D], F32R) for i in range(2)]
        d_lo = [sb(f"d_lo{i}", [P, D], F32R) for i in range(2)]
        x_hi = [sb(f"x_hi{i}", [P, DC, FB], F32R) for i in range(2)]
        x_lo = [sb(f"x_lo{i}", [P, DC, FB], F32R) for i in range(2)]
        sg, hf = [sb(f"sg{i}", [P, FB]) for i in range(2)], [sb(f"hf{i}", [P, FB]) for i in range(2)]
        h_hi = [sb(f"h_hi{i}", [P, FB], F32R) for i in range(2)]
        h_lo = [sb(f"h_lo{i}", [P, FB], F32R) for i in range(2)]
        y = sb("y", [P, FT, D])
        bn, mv, power = sb("bn", [P, FT, 6]), sb("mv", [P, FT, 2]), sb("power", [P, 3, FT])
        rstd = sb("rstd", [P, 2, FT])
        acc = ps("acc", [P, FT, 512])
        g_ps, u_ps = ps("g_ps", [P, 512]), ps("u_ps", [P, 512])

        gate_s, up_s, down_s = signal("gate_s", 1), signal("up_s", 1), signal("down_s", 1)
        silu_s, prod_s, h_hi_s, h_lo_s = signal("silu_s", 1), signal("prod_s", 1), signal("h_hi_s", 1), signal("h_lo_s", 1)
        gu_hi_s, gu_lo_s, d_hi_s, d_lo_s = signal("gu_hi_s", 1), signal("gu_lo_s", 1), signal("d_hi_s", 1), signal("d_lo_s", 1)
        xraw_in, x1_in, x_hi_s, x_lo_s = signal("xraw_in", 16), signal("x1_in", 16), signal("x_hi_s", FT), signal("x_lo_s", 1)
        added, bn_s, var_s, pow_s = signal("added", FT), signal("bn_s", 2 * FT), signal("var_s", 1), signal("pow_s", 1)
        rstd_s, normed, stored = signal("rstd_s", 2), signal("normed", 1), signal("stored", 16)
        power_set, dve_past = sem("power_set"), sem("dve_past")
        end_down, end_stat, end_var, end_neg, end_pow, end_rstd, end_norm = (
            sem(n) for n in ("end_down", "end_stat", "end_var", "end_neg", "end_pow", "end_rstd", "end_norm"))

        def prime(eng, *signals):
            for s in signals:
                eng.sem_inc(s.sem, s.per)

        def blocks(eng, body):
            body(0, 0, True, False)
            with eng.Fori(0, FBLK // 2 - 1) as pair:
                body(pair * 2 + 1, 1, False, False)
                body(pair * 2 + 2, 0, False, False)
            body(FBLK - 1, 1, False, True)

        def steps(eng, step):
            for i in (1, 2, 3):
                step(i, i % 2, False)
            with eng.Fori(0, (IC - 6) // 2) as j:
                step(j * 2 + 4, 0, False)
                step(j * 2 + 5, 1, False)
            step(IC - 2, 0, False)
            step(IC - 1, 1, False)
            step(IC, 0, True)

        block = ctx.enter_context(nc.Block())

        @block.sync
        def _(sp):
            prime(sp, xraw_in, x1_in, stored)

            def load(blk):
                sp.wait_ge(*x_lo_s.last(blk, 1))
                sp.wait_ge(*x_hi_s.last(blk, FT))
                sp.dma_start(xraw[:, :, :, :], x1t_dram[blk]).then_inc(xraw_in.sem, 16)

            def store(blk):
                sp.wait_ge(*normed.now(blk, 1))
                sp.dma_start(out_dram[blk], y[:, :, :]).then_inc(stored.sem, 16)

            def body(blk, parity, first, last):
                if not last:
                    load(blk + 1)
                if not first:
                    store(blk - 1)
                sp.wait_ge(*stored.last(blk, 16))
                sp.dma_start(y[:, :, :], x1_dram[blk]).then_inc(x1_in.sem, 16)

            sp.sem_inc(xraw_in.sem, 16)
            blocks(sp, body)
            for t in range(FT):
                sp.wait_ge(end_norm, t + 1)
                sp.dma_start(out_dram[FBLK - 1, :, t], y[:, t, :]).then_inc(stored.sem, 16)
            sp.wait_ge(*stored.now(FBLK - 1, 16 * FT))

        @block.gpsimd
        def _(pool):
            prime(pool, var_s, pow_s, rstd_s)
            for i, v in enumerate((-0.5, EPS, -1.0)):
                pool.memset(power[:, i, :], v).then_inc(power_set, 1)
            pool.wait_ge(power_set, 3)
            with pool.Fori(0, FBLK - 1) as blk:
                pool.wait_ge(*bn_s.now(blk, 2 * FT))
                pool.wait_ge(*normed.last(blk, 1))
                r, m = rstd[:, 0, :], rstd[:, 1, :]
                pool.tensor_tensor(r, mv[:, :, 1], power[:, 1, :], ALU.add).then_inc(var_s.sem, 1)
                pool.tensor_tensor(m, mv[:, :, 0], power[:, 2, :], ALU.mult).then_inc(rstd_s.sem, 1)
                pool.wait_ge(*var_s.now(blk, 1))
                pool.tensor_tensor(r, r, power[:, 0, :], ALU.pow).then_inc(pow_s.sem, 1)
                pool.wait_ge(*pow_s.now(blk, 1))
                pool.wait_ge(*rstd_s.now(blk, 1))
                pool.tensor_tensor(m, m, r, ALU.mult).then_inc(rstd_s.sem, 1)
            pool.wait_ge(*normed.last(FBLK - 1, 1))
            for t in range(FT):
                r, m = rstd[:, 0, t:t + 1], rstd[:, 1, t:t + 1]
                pool.wait_ge(end_stat, t + 1)
                pool.tensor_tensor(r, mv[:, t, 1:2], power[:, 1, 0:1], ALU.add).then_inc(end_var, 1)
                pool.tensor_tensor(m, mv[:, t, 0:1], power[:, 2, 0:1], ALU.mult).then_inc(end_neg, 1)
                pool.wait_ge(end_var, t + 1)
                pool.tensor_tensor(r, r, power[:, 0, 0:1], ALU.pow).then_inc(end_pow, 1)
                pool.wait_ge(end_pow, t + 1)
                pool.wait_ge(end_neg, t + 1)
                pool.tensor_tensor(m, m, r, ALU.mult).then_inc(end_rstd, 1)

        def gate_up_chunk(w, i):
            return w[:, :, bass.ds(i * P, P)]

        @block.scalar
        def _(act):
            prime(act, silu_s, h_hi_s, gu_hi_s, d_hi_s, x_hi_s, normed)

            def split_x(blk, p):
                act.wait_ge(*xraw_in.now(blk, 16))
                for t in range(FT):
                    act.activation(x_hi[p][:, :, P * t:P * t + P], xraw[:, t, :, :], ACT.Copy).then_inc(x_hi_s.sem, 1)

            def split_gu(s, i, q):
                act.wait_ge(up_s.sem, s)
                act.activation(gu_hi[q][:, 0, :, :], gate_up_chunk(wg, i), ACT.Copy)
                act.activation(gu_hi[q][:, 1, :, :], gate_up_chunk(wu, i), ACT.Copy).then_inc(gu_hi_s.sem, 1)

            def chunk_work(s, i, q):
                act.wait_ge(*gate_s.now(s, 1))
                if not isinstance(s, int) or s > 0:
                    act.wait_ge(prod_s.sem, s)
                act.activation(sg[q][:, :], g_ps[:, :], ACT.Silu, scale=ug_scale[:, 1, bass.ds(i, 1)]).then_inc(silu_s.sem, 1)
                if not isinstance(s, int) or s > 0:
                    act.wait_ge(down_s.sem, s)
                act.activation(d_hi[q][:, :], wd[:, bass.ds(i, 1), :].rearrange("p a n -> p (a n)"), ACT.Copy).then_inc(d_hi_s.sem, 1)

            def round_h(s, q):
                act.wait_ge(*prod_s.now(s, 1))
                act.activation(h_hi[q][:, :], hf[q][:, :], ACT.Copy).then_inc(h_hi_s.sem, 1)

            def normalise(blk):
                act.wait_ge(*rstd_s.now(blk, 2))
                for t in range(FT):
                    i = act.activation(y[:, t, :], y[:, t, :], ACT.Identity, bias=rstd[:, 1, t:t + 1], scale=rstd[:, 0, t:t + 1])
                i.then_inc(normed.sem, 1)

            def body(blk, parity, first, last):
                def step(i, q, wrap):
                    s = blk * IC + i
                    if wrap and last:
                        return
                    if wrap:
                        chunk_work(s, 0, q)
                        split_gu(s + 1, 1, 1 - q)
                        round_h(s, q)
                        return
                    chunk_work(s, i, q)
                    if isinstance(i, int) and i == IC - 1:
                        if not last:
                            split_gu(s + 1, 0, 1 - q)
                    else:
                        split_gu(s + 1, i + 1, 1 - q)
                    round_h(s, q)
                    if isinstance(i, int) and i == 2 and not first:
                        normalise(blk - 1)
                    if isinstance(i, int) and i == IC - 2 and not last:
                        split_x(blk + 1, 1 - parity)

                steps(act, step)

            split_x(0, 0)
            act.activation(gu_hi[0][:, 0, :, :], wg[:, :, 0:P], ACT.Copy)
            act.activation(gu_hi[0][:, 1, :, :], wu[:, :, 0:P], ACT.Copy).then_inc(gu_hi_s.sem, 1)
            chunk_work(0, 0, 0)
            split_gu(1, 1, 1)
            round_h(0, 0)
            blocks(act, body)
            for t in range(FT):
                act.wait_ge(end_rstd, t + 1)
                act.activation(y[:, t, :], y[:, t, :], ACT.Identity, bias=rstd[:, 1, t:t + 1], scale=rstd[:, 0, t:t + 1]).then_inc(end_norm, 1)

        @block.vector
        def _(dve):
            prime(dve, prod_s, h_lo_s, gu_lo_s, d_lo_s, x_lo_s, added, bn_s)

            def split_x(blk, p):
                for t in range(FT):
                    dve.wait_ge(*x_hi_s.now(blk, t + 1))
                    k = slice(P * t, P * t + P)
                    i = dve.tensor_tensor(x_lo[p][:, :, k], xraw[:, t, :, :], x_hi[p][:, :, k].bitcast(F32), ALU.subtract)
                i.then_inc(x_lo_s.sem, 1)

            def split_gu(s, i, q):
                dve.wait_ge(*gu_hi_s.now(s, 1))
                dve.tensor_tensor(gu_lo[q][:, 0, :, :], gate_up_chunk(wg, i), gu_hi[q][:, 0, :, :].bitcast(F32), ALU.subtract)
                dve.tensor_tensor(gu_lo[q][:, 1, :, :], gate_up_chunk(wu, i), gu_hi[q][:, 1, :, :].bitcast(F32), ALU.subtract).then_inc(gu_lo_s.sem, 1)

            def chunk_work(s, i, q):
                dve.wait_ge(*d_hi_s.now(s, 1))
                dve.tensor_tensor(d_lo[q][:, :], wd[:, bass.ds(i, 1), :].rearrange("p a n -> p (a n)"), d_hi[q][:, :].bitcast(F32),
                                  ALU.subtract).then_inc(d_lo_s.sem, 1)
                dve.wait_ge(*up_s.now(s, 1))
                dve.wait_ge(*silu_s.now(s, 1))
                dve.scalar_tensor_tensor(hf[q][:, :], u_ps[:, :], ug_scale[:, 0, bass.ds(i, 1)], sg[q][:, :], ALU.mult, ALU.mult).then_inc(prod_s.sem, 1)

            def lower_h(s, q):
                dve.wait_ge(*h_hi_s.now(s, 1))
                dve.wait_ge(*prod_s.now(s, 1))
                dve.tensor_tensor(h_lo[q][:, :], hf[q][:, :], h_hi[q][:, :].bitcast(F32), ALU.subtract).then_inc(h_lo_s.sem, 1)

            def residual(blk):
                dve.wait_ge(*x1_in.now(blk, 16))
                for t in range(FT):
                    dve.wait_ge(down_s.sem, (blk + 1) * IC + 1)
                    dve.tensor_tensor(y[:, t, :], acc[:, t, :], y[:, t, :], ALU.add).then_inc(added.sem, 1)

            def statistics(blk):
                dve.wait_ge(*rstd_s.last(blk, 2))
                for t in range(FT):
                    dve.wait_ge(*added.now(blk, t + 1))
                    dve.bn_stats(bn[:, t, :], y[:, t, :]).then_inc(bn_s.sem, 1)
                dve.wait_ge(*bn_s.now(blk, FT))
                dve.sem_inc(dve_past, 1)
                for t in range(FT):
                    dve.bn_aggr(mv[:, t, :], bn[:, t, :]).then_inc(bn_s.sem, 1)

            def body(blk, parity, first, last):
                def step(i, q, wrap):
                    s = blk * IC + i
                    if wrap and last:
                        return
                    nxt = 0 if isinstance(i, int) and i == IC - 1 else (1 if wrap else i + 1)
                    if not (last and isinstance(i, int) and i == IC - 1):
                        split_gu(s + 1, nxt, 1 - q)
                    chunk_work(s, 0 if wrap else i, q)
                    lower_h(s, q)
                    if wrap:
                        residual(blk)
                    if isinstance(i, int) and i == 1 and not first:
                        statistics(blk - 1)
                    if isinstance(i, int) and i == IC - 2 and not last:
                        split_x(blk + 1, 1 - parity)

                steps(dve, step)

            split_x(0, 0)
            split_gu(0, 0, 0)
            split_gu(1, 1, 1)
            chunk_work(0, 0, 0)
            lower_h(0, 0)
            blocks(dve, body)
            dve.wait_ge(*x1_in.now(FBLK - 1, 16))
            dve.wait_ge(*rstd_s.last(FBLK - 1, 2))
            for t in range(FT):
                dve.wait_ge(end_down, t + 1)
                dve.tensor_tensor(y[:, t, :], acc[:, t, :], y[:, t, :], ALU.add).then_inc(added.sem, 1)
                dve.wait_ge(*added.now(FBLK - 1, t + 1))
                dve.bn_stats(bn[:, t, :], y[:, t, :]).then_inc(bn_s.sem, 1)
                dve.wait_ge(*bn_s.now(FBLK - 1, t + 1))
                dve.sem_inc(dve_past, 1)
                dve.bn_aggr(mv[:, t, :], bn[:, t, :]).then_inc(end_stat, 1)

        @block.tensor
        def _(pe):
            prime(pe, gate_s, up_s, down_s)

            def gate_up(s, q, p):
                pe.wait_ge(*gu_lo_s.now(s, 1))
                for m, bank, free, done in ((0, g_ps, silu_s, gate_s), (1, u_ps, prod_s, up_s)):
                    pe.wait_ge(free.sem, s + 1)
                    for c in range(DC):
                        i = three_passes(pe, bank[:, :], gu_hi[q][:, m, c, :], gu_lo[q][:, m, c, :], x_hi[p][:, c, :], x_lo[p][:, c, :],
                                         c == 0, c == DC - 1)
                    i.then_inc(done.sem, 1)

            def down(s, q, first, last, end=False):
                pe.wait_ge(*h_lo_s.now(s, 1))
                pe.wait_ge(*d_lo_s.now(s, 1))
                for t in range(FT):
                    k = slice(P * t, P * t + P)
                    i = three_passes(pe, acc[:, t, :], h_hi[q][:, k], h_lo[q][:, k], d_hi[q][:, :], d_lo[q][:, :], first, last)
                    if end:
                        i.then_inc(end_down, 1)
                if not end:
                    i.then_inc(down_s.sem, 1)

            def body(blk, parity, first, last):
                def step(i, q, wrap):
                    s = blk * IC + i
                    if wrap:
                        if not last:
                            pe.wait_ge(*x_lo_s.now(blk + 1, 1))
                            gate_up(s, q, 1 - parity)
                        down(s - 1, 1 - q, False, True, last)
                        return
                    gate_up(s, q, parity)
                    start = isinstance(i, int) and i == 1
                    if start:
                        pe.wait_ge(*added.last(blk, FT))
                    down(s - 1, 1 - q, start, False)

                steps(pe, step)

            pe.wait_ge(*x_lo_s.now(0, 1))
            gate_up(0, 0, 0)
            blocks(pe, body)


def layer_kernel(nc, io, out):
    x1_dram = nc.dram_tensor("x1_scratch", [B * T, D], F32, kind="Internal").ap()
    x1t_dram = nc.dram_tensor("x1t_scratch", [B * TILES, P, D], F32, kind="Internal").ap()
    io["x"] = io["x"].rearrange("b (t p) d -> b t p d", p=P)
    sems = ExitStack()
    with sems:
        whole_layer(nc, sems, io, x1_dram, x1t_dram, out)


def whole_layer(nc, sems, io, x1_dram, x1t_dram, out):
    attention_block(nc, sems, io, x1_dram.rearrange("(b t p) d -> b t p d", t=TILES, p=P),
                    x1t_dram.rearrange("(b t) p d -> b t p d", t=TILES))
    ctx = ExitStack()
    with ctx:
        x1t_blocks = x1t_dram.rearrange("(n t) p (c q) -> n p t c q", t=FT, c=DC)
        folded = weights_block(nc, sems, io, x1t_blocks, ctx)
        ffn_block(nc, sems, x1_dram.rearrange("(n t p) d -> n p t d", t=FT, p=P), x1t_blocks,
                  out.rearrange("b (m t p) d -> (b m) p t d", t=FT, p=P), *folded)


def shape_tables():
    import numpy as np
    f = np.float32
    p = np.arange(P)
    inv = f(1.0) / (f(10000.0) ** (np.arange(0, DG, 2, dtype=f) / f(DG)))
    ang = np.arange(T, dtype=f)[:, None] * inv.astype(f)[None, :]
    cos, sin = np.cos(ang).astype(f), np.sin(ang).astype(f)
    rope = np.stack([cos, sin], 1).reshape(TILES, P, 2, HALF).transpose(1, 0, 2, 3)
    own = lambda n, w, k: np.repeat((p[:, None] // w == np.arange(n)[None, :]).astype(f), k, axis=1)
    pos = np.arange(REMOTE).reshape(RT, P).T[:, :, None]
    k = np.arange(NB)[None, None, :]
    pool_w = np.where(pos // MB == k, f(1.0 / MB), f(0)).astype(f)
    sees = MB * k + MB - 1 <= pos
    keep, hide = sees.astype(f), np.where(sees, f(0), f(NEG)).astype(f)
    none = ~sees.any(-1)
    spread, rest = np.where(none, f(KEYS / NB), f(1)).astype(f), np.where(none, f(1.0 / KEYS), f(0)).astype(f)
    causal = np.where(p[None, :] <= p[:, None], f(0), f(NEG)).astype(f)
    small = np.concatenate([own(4, DS, NB), own(8, HALF, NB), own(2, DV, NK), pool_w.reshape(P, -1), keep.reshape(P, -1),
                            hide.reshape(P, -1), spread, rest, causal], axis=1)
    had = np.array([[1 - 2 * (bin(i & j).count("1") % 2) for j in range(P)] for i in range(P)], f)
    return {"ident": np.eye(P, dtype=f), "cos_t": np.tile(cos[:REMOTE].T, (P // HALF, 1)), "sin_t": np.tile(sin[:REMOTE].T, (P // HALF, 1)),
            "rope": rope, "small": small, "had": np.stack([had, -had], 1)}


def kernel(**inputs):
    import numpy as np
    import concourse.bacc as bacc
    from concourse.bass_utils import run_bass_kernel_spmd as run

    a = {n: np.asarray(v) for n, v in inputs.items()}
    x = a["L0_attn_x"]
    rows = lambda w: w.reshape(w.shape[0] // P, P, -1).transpose(1, 0, 2)
    halves = lambda w, h: w.reshape(D, h, 2, HALF).transpose(0, 2, 1, 3).reshape(D, -1)
    ls = a["L0_attn_logit_scale"]
    chunk_rows = np.repeat(ls, DS).reshape(DC, P).T
    wo = a["L0_attn_Wo"].reshape(2, 2, 4, DV, D).transpose(1, 3, 0, 2, 4).reshape(P, 8, D)
    arrays = {
        "x": x,
        "xt": x.transpose(0, 2, 1).reshape(B, DC, P, T).transpose(0, 2, 1, 3),
        "wq": rows(np.concatenate([a["L0_attn_Wq_sem"], halves(a["L0_attn_Wq_geo"], H)], 1)),
        "wqs": rows(a["L0_attn_Wq_sem"].T),
        "wkv": rows(np.concatenate([halves(a["L0_attn_Wk_geo"], HKV), a["L0_attn_Wk_sem"], a["L0_attn_Wv"]], 1)),
        "wo": wo,
        "logit_scale": np.concatenate([np.broadcast_to(ls, (P, H)), chunk_rows], 1),
        "wg": rows(a["L0_ffn_W_gate"].T), "wu": rows(a["L0_ffn_W_up"].T), "wd": rows(a["L0_ffn_W_down"].T),
        "su": a["L0_ffn_SU_ug"].reshape(DC, P).T, "sd": a["L0_ffn_SU_dp"].reshape(IC, P).T,
        "dps": np.broadcast_to(a["L0_ffn_Wscale_dp"], (P, D)),
        "ug_scale": a["L0_ffn_Wscale_ug"].reshape(2, IC, P).transpose(2, 0, 1),
        **shape_tables(),
    }
    arrays = {f"in_{n}": np.ascontiguousarray(v) for n, v in arrays.items()}
    nc = bacc.Bacc("TRN2", target_bir_lowering=False, num_devices=1)
    io = {n[3:]: nc.dram_tensor(n, v.shape, mybir.dt.from_np(v.dtype), kind="ExternalInput").ap() for n, v in arrays.items()}
    out = nc.dram_tensor("out", (B, T, D), F32, kind="ExternalOutput").ap()
    layer_kernel(nc, io, out)
    return run(nc, [arrays], core_ids=[0]).results[0]["out"]
```
